# Optimizing a Trainium2 kernel written in Bass

```python
import numpy as np
import jax
import jax.numpy as jnp

def _softmax(x, axis=-1):
    return jax.nn.softmax(x, axis=axis)

def _gelu(x):
    return jax.nn.gelu(x, approximate=True)

def _silu(x):
    return jax.nn.silu(x)

def _sigmoid(x):
    return jax.nn.sigmoid(x)

def _layernorm(x, axis=-1, eps=1e-05):
    m = jnp.mean(x, axis=axis, keepdims=True)
    v = jnp.var(x, axis=axis, keepdims=True)
    return (x - m) / jnp.sqrt(v + eps)

def _scatter_add(tgt, idx, src, axis=0):
    return tgt.at[idx].add(src)

def _segment_sum(src, seg, n):
    return jax.ops.segment_sum(src, seg, n)
kernel_name = 'mk_perceiver_d1_seqx_r2_5350fa'

def setup_inputs(seed: int=0):
    np.random.seed(seed)
    _w = jnp.asarray

    def _rec_inputs():
        import jax
        import jax.numpy as jnp
        _rk = jax.random.key(seed)
        x = 0.002226 + 0.9996 * jax.random.normal(jax.random.fold_in(_rk, 1), (2, 128, 512), jnp.float32)
        _lenS = 128 - jax.random.randint(jax.random.fold_in(_rk, 7), (2,), 0, max(1, 128 // 4) + 1, jnp.int32)
        _lenS2 = 2048 - jax.random.randint(jax.random.fold_in(_rk, 8), (2,), 0, max(1, 2048 // 4) + 1, jnp.int32)
        _ctx_1024P = jax.random.normal(jax.random.fold_in(_rk, 11), (2, 16, 512), jnp.float32)
        _ctx_1024c = jax.random.dirichlet(jax.random.fold_in(_rk, 511), 0.3 * jnp.ones((16,), jnp.float32), (2, 2048))
        _ctx_1024t = jnp.einsum('bsk,bkd->bsd', _ctx_1024c, _ctx_1024P)
        _ctx_1024t = _ctx_1024t * jax.lax.rsqrt(jnp.mean(jnp.square(_ctx_1024t)) + 1e-12) * 0.953939
        ctx_1024 = -0.000125008 + 0.999885 * (_ctx_1024t + 0.3 * jax.random.normal(jax.random.fold_in(_rk, 611), (2, 2048, 512), jnp.float32))
        _validS = jnp.arange(128)[None, :] < _lenS[:, None]
        _validS2 = jnp.arange(2048)[None, :] < _lenS2[:, None]
        _causal = jnp.tril(jnp.ones((128, 128), dtype=bool))
        mask_BxS2_bk0 = jnp.logical_not(jnp.broadcast_to(_validS2[:, :], (2, 2048)))
        return (x, ctx_1024, mask_BxS2_bk0)
    x, ctx_1024, mask_BxS2_bk0 = _rec_inputs()

    def _L0_xattn_setup():
        import jax, jax.numpy as jnp
        import numpy as np
        EPS = 1e-05

        def layer_norm(x, g, b):
            mu = jnp.mean(x, axis=-1, keepdims=True)
            var = jnp.mean((x - mu) ** 2, axis=-1, keepdims=True)
            return (x - mu) * jax.lax.rsqrt(var + EPS) * g + b
        key = jax.random.key(seed)
        ks = jax.random.split(key, 8)
        b, n, l, D = (8, 2048, 64, 512)
        heads, dim_head = (16, 64)
        inner = heads * dim_head
        x = jax.random.normal(ks[0], (b, n, D), dtype=jnp.float32)
        latents = jax.random.normal(ks[1], (b, l, D), dtype=jnp.float32)
        mask = jax.random.randint(ks[2], (b, n), 0, 2) > 0
        Wq = jax.random.normal(ks[3], (D, inner), dtype=jnp.float32) * D ** (-0.5)
        Wkv = jax.random.normal(ks[4], (D, 2 * inner), dtype=jnp.float32) * D ** (-0.5)
        Wout = jax.random.normal(ks[5], (inner, D), dtype=jnp.float32) * inner ** (-0.5)
        g1 = jnp.ones((D,), jnp.float32)
        b1 = jnp.zeros((D,), jnp.float32)
        g2 = jnp.ones((D,), jnp.float32)
        b2 = jnp.zeros((D,), jnp.float32)
        return {'x': x, 'latents': latents, 'mask': mask, 'g1': g1, 'b1': b1, 'g2': g2, 'b2': b2, 'Wq': Wq, 'Wkv': Wkv, 'Wout': Wout}
    _L0_xattn_all = _L0_xattn_setup()
    _L0_xattn_in = {k: v for k, v in _L0_xattn_all.items() if k in ('g1', 'b1', 'g2', 'b2', 'Wq', 'Wkv', 'Wout')}
    del _L0_xattn_all

    def _L0_attn_setup():
        import jax, jax.numpy as jnp
        import numpy as np
        D_MODEL, N_HEADS, BATCH, SEQ = (512, 16, 2, 1024)

        def get_freqs(seq, n_dim):
            inv_freq = 1.0 / 10000.0 ** (jnp.arange(0, n_dim, 2, dtype=jnp.float32) / n_dim)
            pos = jnp.arange(seq, dtype=jnp.float32)
            return pos[:, None] * inv_freq[None, :]

        def rope(x, freq):
            cos = jnp.cos(freq)[None, :, None, :]
            sin = jnp.sin(freq)[None, :, None, :]
            x1, x2 = (x[..., ::2], x[..., 1::2])
            r1 = x1 * cos - x2 * sin
            r2 = x1 * sin + x2 * cos
            return jnp.stack([r1, r2], axis=-1).reshape(x.shape)
        key = jax.random.key(seed)
        ks = jax.random.split(key, 5)
        w_scale = 0.01
        return {'x': jax.random.normal(ks[0], (BATCH, SEQ, D_MODEL), dtype=jnp.float32), 'qw': jax.random.normal(ks[1], (D_MODEL, D_MODEL), dtype=jnp.float32) * w_scale, 'kw': jax.random.normal(ks[2], (D_MODEL, D_MODEL), dtype=jnp.float32) * w_scale, 'vw': jax.random.normal(ks[3], (D_MODEL, D_MODEL), dtype=jnp.float32) * w_scale, 'ow': jax.random.normal(ks[4], (D_MODEL, D_MODEL), dtype=jnp.float32) * w_scale}
    _L0_attn_all = _L0_attn_setup()
    _L0_attn_in = {k: v for k, v in _L0_attn_all.items() if k in ('qw', 'kw', 'vw', 'ow')}
    del _L0_attn_all

    def _L0_ffn_setup():
        import jax, jax.numpy as jnp
        import numpy as np
        B, T, D = (2, 1024, 512)
        DCD = 2048
        RET = 128
        NEXP = 2048
        NKEYS = 64
        H = 4
        KPH = 8
        key = jax.random.key(seed)
        ks = jax.random.split(key, 10)
        s = lambda k, shape, scale: jax.random.normal(k, shape, jnp.float32) * scale
        return {'hidden_states': jax.random.normal(ks[0], (B, T, D), jnp.float32), 'Wg': s(ks[1], (D, DCD), 0.02), 'bg': jnp.zeros((DCD,), jnp.float32), 'Wu': s(ks[2], (D, DCD), 0.02), 'bu': jnp.zeros((DCD,), jnp.float32), 'Wd': s(ks[3], (DCD, D), 0.02), 'bd': jnp.zeros((D,), jnp.float32), 'Wq': s(ks[4], (D, RET * H), 0.02), 'keys': s(ks[5], (H, NKEYS, 2, RET // 2), 0.02), 'down_embed': s(ks[6], (NEXP, D), 0.02), 'up_embed': s(ks[7], (NEXP, D), 0.02)}
    _L0_ffn_all = _L0_ffn_setup()
    _L0_ffn_in = {k: v for k, v in _L0_ffn_all.items() if k in ('Wg', 'bg', 'Wu', 'bu', 'Wd', 'bd', 'Wq', 'keys', 'down_embed', 'up_embed')}
    del _L0_ffn_all
    return {'x': x, 'ctx_1024': ctx_1024, 'mask_BxS2_bk0': mask_BxS2_bk0, 'L0_xattn_g1': _L0_xattn_in['g1'], 'L0_xattn_b1': _L0_xattn_in['b1'], 'L0_xattn_g2': _L0_xattn_in['g2'], 'L0_xattn_b2': _L0_xattn_in['b2'], 'L0_xattn_Wq': _L0_xattn_in['Wq'], 'L0_xattn_Wkv': _L0_xattn_in['Wkv'], 'L0_xattn_Wout': _L0_xattn_in['Wout'], 'L0_attn_qw': _L0_attn_in['qw'], 'L0_attn_kw': _L0_attn_in['kw'], 'L0_attn_vw': _L0_attn_in['vw'], 'L0_attn_ow': _L0_attn_in['ow'], 'L0_ffn_Wg': _L0_ffn_in['Wg'], 'L0_ffn_bg': _L0_ffn_in['bg'], 'L0_ffn_Wu': _L0_ffn_in['Wu'], 'L0_ffn_bu': _L0_ffn_in['bu'], 'L0_ffn_Wd': _L0_ffn_in['Wd'], 'L0_ffn_bd': _L0_ffn_in['bd'], 'L0_ffn_Wq': _L0_ffn_in['Wq'], 'L0_ffn_keys': _L0_ffn_in['keys'], 'L0_ffn_down_embed': _L0_ffn_in['down_embed'], 'L0_ffn_up_embed': _L0_ffn_in['up_embed']}

def reference(x, ctx_1024, mask_BxS2_bk0, L0_xattn_g1, L0_xattn_b1, L0_xattn_g2, L0_xattn_b2, L0_xattn_Wq, L0_xattn_Wkv, L0_xattn_Wout, L0_attn_qw, L0_attn_kw, L0_attn_vw, L0_attn_ow, L0_ffn_Wg, L0_ffn_bg, L0_ffn_Wu, L0_ffn_bu, L0_ffn_Wd, L0_ffn_bd, L0_ffn_Wq, L0_ffn_keys, L0_ffn_down_embed, L0_ffn_up_embed):
    import jax
    import jax.numpy as jnp

    def _L0_xattn_ref(x, latents, mask, g1, b1, g2, b2, Wq, Wkv, Wout):
        import jax, jax.numpy as jnp
        import numpy as np
        EPS = 1e-05

        def layer_norm(x, g, b):
            mu = jnp.mean(x, axis=-1, keepdims=True)
            var = jnp.mean((x - mu) ** 2, axis=-1, keepdims=True)
            return (x - mu) * jax.lax.rsqrt(var + EPS) * g + b
        heads, dim_head = (16, 64)
        b, n, D = x.shape
        l = latents.shape[1]
        xn = layer_norm(x, g1, b1)
        ln_lat = layer_norm(latents, g2, b2)
        q = ln_lat @ Wq
        kv = jnp.concatenate([xn, ln_lat], axis=1) @ Wkv
        k, v = jnp.split(kv, 2, axis=-1)

        def to_heads(t):
            return t.reshape(t.shape[0], t.shape[1], heads, dim_head).transpose(0, 2, 1, 3)
        q, k, v = (to_heads(q), to_heads(k), to_heads(v))
        scale = 1.0 / np.sqrt(np.sqrt(dim_head)).astype(np.float32)
        weight = jnp.einsum('bhld,bhnd->bhln', q * scale, k * scale)
        full_mask = jnp.concatenate([mask, jnp.ones((b, l), dtype=bool)], axis=1)
        neg = -jnp.finfo(weight.dtype).max
        weight = jnp.where(full_mask[:, None, None, :], weight, neg)
        weight = jax.nn.softmax(weight.astype(jnp.float32), axis=-1).astype(q.dtype)
        out = jnp.einsum('bhln,bhnd->bhld', weight, v)
        out = out.transpose(0, 2, 1, 3).reshape(b, l, heads * dim_head)
        return out @ Wout

    def _L0_attn_ref(x, qw, kw, vw, ow):
        import jax, jax.numpy as jnp
        import numpy as np
        D_MODEL, N_HEADS, BATCH, SEQ = (512, 16, 2, 1024)

        def get_freqs(seq, n_dim):
            inv_freq = 1.0 / 10000.0 ** (jnp.arange(0, n_dim, 2, dtype=jnp.float32) / n_dim)
            pos = jnp.arange(seq, dtype=jnp.float32)
            return pos[:, None] * inv_freq[None, :]

        def rope(x, freq):
            cos = jnp.cos(freq)[None, :, None, :]
            sin = jnp.sin(freq)[None, :, None, :]
            x1, x2 = (x[..., ::2], x[..., 1::2])
            r1 = x1 * cos - x2 * sin
            r2 = x1 * sin + x2 * cos
            return jnp.stack([r1, r2], axis=-1).reshape(x.shape)
        batch, seq, dim = x.shape
        n_heads = N_HEADS
        n_dim = dim // n_heads
        Q = (x @ qw).astype(jnp.float32).reshape(batch, seq, n_heads, n_dim)
        K = (x @ kw).astype(jnp.float32).reshape(batch, seq, n_heads, n_dim)
        V = (x @ vw).astype(jnp.float32).reshape(batch, seq, n_heads, n_dim)
        freq = get_freqs(seq, n_dim)
        Q = rope(Q, freq)
        K = rope(K, freq)
        Q = jnp.transpose(Q, (0, 2, 1, 3))
        K = jnp.transpose(K, (0, 2, 1, 3))
        V = jnp.transpose(V, (0, 2, 1, 3))
        scale = jnp.sqrt(jnp.float32(n_dim))
        score = jnp.einsum('bhqd,bhkd->bhqk', Q, K) / scale
        causal = jnp.tril(jnp.ones((1, 1, seq, seq), dtype=jnp.float32))
        score = score - 10000000000.0 * (1.0 - causal)
        score = score - jnp.max(score, axis=-1, keepdims=True)
        weights = jax.nn.softmax(score, axis=-1)
        attn = jnp.einsum('bhqk,bhkd->bhqd', weights, V)
        merged = jnp.transpose(attn, (0, 2, 1, 3)).reshape(batch, seq, dim)
        return (merged @ ow).astype(x.dtype)

    def _L0_ffn_ref(hidden_states, Wg, bg, Wu, bu, Wd, bd, Wq, keys, down_embed, up_embed):
        import jax, jax.numpy as jnp
        import numpy as np
        B, T, D = (2, 1024, 512)
        DCD = 2048
        RET = 128
        NEXP = 2048
        NKEYS = 64
        H = 4
        KPH = 8
        b, t, d = hidden_states.shape
        q = (hidden_states @ Wq).reshape(b, t, 2, H, RET // 2)
        sim = jnp.einsum('btphn,hkpn->pbthk', q, keys)
        sc, ix = jax.lax.top_k(sim, KPH)
        sx, sy = (sc[0], sc[1])
        ixx, ixy = (ix[0], ix[1])
        all_sc = (sx[..., :, None] + sy[..., None, :]).reshape(b, t, H, KPH * KPH)
        all_ix = (ixx[..., :, None] * NKEYS + ixy[..., None, :]).reshape(b, t, H, KPH * KPH)
        scores, pk = jax.lax.top_k(all_sc, KPH)
        idx = jnp.take_along_axis(all_ix, pk, axis=-1)
        de = down_embed[idx]
        ue = up_embed[idx]
        w = jnp.einsum('btd,bthkd->bthk', hidden_states, de)
        w = jax.nn.silu(w) * jax.nn.softmax(scores, axis=-1)
        experts_states = jnp.einsum('bthk,bthkd->btd', w, ue)
        mlp = jax.nn.silu(hidden_states @ Wg + bg) * (hidden_states @ Wu + bu) @ Wd + bd
        return mlp + experts_states
    x = x + _L0_xattn_ref(ctx_1024, _layernorm(x, axis=-1), mask_BxS2_bk0, L0_xattn_g1, L0_xattn_b1, L0_xattn_g2, L0_xattn_b2, L0_xattn_Wq, L0_xattn_Wkv, L0_xattn_Wout)
    x = x + _L0_attn_ref(_layernorm(x, axis=-1), L0_attn_qw, L0_attn_kw, L0_attn_vw, L0_attn_ow)
    x = x + _L0_ffn_ref(_layernorm(x, axis=-1), L0_ffn_Wg, L0_ffn_bg, L0_ffn_Wu, L0_ffn_bu, L0_ffn_Wd, L0_ffn_bd, L0_ffn_Wq, L0_ffn_keys, L0_ffn_down_embed, L0_ffn_up_embed)
    return x

_drawn_inputs = setup_inputs


def setup_inputs(seed=0):
    import zlib

    import numpy as np

    out = dict(_drawn_inputs(seed))
    spreads = {'L0_xattn_g1': (1.0, 0.2),
     'L0_xattn_b1': (0.0, 0.1),
     'L0_xattn_g2': (1.0, 0.2),
     'L0_xattn_b2': (0.0, 0.1),
     'L0_ffn_bg': (0.0, 0.367),
     'L0_ffn_bu': (0.0, 0.379),
     'L0_ffn_bd': (0.0, 0.1)}
    factors = {'L0_attn_qw': 8.0,
     'L0_attn_kw': 8.0,
     'L0_attn_vw': 3.368,
     'L0_attn_ow': 3.325,
     'L0_ffn_Wq': 8.0,
     'L0_ffn_keys': 8.0,
     'L0_ffn_down_embed': 6.963,
     'L0_ffn_up_embed': 6.208}
    for name, (base, spread) in spreads.items():
        noise = np.random.default_rng([zlib.crc32(name.encode()), seed]).standard_normal(out[name].shape)
        drawn = base * np.exp(spread * noise) if base else spread * noise
        out[name] = jnp.asarray(drawn.astype(out[name].dtype))
    for name, factor in factors.items():
        out[name] = (out[name] * factor).astype(out[name].dtype)
    return out
```

```python
from contextlib import ExitStack

import numpy as np
import concourse.bass as bass
from concourse import mybir

F32 = mybir.dt.float32
F32R = mybir.dt.float32r
U8 = mybir.dt.uint8
U32 = mybir.dt.uint32
ALU = mybir.AluOpType
ACT = mybir.ActivationFunctionType
AX = mybir.AxisListType

P = 128
EPS = 1e-5
HI, LO = 0, 1


def perceiver_layer(nc, x, ctx1024, mask, g1, b1, g2, b2, Wq, Wkv, Wout, qw, kw, vw, ow,
                    Wg, bg, Wu, bu, Wd, bd, fWq, keys, down, up, rope_cos, rope_sin, causal, select, out):
    B, L, D = x.shape
    N = ctx1024.shape[1]
    KD = D // P
    INNER = Wq.shape[1]
    DH = 64
    H = INNER // DH
    CW = 512
    NT = CW // P
    ROUNDS = N // CW
    HG = 4
    G = H // HG
    STEPS = B * H
    UNITS = B * G
    XSC = DH ** -0.5
    SH, SD = 16, D // 16
    SSC = SD ** -0.5
    BIG = 1e30
    T2 = B * L
    F = Wg.shape[1]
    NEXP = down.shape[0]
    NK = 64
    RH = 4
    ETS = NEXP // P
    assert (B, L, D, N, F, NEXP) == (2, 128, 512, 2048, 2048, 2048)

    with ExitStack() as stack:
        def sb(name, shape, dt=F32):
            return stack.enter_context(nc.sbuf_tensor(name, shape, dt))

        def sem(name):
            return stack.enter_context(nc.semaphore(name))

        W = sb("W", [P, 16384], F32R)
        with nc.sbuf_tensor("QA", [P, 8192], F32R) as QA:
            pass
        with nc.sbuf_tensor("OTA", [P, 4096], F32R) as OTA:
            pass
        tail = sb("tail", [P, 4096])
        late = sb("late", [P, 4096])
        XA = sb("XA", [P, 8192], F32R)
        KV = sb("KV", [P, 8192], F32R)
        raw = sb("raw", [P, 2048])
        work = sb("work", [P, 2048])
        xst = sb("xst", [P, CW])
        PT = sb("PT", [P, 2, 2, CW], F32R)
        O = sb("O", [P, B, INNER])
        xres = sb("xres", [P, B, D])
        ident = sb("ident", [P, P])
        vrow = sb("vrow", [48, P])
        vec = sb("vec", [P, 48])
        nbg = sb("nbg", [P, 16])
        mraw = sb("mraw", [P, CW], U8)
        st = sb("st", [P, 4, 6])
        mv = sb("mv", [P, 4, 2])
        rstd = sb("rstd", [P, 4])
        half = sb("half", [P, 4])
        mold = sb("mold", [P, B, H])
        mcur = sb("mcur", [P, 2, HG])
        negm = sb("negm", [P, 2, HG])
        dm = sb("dm", [P, 2, HG])
        alpha = sb("alpha", [P, 2, HG])
        rs = sb("rs", [P, 2, HG])
        lsum = sb("lsum", [P, B, H])
        small = sb("small", [P, 64])

        pS = stack.enter_context(nc.psum_tensor("pS", [P, 2, 512], F32))
        pJ = stack.enter_context(nc.psum_tensor("pJ", [P, 2, 512], F32))
        pT = stack.enter_context(nc.psum_tensor("pT", [P, 2, 512], F32))
        pV = stack.enter_context(nc.psum_tensor("pV", [P, 512], F32))
        pX = stack.enter_context(nc.psum_tensor("pX", [P, 512], F32))

        WKV = W[:, :].rearrange("p (s k n) -> p s k n", s=2, k=KD)
        WQ = KV[:, :].rearrange("p (s k n) -> p s k n", s=2, k=KD)
        QT = QA[:, :].rearrange("p (s h t) -> p s h t", s=2, h=H)
        XT = XA[:, :].rearrange("p (c s k n) -> p c s k n", c=2, s=2, k=KD)
        KT = KV[:, 0:4096].rearrange("p (c s j n) -> p c s j n", c=2, s=2, j=2)
        VT = KV[:, 4096:8192].rearrange("p (c s t n) -> p c s t n", c=2, s=2, t=NT)
        SP = work[:, 0:1024].rearrange("p (c n) -> p c n", c=2)
        MB = work[:, 1024:2048].rearrange("p (c n) -> p c n", c=2)
        rawc = raw[:, :].rearrange("p (t d) -> p t d", t=NT)
        Of = O[:, :, :].rearrange("p b n -> p (b n)")
        Kg1, Kb1, Kg2, Kb2, Kbg, Kbu = 0, 4, 8, 12, 16, 32

        d_x = sem("d_x"); d_vec = sem("d_vec"); d_wq = sem("d_wq"); d_wkv = [sem("d_wkvA"), sem("d_wkvB")]
        d_raw = sem("d_raw"); d_mask = sem("d_mask")
        s_ident = sem("s_ident"); s_zero = sem("s_zero"); s_vt = sem("s_vt"); s_vec = sem("s_vec")
        s_wqh = sem("s_wqh"); s_wql = sem("s_wql"); s_wkvh = sem("s_wkvh"); s_wkvl = sem("s_wkvl")
        s_q = sem("s_q"); s_qh = sem("s_qh"); s_ql = sem("s_ql")
        s_stat = sem("s_stat"); s_rst = sem("s_rst"); s_lat = sem("s_lat"); s_latn = sem("s_latn"); s_bn = sem("s_bn"); s_ch = sem("s_chain")
        s_norm = sem("s_norm"); s_xtr = sem("s_xtr"); s_xev = sem("s_xev"); s_xh = sem("s_xh"); s_xT = sem("s_xT")
        s_mb = sem("s_mb")
        s_qk = sem("s_qk"); s_ttr = sem("s_ttr"); s_negm = sem("s_negm"); s_exp = sem("s_exp")
        s_proj = sem("s_proj"); s_kvh = sem("s_kvh"); s_kvl = sem("s_kvl")
        s_tr = sem("s_tr"); s_pth = sem("s_pth"); s_ptl = sem("s_ptl"); s_pv = sem("s_pv")
        s_dmt = sem("s_dmt"); s_dm = sem("s_dm"); s_alpha = sem("s_alpha"); s_lt = sem("s_lt"); s_osc = sem("s_osc"); s_oadd = sem("s_oadd")

        d_wA = sem("d_wA"); d_wB = sem("d_wB"); d_key = sem("d_key"); d_rope = sem("d_rope"); d_sel = sem("d_sel"); d_out = sem("d_out"); d_bd = sem("d_bd")
        s_whi = sem("s_whi"); s_wlo = sem("s_wlo"); s_wuse = sem("s_wuse")
        s_src = sem("s_src")
        s_tt = sem("s_tt"); s_th = sem("s_th"); s_tl = sem("s_tl")
        s_dve = sem("s_dve"); s_ln = sem("s_ln"); s_pn = sem("s_pn")
        s_yread = sem("s_yread")
        s_vh = sem("s_vh"); s_vl = sem("s_vl"); s_rope = sem("s_rope"); s_kz = sem("s_kz")
        s_sc = sem("s_sc"); s_sm = sem("s_sm"); s_se = sem("s_se"); s_pt2 = sem("s_pt2"); s_p2h = sem("s_p2h"); s_p2l = sem("s_p2l"); s_pv2 = sem("s_pv2")
        s_kt = sem("s_kt"); s_kh = sem("s_kh"); s_kl = sem("s_kl"); s_q2 = sem("s_q2"); s_q2h = sem("s_q2h"); s_q2l = sem("s_q2l"); s_sim = sem("s_sim")
        s_gu = sem("s_gu"); s_ge = sem("s_ge"); s_gur = sem("s_gur"); s_a = sem("s_a"); s_ah = sem("s_ah"); s_al = sem("s_al"); s_mo = sem("s_mo")
        s_dve2 = sem("s_dve2"); s_tk = sem("s_tk"); s_tke = sem("s_tke"); s_gn = sem("s_gn"); s_pl = sem("s_pl"); s_simc = sem("s_simc"); s_gt = sem("s_gt"); s_gh = sem("s_gh"); s_gl = sem("s_gl")
        s_selr = sem("s_selr"); s_iota = sem("s_iota")
        s_gd = sem("s_gd"); s_gexp = sem("s_gexp"); s_md = sem("s_md"); s_hs = sem("s_hs"); s_hs1 = sem("s_hs1"); s_dt = sem("s_dt"); s_dh = sem("s_dh"); s_dl = sem("s_dl")
        s_w = sem("s_w"); s_we = sem("s_we"); s_wr = sem("s_wr"); s_c = sem("s_c"); s_chi = sem("s_chi"); s_cl = sem("s_cl"); s_eo = sem("s_eo")
        s_ex = sem("s_ex"); s_exe = sem("s_exe"); s_fin = sem("s_fin")

        w4 = lambda w: w.rearrange("(k p) n -> p k n", p=P)
        blocks = [w4(Wout)[:, 0:4, :], w4(Wout)[:, 4:8, :], w4(qw), w4(kw), w4(vw), w4(ow), w4(fWq)]
        for f in range(4):
            blocks += [w4(Wg)[:, :, 512 * f:512 * f + 512], w4(Wu)[:, :, 512 * f:512 * f + 512],
                       w4(Wd)[:, 4 * f:4 * f + 4, :]]
        for f in range(4):
            blocks += [w4(down)[:, 4 * f:4 * f + 4, :], w4(up)[:, 4 * f:4 * f + 4, :]]
        NB = len(blocks)
        FB = 7
        EB = FB + 12
        is_down = lambda n: n >= EB and (n - EB) % 2 == 0
        n_split = lambda n: sum(not is_down(m) for m in range(n))
        EARLY = 4
        stage_of = lambda n: 0 if n < EARLY or n % 2 == 0 else 1
        users = lambda n: [m for m in range(n) if stage_of(m) == stage_of(n)]
        staged = lambda n: (raw, work)[stage_of(n)][:, :]
        slot_of = lambda n: n % 4 if n < FB else (n - FB) % 5
        slot = lambda n, part: (XA[:, 4096:8192] if slot_of(n) == 4 else W[:, 4096 * slot_of(n):4096 * slot_of(n) + 4096])[
            :, 2048 * part:2048 * part + 2048]

        def wait_used(eng, n):
            kind, q = ((n - FB) % 3, (n - FB) // 3) if n < EB else ((n - EB) % 2, (n - EB) // 2)
            if n < 6:
                eng.wait_ge(s_wuse, n + 1)
            elif n == 6:
                eng.wait_ge(s_q2, 2)
            elif n < EB:
                eng.wait_ge(s_mo if kind == 2 else s_gu, 4 * q + 4)
            else:
                eng.wait_ge(s_eo if kind == 1 else s_w, 4 * q + 4)

        def slot_free(eng, n):
            before = [m for m in range(n) if slot_of(m) == slot_of(n)]
            if before or slot_of(n) == 4:
                wait_used(eng, before[-1] if before else 5)

        slot4 = lambda n, part: slot(n, part).rearrange("p (k n) -> p k n", k=4)

        def wait_staged(eng, n):
            eng.wait_ge((d_wA, d_wB)[stage_of(n)], 16 * (len(users(n)) + 1))

        OT = OTA[:, :].rearrange("p (s c t) -> p s c t", s=2, c=8)
        HT = XA[:, 0:2048].rearrange("p (s c t) -> p s c t", s=2, c=4)
        QTs = XA[:, 2048:4096].rearrange("p (s c t) -> p s c t", s=2, c=4)
        AT = XA[:, 4096:6144].rearrange("p (s c t) -> p s c t", s=2, c=4)
        VV = XA[:, 6144:8192].rearrange("p (s b n) -> p s b n", s=2, b=B)
        KB = KV[:, :].rearrange("p (s c b h t) -> p s c b h t", s=2, c=4, b=B, h=4)
        rope = sb("rope", [P, 2, 16])
        cmask = sb("cmask", [P, P])
        QR = late[:, 0:1024].rearrange("p (b n) -> p b n", b=B)
        KR = late[:, 1024:2048].rearrange("p (b n) -> p b n", b=B)
        RTMP = late[:, 2048:3072].rearrange("p (i h e) -> p i h e", i=4, h=SH)
        SM = late[:, 3072:4096].rearrange("p (c n) -> p c n", c=2)
        hn = Of[:, 0:1024].rearrange("p (b n) -> p b n", b=B)
        an = Of[:, 1024:2048].rearrange("p (b n) -> p b n", b=B)

        def passed(eng):
            eng.sem_inc(s_passed, 1)

        s_passed = sem("s_passed")

        QT2 = XA[:, 2048:4096].rearrange("p (s m t) -> p s m t", s=2, m=4)
        KBk = KV[:, 0:1024].rearrange("p (s m n) -> p s m n", s=2, m=4)
        SEL = KV[:, 1024:3072].rearrange("p (e n) -> p e n", e=ETS)
        GT = KV[:, 3072:4096].rearrange("p (c s n) -> p c s n", c=2, s=2)
        ACTT = KV[:, 4096:5120].rearrange("p (c s n) -> p c s n", c=2, s=2)
        RT = KV[:, 5120:6144].rearrange("p (h b t) -> p h b t", h=RH, b=B)
        GX = KV[:, 6144:8192].rearrange("p (s h b t) -> p s h b t", s=2, h=RH, b=B)
        SIM = late[:, 0:1024].rearrange("p (b n) -> p b n", b=B)
        SC = late[:, 1024:1280]
        REP = late[:, 1280:1536]
        CM = late[:, 1536:1792]
        EXC = late[:, 1792:2048]
        EQ = late[:, 2048:4096]
        EW, MW = late[:, 2048:3072], late[:, 3072:4096]
        GN = tail[:, 0:512].rearrange("p (h n) -> p h n", h=RH)
        RN = tail[:, 512:1024].rearrange("p (h n) -> p h n", h=RH)
        ME, MR = tail[:, 1024:1280], tail[:, 1280:1536]
        MA = tail[:, 1536:2048].rearrange("p (c n) -> p c n", c=2)
        HS = tail[:, 2048:2560].rearrange("p (c n) -> p c n", c=2)
        WE, WR_ = tail[:, 2560:2816], tail[:, 2816:3072]
        WC = tail[:, 3072:3584].rearrange("p (c n) -> p c n", c=2)
        V8, IXF, VALS, EV, N8 = (tail[:, a:b] for a, b in ((3584, 3648), (3648, 3712), (3712, 3744), (3744, 3776), (3776, 3808)))
        ZS, OFF, EXB = tail[:, 3808:3812], tail[:, 3812:3816], tail[:, 3816:3818]
        IOTA, W8, GE = tail[:, 3818:3882], tail[:, 3882:3890], tail[:, 3890:3922]
        IX = sb("IX", [P, 64], U32)
        delta = sb("delta", [1, P])
        exrow = sb("exrow", [1, T2])
        EXT = xst[:, 256:512]

        def tile_splits(ft):
            q, j = ft // 4, ft % 4
            if q < 3:
                return [FB + 3 * (q + 1) + {0: 0, 1: 1, 3: 2}[j]] if j != 2 else []
            return [EB + 1] if j == 1 else []
        block = stack.enter_context(nc.Block())
        x_v = x.rearrange("b p d -> p b d")
        ctx_v = ctx1024.rearrange("b (j n p) d -> b j p n d", n=NT, p=P)
        mask_v = mask.rearrange("b (j n) -> b j n", n=CW)

        @block.sync
        def _(sp):
            sp.dma_start(xres[:, :, :], x_v).then_inc(d_x, 16)
            for v, (w, at) in enumerate(((g1, 0), (b1, 4), (g2, 8), (b2, 12), (bg, 16), (bu, 32))):
                n = w.shape[0] // P
                sp.dma_start(vrow[at:at + n, :], w.rearrange("(a p) -> a p", p=P)).then_inc(d_vec, 16)
            sp.dma_start(raw[:, :].rearrange("p (k n) -> p k n", k=2), w4(Wq)[:, 0:2, :]).then_inc(d_wq, 16)
            sp.dma_start(O[:, :, :], w4(Wq)[:, 2:4, :]).then_inc(d_wq, 16)
            for k in range(KD):
                if k < 2:
                    sp.wait_ge(s_wql, k + 1)
                else:
                    sp.wait_ge(s_wkvl, k - 1)
                sp.dma_start((raw[:, :], Of)[k % 2], w4(Wkv)[:, k, :]).then_inc(d_wkv[k % 2], 16)

            def load_chunk(b, j):
                sp.dma_start(rawc, ctx_v[b, j]).then_inc(d_raw, 16)
                sp.dma_start(mraw[:, :], mask_v[b, j].partition_broadcast(P)).then_inc(d_mask, 16)

            sp.wait_ge(s_wkvl, 3)
            load_chunk(0, 0)

            def round_(it, last):
                if not (type(it) is int and it == 0) and not last:
                    r = 2 * it - 1
                    sp.wait_ge(s_xtr, 4 * r + 8)
                    passed(sp)
                    sp.wait_ge(s_mb, r + 1)
                    passed(sp)
                    load_chunk(0, it)
                if not last:
                    r = 2 * it
                    sp.wait_ge(s_xtr, 4 * r + 8)
                    passed(sp)
                    sp.wait_ge(s_mb, r + 1)
                    passed(sp)
                    load_chunk(1, it)

            round_(0, False)
            with sp.Fori(1, ROUNDS) as it:
                round_(it, False)

            sp.dma_start(rope[:, 0, :], rope_cos).then_inc(d_rope, 16)
            sp.dma_start(rope[:, 1, :], rope_sin).then_inc(d_rope, 16)
            sp.dma_start(cmask[:, :], causal).then_inc(d_rope, 16)
            for n in range(NB):
                if n == FB:
                    sp.wait_ge(s_pv2, 8)
                    sp.dma_start(EQ, select).then_inc(d_sel, 16)
                    for side in range(2):
                        sp.dma_start(xst[0:NK, 256 * side:256 * side + 256].rearrange("k (h n) -> k h n", h=RH),
                                     keys.rearrange("h k p n -> p k h n")[side]).then_inc(d_key, 16)
                if n == FB + 3:
                    sp.wait_ge(s_tt, 14)
                    sp.dma_start(hn[:, 0, :], bd.partition_broadcast(P)).then_inc(d_bd, 16)
                if n == 0:
                    sp.wait_ge(s_xtr, 4 * 2 * ROUNDS + 4)
                if n == EARLY + 1:
                    sp.wait_ge(s_pv, STEPS * (ROUNDS + 1))
                if users(n):
                    m = users(n)[-1]
                    if is_down(m):
                        sp.wait_ge(s_dt, 4 * ((m - EB) // 2 + 1))
                    else:
                        sp.wait_ge(s_wlo, n_split(m) + 1)
                sp.dma_start(staged(n).rearrange("p (k n) -> p k n", k=4), blocks[n]).then_inc((d_wA, d_wB)[stage_of(n)], 16)
            sp.wait_ge(s_fin, 1)
            sp.dma_start(out.rearrange("b p d -> p b d"), an).then_inc(d_out, 16)
            sp.wait_ge(d_out, 16)

        @block.gpsimd
        def _(pool):
            gp = nc.gpsimd
            gp.memset(ident[:, :], 0.0).then_inc(s_ident, 1)
            gp.memset(half[:, :], -0.5).then_inc(s_zero, 1)
            gp.memset(QA[:, :].bitcast(U32), 0).then_inc(s_zero, 1)
            gp.memset(work[:, :], 0.0).then_inc(s_zero, 1)
            pool.wait_ge(s_ident, 1)
            gp.affine_select(out=ident[:, :], in_=ident[:, :], compare_op=ALU.not_equal, fill=1.0,
                             base=0, pattern=[[-1, P]], channel_multiplier=1).then_inc(s_ident, 1)

            def rsqrt(n, ready, count, done):
                pool.wait_ge(ready, count)
                gp.tensor_scalar(rstd[:, 0:n], mv[:, 0:n, 1], EPS, None, ALU.add).then_inc(s_rst, 1)
                rs_count[0] += 1
                pool.wait_ge(s_rst, rs_count[0])
                gp.tensor_tensor(rstd[:, 0:n], rstd[:, 0:n], half[:, 0:n], ALU.pow).then_inc(done, 1)

            rs_count = [0]
            pool.wait_ge(s_zero, 3)
            rsqrt(2, s_stat, 1, s_lat)
            rsqrt(2, s_stat, 2, s_lat)

            def split_block(e, dst_hi, dst_lo, n, view):
                pool.wait_ge(s_xev, e + 1)
                passed(pool)
                gp.tensor_copy(dst_hi, view(xst[:, 0:n])).then_inc(s_xh, 1)
                pool.wait_ge(s_xh, e + 1)
                gp.tensor_tensor(dst_lo, view(xst[:, 0:n]), dst_hi.bitcast(F32), ALU.subtract).then_inc(s_xT, 1)

            for k in range(KD):
                split_block(k, XT[:, :, HI, k, 0:P], XT[:, :, LO, k, 0:P], T2, lambda v: v.rearrange("p (b n) -> p b n", b=B))

            def chunk_norm(r, par):
                pool.wait_ge(s_stat, r + 3)
                passed(pool)
                gp.tensor_scalar(rstd[:, :], mv[:, :, 1], EPS, None, ALU.add).then_inc(s_rst, 1)
                pool.wait_ge(s_rst, 2 * r + 3)
                gp.tensor_tensor(rstd[:, :], rstd[:, :], half[:, :], ALU.pow).then_inc(s_rst, 1)
                pool.wait_ge(s_rst, 2 * r + 4)
                passed(pool)
                for t in range(NT):
                    last = gp.tensor_scalar(rawc[:, t, :], rawc[:, t, :], mv[:, t, 0:1], rstd[:, t:t + 1],
                                            ALU.subtract, ALU.mult)
                last.then_inc(s_norm, 1)
                pool.wait_ge(d_mask, 16 * r + 16)
                passed(pool)
                gp.tensor_scalar(MB[:, par, :], mraw[:, :], BIG, -BIG, ALU.mult, ALU.add).then_inc(s_mb, 1)

            def unit(it, u, first):
                b, g, par = u // G, u % G, u % 2
                U = UNITS * it + u
                hs = slice(HG * g, HG * g + HG)
                pool.wait_ge(s_negm, HG * U + HG)
                if not first:
                    gp.tensor_tensor(dm[:, par, :], mold[:, b, hs], mcur[:, par, :], ALU.subtract).then_inc(s_dmt, 1)
                    pool.wait_ge(s_dmt, U - UNITS + 1)
                passed(pool)
                gp.tensor_copy(mold[:, b, hs], mcur[:, par, :]).then_inc(s_dm, 1)
                pool.wait_ge(s_exp, HG * U + HG)
                if first:
                    gp.tensor_copy(lsum[:, b, hs], rs[:, par, :]).then_inc(s_osc, 1)
                else:
                    pool.wait_ge(s_alpha, U - UNITS + 1)
                    gp.tensor_tensor(lsum[:, b, hs], lsum[:, b, hs], alpha[:, par, :], ALU.mult).then_inc(s_lt, 1)
                    ov = O[:, b, 256 * g:256 * g + 256].rearrange("p (h e) -> p h e", h=HG)
                    gp.tensor_tensor(ov, ov, alpha[:, par, :].unsqueeze(2).broadcast_to([P, HG, DH]), ALU.mult)
                    pool.wait_ge(s_lt, U - UNITS + 1)
                    gp.tensor_tensor(lsum[:, b, hs], lsum[:, b, hs], rs[:, par, :], ALU.add).then_inc(s_osc, 1)

            def round_(it, first, last):
                for u in range(UNITS):
                    c = u // G
                    prep = (c == 0 and not first) or (c == 1 and not last)
                    r = 2 * it - 1 + c
                    if prep and u % G in (1, 2):
                        for k in (2 * (u % G) - 2, 2 * (u % G) - 1):
                            split_block(4 + 4 * r + k, XT[:, 1 - c, HI, k, :], XT[:, 1 - c, LO, k, :], CW, lambda v: v)
                    unit(it, u, first)
                    if prep and u % G == 0:
                        chunk_norm(r, 1 - c)

            round_(0, True, False)
            with pool.Fori(1, ROUNDS) as it:
                round_(it, False, False)
            round_(ROUNDS, False, True)

            def split_hi(n):
                wait_staged(pool, n)
                if n == 0:
                    pool.wait_ge(s_proj, STEPS * (ROUNDS + 1))
                slot_free(pool, n)
                gp.tensor_copy(slot(n, HI), staged(n)).then_inc(s_whi, 1)

            def row_rstd(i):
                pool.wait_ge(s_ln, i + 1)
                gp.tensor_scalar(rstd[:, 0:2], mv[:, 0:2, 1], EPS, None, ALU.add).then_inc(s_rst, 1)
                pool.wait_ge(s_rst, 2 + 2 * 2 * ROUNDS + i + 1)
                gp.tensor_tensor(rstd[:, 0:2], rstd[:, 0:2], half[:, 0:2], ALU.pow).then_inc(s_pn, 1)

            for n in range(EARLY):
                split_hi(n)
            pool.wait_ge(s_pv, STEPS * (ROUNDS + 1))
            gp.memset(KV[:, :].bitcast(U32), 0).then_inc(s_kz, 1)
            row_rstd(0)
            for n in range(EARLY, FB):
                split_hi(n)
            row_rstd(1)
            pool.wait_ge(s_pv2, 8)
            gp.memset(KV[:, 0:1024].bitcast(U32), 0).then_inc(s_kz, 1)
            gp.iota(IOTA, [[1, NK]], base=0, channel_multiplier=0, allow_small_or_imprecise_dtypes=True)
            gp.iota(W8, [[-1, 8]], base=8, channel_multiplier=0, allow_small_or_imprecise_dtypes=True)
            gp.memset(delta[:, :], 0.0).then_inc(s_iota, 1)
            pool.wait_ge(s_iota, 1)
            gp.memset(delta[:, P - 1:P], 1.0).then_inc(s_iota, 1)
            pool.wait_ge(d_sel, 16)
            gp.tensor_copy(KV[:, 1024:3072], EQ).then_inc(s_selr, 1)
            for n in range(FB, FB + 3):
                split_hi(n)
            for ft in range(16):
                for n in tile_splits(ft):
                    split_hi(n)
            for e in range(ETS):
                if e % 4 == 0 and e > 0:
                    split_hi(EB + 2 * (e // 4) + 1)
                pool.wait_ge(s_md, e + 1)
                gp.tensor_tensor(MW[:, 0:512], MW[:, 0:512], MW[:, 512:1024], ALU.add).then_inc(s_hs1, 1)
                pool.wait_ge(s_hs1, e + 1)
                if e >= 2:
                    pool.wait_ge(s_c, e - 1)
                gp.tensor_tensor(HS[:, e % 2, :], MW[:, 0:256], MW[:, 256:512], ALU.add).then_inc(s_hs, 1)


        @block.scalar
        def _(act):
            ac = nc.scalar
            act.wait_ge(s_vt, 1)
            ac.activation(vec[:, :], pX[:, 0:48], ACT.Copy).then_inc(s_vec, 1)
            act.wait_ge(d_wq, 32)
            ac.activation(WQ[:, HI, 0:2, :], raw[:, :].rearrange("p (k n) -> p k n", k=2), ACT.Copy).then_inc(s_wqh, 1)
            ac.activation(WQ[:, HI, 2:4, :], O[:, :, :], ACT.Copy).then_inc(s_wqh, 1)
            act.wait_ge(s_vec, 1)
            ac.mul(nbg[:, :], vec[:, Kbg:Kbg + 16], -1.0)

            def wkv_hi(k):
                act.wait_ge(d_wkv[k % 2], 16 * (k // 2 + 1))
                ac.activation(WKV[:, HI, k, :], (raw[:, :], Of)[k % 2], ACT.Copy).then_inc(s_wkvh, 1)

            def x_evac(e, n, kg, kb):
                act.wait_ge(s_xtr, e + 1)
                if not (type(e) is int and e == 0):
                    act.wait_ge(s_xT, e)
                ac.activation(xst[:, 0:n], pX[:, 0:n], ACT.Identity, bias=vec[:, kb:kb + 1],
                              scale=vec[:, kg:kg + 1]).then_inc(s_xev, 1)

            for k in range(KD):
                x_evac(k, T2, Kg2 + k, Kb2 + k)
            for k in range(2):
                wkv_hi(k)
            for m in range(H // 2):
                act.wait_ge(s_q, m + 1)
                if m == 0:
                    act.wait_ge(s_zero, 3)
                ac.activation(QT[0:DH, HI, 2 * m, :], pJ[0:DH, m % 2, 0:T2], ACT.Copy)
                ac.activation(QT[DH:P, HI, 2 * m + 1, :], pJ[DH:P, m % 2, 0:T2], ACT.Copy).then_inc(s_qh, 1)
                if m in (2, 5):
                    wkv_hi(2 + m // 5)

            def kv_hi(it, u, i, w, first):
                par = u % 2
                q = STEPS * it + HG * u + i
                act.wait_ge(s_proj, q + 1)
                if not (first and u < 2):
                    act.wait_ge(s_qk if i < 2 else s_pv, q - i - HG)
                kv_copy(par, i, w, lambda dst, src: ac.activation(dst, src, ACT.Copy)).then_inc(s_kvh, 1)

            def kv_copy(par, i, w, op):
                src = pJ[:, i % 2, 0:w]
                if i < 2:
                    return op(KT[:, par, HI, i, 0:w], src)
                if w == CW:
                    return op(VT[:, par, HI, 2 * i - 4:2 * i - 2, :], src.rearrange("p (t n) -> p t n", t=2))
                return op(VT[:, par, HI, 0, P * (i - 2):P * (i - 1)], src)

            for i in range(HG):
                kv_hi(0, 0, i, P, True)

            def round_(it, first, last):
                w = P if first else CW

                def pt_hi(t):
                    T = STEPS * it + t
                    act.wait_ge(s_tr, T + 1)
                    if not (first and t < 2):
                        act.wait_ge(s_pv, T - 1)
                    ac.activation(PT[:, t % 2, HI, 0:w], pT[:, t % 2, 0:w], ACT.Copy).then_inc(s_pth, 1)

                def rescale(u):
                    if not first:
                        U = UNITS * it + u
                        act.wait_ge(s_dm, U + 1)
                        ac.activation(alpha[:, u % 2, :], dm[:, u % 2, :], ACT.Exp, scale=XSC).then_inc(s_alpha, 1)

                for t in range(STEPS):
                    u, i, c = t // HG, t % HG, t // (STEPS // 2)
                    par = u % 2
                    T = STEPS * it + t
                    act.wait_ge(s_negm, T + 1)
                    if i == 0 and not (first and u < 2):
                        act.wait_ge(s_osc, UNITS * it + u - 1)
                    ac.activation(SP[:, t % 2, 0:w], SP[:, t % 2, 0:w], ACT.Exp, bias=negm[:, par, i:i + 1],
                                  scale=XSC, accum_out=rs[:, par, i:i + 1]).then_inc(s_exp, 1)
                    if not (last and u == UNITS - 1):
                        kv_hi(it, u + 1, i, w if u + 1 < UNITS else CW, first)
                    if i == 0 and u > 0:
                        rescale(u - 1)
                    if t > 0:
                        pt_hi(t - 1)
                    k = t % (STEPS // 2) - 6
                    if 0 <= k < KD and ((c == 0 and not first) or (c == 1 and not last)):
                        x_evac(4 + 4 * (2 * it - 1 + c) + k, CW, Kg1 + k, Kb1 + k)
                rescale(UNITS - 1)
                pt_hi(STEPS - 1)

            round_(0, True, False)
            with act.Fori(1, ROUNDS) as it:
                round_(it, False, False)
            round_(ROUNDS, False, True)

            nb = [0]

            def transposed_hi(dst, n_banks):
                for cc in range(n_banks):
                    act.wait_ge(s_tt, nb[0] + 1)
                    ac.activation(dst[:, HI, 2 * cc:2 * cc + 2, :], pT[:, nb[0] % 2, :].rearrange("p (c t) -> p c t", c=2),
                                  ACT.Copy).then_inc(s_th, 1)
                    nb[0] += 1

            transposed_hi(OT, 4)
            transposed_hi(HT, 2)
            act.wait_ge(s_wuse, 5)
            for b in range(B):
                ac.activation(VV[:, HI, b, :], (pV, pX)[b][:, :], ACT.Copy).then_inc(s_vh, 1)
            transposed_hi(QTs, 2)
            act.wait_ge(s_kz, 1)
            for cc in range(2):
                act.wait_ge(s_tt, nb[0] + 1)
                for h in range(4):
                    rows = slice(SD * h, SD * h + SD)
                    last = ac.activation(KB[rows, HI, 2 * cc:2 * cc + 2, :, h, :],
                                         pT[rows, nb[0] % 2, :].rearrange("p (c b t) -> p c b t", c=2, b=B), ACT.Copy)
                last.then_inc(s_th, 1)
                nb[0] += 1

            def p_hi(n):
                act.wait_ge(s_pt2, n + 1)
                if n >= 2:
                    act.wait_ge(s_pv2, n - 1)
                ac.activation(PT[:, n % 2, HI, :], pJ[:, n % 2, :], ACT.Copy).then_inc(s_p2h, 1)

            for n in range(8):
                act.wait_ge(s_sm, n + 1)
                ac.activation(SM[:, n % 2, :], SM[:, n % 2, :], ACT.Exp, scale=SSC).then_inc(s_se, 1)
                if n >= 1:
                    p_hi(n - 1)
            p_hi(7)
            transposed_hi(AT, 2)
            transposed_hi(HT, 2)

            act.wait_ge(s_kt, 1)
            act.wait_ge(s_kz, 2)
            kz = pV[:, 0:256].rearrange("p (m n) -> p m n", m=4)
            ac.activation(KBk[0:NK, HI, :, 0:NK], kz[0:NK], ACT.Copy)
            ac.activation(KBk[NK:P, HI, :, NK:P], kz[NK:P], ACT.Copy).then_inc(s_kh, 1)
            for j in range(2):
                act.wait_ge(s_q2, j + 1)
                ac.activation(QT2[:, HI, 2 * j:2 * j + 2, :], pS[:, j, :].rearrange("p (m t) -> p m t", m=2), ACT.Copy).then_inc(s_q2h, 1)

            def gate_exp(ft):
                act.wait_ge(s_gu, ft + 1)
                if ft >= 1:
                    act.wait_ge(s_a, ft)
                ac.activation(ME, pS[:, ft % 2, 0:T2], ACT.Exp, bias=nbg[:, ft:ft + 1], scale=-1.0).then_inc(s_ge, 1)

            gate_exp(0)
            for ft in range(16):
                act.wait_ge(s_a, ft + 1)
                if ft >= 2:
                    act.wait_ge(s_mo, ft - 1)
                ac.activation(ACTT[:, ft % 2, HI, :], MA[:, ft % 2, :], ACT.Copy).then_inc(s_ah, 1)
                if ft < 15:
                    gate_exp(ft + 1)
                j = ft % 5
                if ft < 10 and j == 1:
                    act.wait_ge(s_tk, 3 * (ft // 5) + 1)
                    ac.activation(EV, EV, ACT.Exp).then_inc(s_tke, 1)
                if ft < 10 and j == 2:
                    act.wait_ge(s_tk, 3 * (ft // 5) + 2)
                    ac.activation(ZS, ZS, ACT.Ln).then_inc(s_tke, 1)
                if ft < 10 and j == 3:
                    act.wait_ge(s_tk, 3 * (ft // 5) + 3)
                    ac.activation(EXC, EXC, ACT.Exp).then_inc(s_tke, 1)
                if ft in (6, 11):
                    b = ft // 11
                    act.wait_ge(s_gt, b + 1)
                    ac.activation(GX[:, HI, :, b, :], pJ[:, b, :].rearrange("p (h t) -> p h t", h=RH), ACT.Copy)
                    ac.activation(RT[:, :, b, :], pT[:, b, :].rearrange("p (h t) -> p h t", h=RH), ACT.Copy).then_inc(s_gh, 1)

            def front(e):
                n = EB + 2 * (e // 4)
                act.wait_ge(s_dt, e + 1)
                if e % 4 == 0:
                    slot_free(act, n)
                ac.activation(slot(n, HI)[:, 512 * (e % 4):512 * (e % 4) + 512], pS[:, 0, :], ACT.Copy).then_inc(s_dh, 1)
                act.wait_ge(s_gd, e + 1)
                if e >= 1:
                    act.wait_ge(s_md, e)
                ac.activation(EW, pJ[:, :, :].rearrange("p a n -> p (a n)"), ACT.Exp).then_inc(s_gexp, 1)

            front(0)
            for e in range(ETS):
                if e + 1 < ETS:
                    front(e + 1)
                act.wait_ge(s_w, e + 1)
                if e >= 1:
                    act.wait_ge(s_c, e)
                ac.activation(WE, pS[:, 1, 0:T2], ACT.Exp, scale=-1.0).then_inc(s_we, 1)
                act.wait_ge(s_c, e + 1)
                if e >= 2:
                    act.wait_ge(s_eo, e - 1)
                ac.activation(GT[:, e % 2, HI, :], WC[:, e % 2, :], ACT.Copy).then_inc(s_chi, 1)

        @block.vector
        def _(dve):
            ve = nc.vector
            links = [0]

            def link(ins):
                links[0] += 1
                ins.then_inc(s_ch, 1)
                dve.wait_ge(s_ch, links[0])

            def low(dst, src, hi):
                return ve.tensor_tensor(dst, src, hi.bitcast(F32), ALU.subtract)

            dve.wait_ge(d_x, 16)
            for i, src in enumerate((xres, SP)):
                for b in range(B):
                    last = ve.bn_stats(st[:, b, :], src[:, b, :])
                link(last)
                for b in range(B):
                    last = ve.bn_aggr(mv[:, b, :], st[:, b, :])
                last.then_inc(s_stat, 1)
                dve.wait_ge(s_lat, i + 1)
                dve.wait_ge(s_stat, i + 1)
                for b in range(B):
                    last = ve.tensor_scalar(SP[:, b, :], src[:, b, :], mv[:, b, 0:1], rstd[:, b:b + 1], ALU.subtract, ALU.mult)
                if i == 0:
                    link(last)
                else:
                    last.then_inc(s_latn, 1)
            for j in range(2):
                dve.wait_ge(s_wqh, j + 1)
                src = (raw[:, :].rearrange("p (k n) -> p k n", k=2), O[:, :, :])[j]
                low(WQ[:, LO, 2 * j:2 * j + 2, :], src, WQ[:, HI, 2 * j:2 * j + 2, :]).then_inc(s_wql, 1)

            def wkv_lo(k):
                dve.wait_ge(s_wkvh, k + 1)
                low(WKV[:, LO, k, :], (raw[:, :], Of)[k % 2], WKV[:, HI, k, :]).then_inc(s_wkvl, 1)

            for k in range(2):
                wkv_lo(k)
            for m in range(H // 2):
                dve.wait_ge(s_qh, m + 1)
                low(QT[0:DH, LO, 2 * m, :], pJ[0:DH, m % 2, 0:T2], QT[0:DH, HI, 2 * m, :])
                low(QT[DH:P, LO, 2 * m + 1, :], pJ[DH:P, m % 2, 0:T2], QT[DH:P, HI, 2 * m + 1, :]).then_inc(s_ql, 1)
                if m in (2, 5):
                    wkv_lo(2 + m // 5)

            def kv_lo(it, u, i, w):
                par = u % 2
                dve.wait_ge(s_kvh, STEPS * it + HG * u + i + 1)
                src = pJ[:, i % 2, 0:w]
                if i < 2:
                    ins = low(KT[:, par, LO, i, 0:w], src, KT[:, par, HI, i, 0:w])
                elif w == CW:
                    ts = slice(2 * i - 4, 2 * i - 2)
                    ins = low(VT[:, par, LO, ts, :], src.rearrange("p (t n) -> p t n", t=2), VT[:, par, HI, ts, :])
                else:
                    cs = slice(P * (i - 2), P * (i - 1))
                    ins = low(VT[:, par, LO, 0, cs], src, VT[:, par, HI, 0, cs])
                ins.then_inc(s_kvl, 1)

            for i in range(HG):
                kv_lo(0, 0, i, P)

            def round_(it, first, last):
                w = P if first else CW

                def pt_lo(t):
                    dve.wait_ge(s_pth, STEPS * it + t + 1)
                    low(PT[:, t % 2, LO, 0:w], pT[:, t % 2, 0:w], PT[:, t % 2, HI, 0:w]).then_inc(s_ptl, 1)

                def add_output(u):
                    U = UNITS * it + u
                    b, g = u // G, u % G
                    o = O[:, b, 256 * g:256 * g + 256]
                    dve.wait_ge(s_pv, HG * U + HG)
                    dve.wait_ge(s_osc, U + 1)
                    if first:
                        ve.tensor_copy(o, pV[:, 0:256]).then_inc(s_oadd, 1)
                    else:
                        ve.tensor_tensor(o, pV[:, 0:256], o, ALU.add).then_inc(s_oadd, 1)

                for t in range(STEPS):
                    u, i, c = t // HG, t % HG, t // (STEPS // 2)
                    b, g, par = u // G, u % G, u % 2
                    T = STEPS * it + t
                    prep = (c == 0 and not first) or (c == 1 and not last)
                    r = 2 * it - 1 + c
                    dve.wait_ge(s_qk, T + 1)
                    if not (first and t < 2):
                        dve.wait_ge(s_tr, T - 1)
                    if i == 0 and not (first and u < 2):
                        dve.wait_ge(s_dm, UNITS * it + u - 1)
                    if t % 16 == 0 and not first:
                        dve.wait_ge(s_mb, 2 * it - 1 + c)
                    passed(dve)
                    ve.tensor_tensor_reduce(out=SP[:, t % 2, 0:w], in0=pS[:, t % 2, 0:w], in1=MB[:, c, 0:w], scale=1.0,
                                            scalar=-3e38 if first else mold[:, b, HG * g + i:HG * g + i + 1],
                                            op0=ALU.add, op1=ALU.max, accum_out=mcur[:, par, i:i + 1]).then_inc(s_ttr, 1)
                    dve.wait_ge(s_ttr, T + 1)
                    ve.tensor_scalar(negm[:, par, i:i + 1], mcur[:, par, i:i + 1], -XSC, None, ALU.mult).then_inc(s_negm, 1)
                    if i == 1 and u > 0:
                        add_output(u - 1)
                    if not (last and u == UNITS - 1):
                        kv_lo(it, u + 1, i, w if u + 1 < UNITS else CW)
                    if t > 0:
                        pt_lo(t - 1)
                    if prep and t % 16 < NT:
                        if t % 16 == 0:
                            dve.wait_ge(d_raw, 16 * r + 16)
                        ve.bn_stats(st[:, t % 16, :], rawc[:, t % 16, :]).then_inc(s_bn, 1)
                        if t % 16 == NT - 1:
                            dve.wait_ge(s_bn, NT * r + NT)
                            passed(dve)
                            for k in range(NT):
                                ins = ve.bn_aggr(mv[:, k, :], st[:, k, :])
                            ins.then_inc(s_stat, 1)
                pt_lo(STEPS - 1)
                add_output(UNITS - 1)

            round_(0, True, False)
            with dve.Fori(1, ROUNDS) as it:
                round_(it, False, False)
            round_(ROUNDS, False, True)

            def split_lo(n):
                dve.wait_ge(s_whi, n_split(n) + 1)
                low(slot(n, LO), staged(n), slot(n, HI)).then_inc(s_wlo, 1)

            for n in range(EARLY):
                split_lo(n)
            nb = [0]

            def transposed_lo(dst, n_banks):
                for cc in range(n_banks):
                    dve.wait_ge(s_th, nb[0] + 1)
                    low(dst[:, LO, 2 * cc:2 * cc + 2, :], pT[:, nb[0] % 2, :].rearrange("p (c t) -> p c t", c=2),
                        dst[:, HI, 2 * cc:2 * cc + 2, :]).then_inc(s_tl, 1)
                    nb[0] += 1

            def add_rows(i, norm):
                dve.wait_ge(s_wuse, (2, 6)[i])
                for b in range(B):
                    last = ve.tensor_tensor(xres[:, b, :], pS[:, b, :], xres[:, b, :], ALU.add)
                last.then_inc(s_yread, 1)
                dve.wait_ge(s_yread, i + 1)
                for b in range(B):
                    last = ve.bn_stats(st[:, b, :], xres[:, b, :])
                link(last)
                for b in range(B):
                    last = ve.bn_aggr(mv[:, b, :], st[:, b, :])
                last.then_inc(s_ln, 1)
                dve.wait_ge(s_ln, i + 1)
                dve.wait_ge(s_pn, i + 1)
                for b in range(B):
                    last = ve.tensor_scalar(hn[:, b, :], xres[:, b, :], mv[:, b, 0:1], rstd[:, b:b + 1], ALU.subtract, ALU.mult)
                last.then_inc(s_src, 1)

            dve.wait_ge(s_osc, UNITS * (ROUNDS + 1))
            dve.wait_ge(s_oadd, UNITS * (ROUNDS + 1))
            link(ve.reciprocal(small[:, 0:32], lsum[:, :, :].rearrange("p b h -> p (b h)")))
            ov = Of.rearrange("p (h e) -> p h e", e=DH)
            ve.tensor_tensor(ov, ov, small[:, 0:32].unsqueeze(2).broadcast_to([P, B * H, DH]), ALU.mult).then_inc(s_src, 1)
            transposed_lo(OT, 4)
            add_rows(0, True)
            transposed_lo(HT, 2)
            for n in range(EARLY, FB):
                split_lo(n)

            dve.wait_ge(d_rope, 48)
            for m, (bank, R) in enumerate(((pS, QR), (pJ, KR))):
                dve.wait_ge(s_wuse, m + 3)
                for b in range(B):
                    z = bank[:, b, :].rearrange("p (h e two) -> p h e two", h=SH, two=2)
                    r = R[:, b, :].rearrange("p (h e two) -> p h e two", h=SH, two=2)
                    cos = rope[:, 0, :].unsqueeze(1).broadcast_to([P, SH, SD // 2])
                    sin = rope[:, 1, :].unsqueeze(1).broadcast_to([P, SH, SD // 2])
                    ve.tensor_tensor(RTMP[:, 0], z[:, :, :, 0], cos, ALU.mult)
                    ve.tensor_tensor(RTMP[:, 1], z[:, :, :, 1], sin, ALU.mult)
                    ve.tensor_tensor(RTMP[:, 2], z[:, :, :, 0], sin, ALU.mult)
                    link(ve.tensor_tensor(RTMP[:, 3], z[:, :, :, 1], cos, ALU.mult))
                    ve.tensor_tensor(r[:, :, :, 0], RTMP[:, 0], RTMP[:, 1], ALU.subtract)
                    ve.tensor_tensor(r[:, :, :, 1], RTMP[:, 2], RTMP[:, 3], ALU.add).then_inc(s_rope, 1)
                    dve.wait_ge(s_rope, 2 * m + b + 1)
            for b in range(B):
                dve.wait_ge(s_vh, b + 1)
                low(VV[:, LO, b, :], (pV, pX)[b][:, :], VV[:, HI, b, :]).then_inc(s_vl, 1)
            transposed_lo(QTs, 2)
            for cc in range(2):
                dve.wait_ge(s_th, nb[0] + 1)
                for h in range(4):
                    rows = slice(SD * h, SD * h + SD)
                    last = low(KB[rows, LO, 2 * cc:2 * cc + 2, :, h, :],
                               pT[rows, nb[0] % 2, :].rearrange("p (c b t) -> p c b t", c=2, b=B),
                               KB[rows, HI, 2 * cc:2 * cc + 2, :, h, :])
                last.then_inc(s_tl, 1)
                nb[0] += 1

            def p_lo(n):
                dve.wait_ge(s_se, n + 1)
                b, c = n // 4, n % 4
                ve.tensor_reduce(small[:, 16 * b + 4 * c:16 * b + 4 * c + 4], SM[:, n % 2, :].rearrange("p (h t) -> p h t", h=4),
                                 AX.X, ALU.add)
                dve.wait_ge(s_p2h, n + 1)
                low(PT[:, n % 2, LO, :], pJ[:, n % 2, :], PT[:, n % 2, HI, :]).then_inc(s_p2l, 1)

            for n in range(8):
                sm = SM[:, n % 2, :].rearrange("p (h t) -> p h t", h=4)
                dve.wait_ge(s_sc, n + 1)
                if n >= 2:
                    dve.wait_ge(s_pt2, n - 1)
                link(ve.tensor_tensor(sm, pS[:, n % 2, :].rearrange("p (h t) -> p h t", h=4),
                                      cmask[:, :].unsqueeze(1).broadcast_to([P, 4, P]), ALU.add))
                link(ve.tensor_reduce(small[:, 32:36], sm, AX.X, ALU.max))
                ve.tensor_tensor(sm, sm, small[:, 32:36].unsqueeze(2).broadcast_to([P, 4, P]), ALU.subtract).then_inc(s_sm, 1)
                if n >= 1:
                    p_lo(n - 1)
            p_lo(7)
            dve.wait_ge(s_p2l, 8)
            link(ve.reciprocal(small[:, 0:32], small[:, 0:32]))
            dve.wait_ge(s_pv2, 8)
            for b in range(B):
                last = ve.tensor_tensor(an[:, b, :].rearrange("p (h e) -> p h e", e=SD),
                                        (pV, pX)[b][:, :].rearrange("p (h e) -> p h e", e=SD),
                                        small[:, 16 * b:16 * b + 16].unsqueeze(2).broadcast_to([P, SH, SD]), ALU.mult)
            last.then_inc(s_src, 1)
            transposed_lo(AT, 2)
            add_rows(1, True)
            transposed_lo(HT, 2)
            for n in (FB, FB + 1):
                split_lo(n)
            dve.wait_ge(s_kh, 1)
            kz = pV[:, 0:256].rearrange("p (m n) -> p m n", m=4)
            low(KBk[0:NK, LO, :, 0:NK], kz[0:NK], KBk[0:NK, HI, :, 0:NK])
            low(KBk[NK:P, LO, :, NK:P], kz[NK:P], KBk[NK:P, HI, :, NK:P]).then_inc(s_kl, 1)
            for j in range(2):
                dve.wait_ge(s_q2h, j + 1)
                low(QT2[:, LO, 2 * j:2 * j + 2, :], pS[:, j, :].rearrange("p (m t) -> p m t", m=2), QT2[:, HI, 2 * j:2 * j + 2, :]).then_inc(s_q2l, 1)
            split_lo(FB + 2)
            for b in range(B):
                dve.wait_ge(s_sim, b + 1)
                ve.tensor_copy(SIM[:, b, :], pJ[:, b, :]).then_inc(s_simc, 1)
            dve.wait_ge(s_simc, 2)
            dve.wait_ge(d_bd, 16)
            for b in range(B):
                ve.tensor_tensor(an[:, b, :], xres[:, b, :], hn[:, 0, :], ALU.add)

            hk = lambda t: t.rearrange("p (h k) -> p h k", h=RH)
            V8v = V8.rearrange("p (s h k) -> p s h k", s=2, h=RH)
            IXv = IX[:, :].rearrange("p (s h k) -> p s h k", s=2, h=RH)
            IXFv = IXF.rearrange("p (s n) -> p s n", s=2)
            SC4 = SC.rearrange("p (h a k) -> p h a k", h=RH, a=8)
            SC3 = SC.rearrange("p (h n) -> p h n", h=RH)
            EXC3 = EXC.rearrange("p (h n) -> p h n", h=RH)
            EQ3 = EQ.rearrange("p (n k) -> p n k", k=NK)

            def top_sides(b):
                for s in range(2):
                    for h in range(RH):
                        col = 256 * s + NK * h
                        last = ve.max(V8v[:, s, h, :], SIM[:, b, col:col + NK])
                link(last)
                for s in range(2):
                    for h in range(RH):
                        col = 256 * s + NK * h
                        last = ve.max_index(IXv[:, s, h, :], V8v[:, s, h, :], SIM[:, b, col:col + NK])
                link(last)
                ve.tensor_copy(IXF, IX[:, :])
                link(ve.tensor_tensor(SC4, V8v[:, 0].unsqueeze(3).broadcast_to([P, RH, 8, 8]),
                                      V8v[:, 1].unsqueeze(2).broadcast_to([P, RH, 8, 8]), ALU.add))

            def top_sums(b):
                for h in range(RH):
                    last = ve.max(hk(VALS)[:, h, :], SC3[:, h, :])
                link(last)
                for h in range(RH):
                    last = ve.match_replace(REP.rearrange("p (h n) -> p h n", h=RH)[:, h, :], hk(VALS)[:, h, :], SC3[:, h, :], -3e38)
                ve.tensor_tensor(hk(EV), hk(VALS), hk(VALS)[:, :, 0:1].broadcast_to([P, RH, 8]), ALU.subtract).then_inc(s_tk, 1)
                dve.wait_ge(s_tk, 3 * b + 1)
                link(ve.tensor_tensor(CM, REP, SC, ALU.not_equal))
                link(ve.tensor_reduce(N8, CM.rearrange("p (n k) -> p n k", k=8), AX.X, ALU.add))

            def softmax_sum(b):
                dve.wait_ge(s_tke, 3 * b + 1)
                ve.tensor_reduce(ZS, hk(EV), AX.X, ALU.add).then_inc(s_tk, 1)

            def place_x(b):
                dve.wait_ge(s_tke, 3 * b + 2)
                if b == 1:
                    dve.wait_ge(s_gt, 1)
                link(ve.tensor_tensor(OFF, hk(VALS)[:, :, 0], ZS, ALU.add))
                ve.tensor_tensor(EXC3, SC3, OFF.unsqueeze(2).broadcast_to([P, RH, NK]), ALU.subtract).then_inc(s_tk, 1)
                sim = SIM[:, b, :].rearrange("p (s h n) -> p s h n", s=2, h=RH)
                ve.tensor_tensor(GN[:, :, 0:NK], sim[:, 0], OFF.unsqueeze(2).broadcast_to([P, RH, NK]), ALU.subtract)
                ve.tensor_copy(GN[:, :, NK:P], sim[:, 1])
                place(0, N8.unsqueeze(2).broadcast_to([P, 32, NK]), EQ3)
                ve.tensor_reduce(RN[:, :, 0:NK], EQ.rearrange("p (h a n) -> p h n a", h=RH, a=8), AX.X, ALU.add).then_inc(s_pl, 1)
                dve.wait_ge(s_pl, 2 * b + 1)

            def place(side, weight, eq):
                if side == 0:
                    dve.wait_ge(s_selr, 1)
                link(ve.tensor_tensor(EQ3, IOTA.unsqueeze(1).broadcast_to([P, 32, NK]),
                                      IXFv[:, side, :].unsqueeze(2).broadcast_to([P, 32, NK]), ALU.is_equal))
                link(ve.tensor_tensor(eq, eq, weight, ALU.mult))

            def place_y(b):
                place(1, W8.unsqueeze(1).unsqueeze(3).broadcast_to([P, RH, 8, NK]), EQ.rearrange("p (h a n) -> p h a n", h=RH, a=8))
                ve.tensor_reduce(RN[:, :, NK:P], EQ.rearrange("p (h a n) -> p h n a", h=RH, a=8), AX.X, ALU.add).then_inc(s_pl, 1)
                dve.wait_ge(s_pl, 2 * b + 2)
                ve.tensor_scalar(RN[:, :, NK:P], RN[:, :, NK:P], -8.0, None, ALU.add).then_inc(s_gn, 1)
                ve.tensor_scalar(GE, IXFv[:, 0, :], float(NEXP // NK), None, ALU.is_ge)
                dve.wait_ge(s_tke, 3 * b + 3)
                link(ve.tensor_tensor(EXC, EXC, CM, ALU.mult))
                e8 = EXC.rearrange("p (n k) -> p n k", k=8)
                link(ve.tensor_tensor(e8, e8, GE.unsqueeze(2).broadcast_to([P, 32, 8]), ALU.mult))
                link(ve.tensor_reduce(EXB[:, b:b + 1], EXC, AX.X, ALU.add))

            dve.wait_ge(s_iota, 2)
            for ft in range(16):
                dve.wait_ge(s_ge, ft + 1)
                link(ve.tensor_scalar(ME, ME, 1.0, None, ALU.add))
                link(ve.reciprocal(MR, ME))
                link(ve.scalar_tensor_tensor(out=MR, in0=pS[:, ft % 2, 0:T2], scalar=vec[:, Kbg + ft:Kbg + ft + 1], in1=MR,
                                             op0=ALU.add, op1=ALU.mult))
                ve.scalar_tensor_tensor(out=MA[:, ft % 2, :], in0=pS[:, ft % 2, T2:2 * T2], scalar=vec[:, Kbu + ft:Kbu + ft + 1],
                                        in1=MR, op0=ALU.add, op1=ALU.mult).then_inc(s_a, 1)
                dve.wait_ge(s_ah, ft + 1)
                low(ACTT[:, ft % 2, LO, :], MA[:, ft % 2, :], ACTT[:, ft % 2, HI, :]).then_inc(s_al, 1)
                for n in tile_splits(ft):
                    split_lo(n)
                if ft < 10:
                    (top_sides, top_sums, softmax_sum, place_x, place_y)[ft % 5](ft // 5)
                if ft in (6, 11):
                    b = ft // 11
                    dve.wait_ge(s_gh, b + 1)
                    low(GX[:, LO, :, b, :], pJ[:, b, :].rearrange("p (h t) -> p h t", h=RH), GX[:, HI, :, b, :]).then_inc(s_gl, 1)
                if ft == 12:
                    dve.wait_ge(s_ex, 1)
                    ve.tensor_copy(exrow[:, :], pJ[0:1, 0, 0:T2]).then_inc(s_exe, 1)
                if ft == 13:
                    dve.wait_ge(s_ex, 2)
                    ve.tensor_copy(EXT, pJ[:, 1, 0:T2]).then_inc(s_exe, 1)

            def front(e):
                n = EB + 2 * (e // 4)
                cs = slice(512 * (e % 4), 512 * (e % 4) + 512)
                dve.wait_ge(s_dh, e + 1)
                low(slot(n, LO)[:, cs], pS[:, 0, :], slot(n, HI)[:, cs]).then_inc(s_dl, 1)
                dve.wait_ge(s_gexp, e + 1)
                if e >= 1:
                    dve.wait_ge(s_hs, e)
                ve.scalar_tensor_tensor(out=MW, in0=pT[:, :, :].rearrange("p a n -> p (a n)"), scalar=0.0, in1=EW,
                                        op0=ALU.is_gt, op1=ALU.mult).then_inc(s_md, 1)

            front(0)
            for e in range(ETS):
                if e + 1 < ETS:
                    front(e + 1)
                if e % 4 == 0 and e > 0:
                    split_lo(EB + 2 * (e // 4) + 1)
                dve.wait_ge(s_we, e + 1)
                link(ve.tensor_scalar(WE, WE, 1.0, None, ALU.add))
                link(ve.reciprocal(WR_, WE))
                link(ve.tensor_tensor(WR_, pS[:, 1, 0:T2], WR_, ALU.mult))
                dve.wait_ge(s_hs, e + 1)
                if e == ETS - 1:
                    link(ve.tensor_tensor(HS[:, e % 2, :], HS[:, e % 2, :], EXT, ALU.add))
                ve.tensor_tensor(WC[:, e % 2, :], WR_, HS[:, e % 2, :], ALU.mult).then_inc(s_c, 1)
                dve.wait_ge(s_chi, e + 1)
                low(GT[:, e % 2, LO, :], WC[:, e % 2, :], GT[:, e % 2, HI, :]).then_inc(s_cl, 1)
            dve.wait_ge(s_eo, ETS)
            for b in range(B):
                last = ve.tensor_tensor(an[:, b, :], (pV, pX)[b][:, :], an[:, b, :], ALU.add)
            last.then_inc(s_fin, 1)

        @block.tensor
        def _(pe):
            te = nc.tensor

            def product(dst, a, b, start, stop):
                te.matmul(dst, a(HI), b(HI), start=start, stop=False)
                te.matmul(dst, a(HI), b(LO), start=False, stop=False)
                return te.matmul(dst, a(LO), b(HI), start=False, stop=stop)

            pe.wait_ge(d_vec, 96)
            pe.wait_ge(s_ident, 2)
            te.transpose(pX[:, 0:48], vrow[:, :], ident[0:48, 0:48]).then_inc(s_vt, 1)
            pe.wait_ge(s_vec, 1)
            pe.wait_ge(s_latn, 1)
            for k in range(KD):
                if k > 0:
                    pe.wait_ge(s_xev, k)
                for b in range(B):
                    last = te.transpose(pX[:, P * b:P * b + P], SP[:, b, P * k:P * k + P], ident[:, :])
                last.then_inc(s_xtr, 1)
            pe.wait_ge(s_xT, KD)
            pe.wait_ge(s_wql, 2)
            for m in range(H // 2):
                if m >= 2:
                    pe.wait_ge(s_ql, m - 1)
                for b in range(B):
                    for k in range(KD):
                        last = product(pJ[:, m % 2, P * b:P * b + P], lambda s: WQ[:, s, k, P * m:P * m + P],
                                       lambda s: XT[:, b, s, k, 0:P], k == 0, k == KD - 1)
                last.then_inc(s_q, 1)

            def project(it, u, i, w, first):
                c, g = (u // G) % 2, u % G
                q = STEPS * it + HG * u + i
                if not (first and u == 0 and i < 2):
                    pe.wait_ge(s_kvl, q - 1)
                if i < 2:
                    for k in range(KD):
                        last = product(pJ[:, i % 2, 0:w], lambda s: WKV[:, s, k, P * (2 * g + i):P * (2 * g + i + 1)],
                                       lambda s: XT[:, c, s, k, 0:w], k == 0, k == KD - 1)
                elif w == CW:
                    for t in (2 * i - 4, 2 * i - 3):
                        for k in range(KD):
                            last = product(pJ[:, i % 2, 256 * (t % 2):256 * (t % 2) + 256],
                                           lambda s: XT[:, c, s, k, P * t:P * t + P],
                                           lambda s: WKV[:, s, k, INNER + 256 * g:INNER + 256 * g + 256], k == 0, k == KD - 1)
                else:
                    for k in range(KD):
                        last = product(pJ[:, i % 2, 0:P], lambda s: XT[:, c, s, k, 0:P],
                                       lambda s: WKV[:, s, k, INNER + 256 * g + P * (i - 2):INNER + 256 * g + P * (i - 1)],
                                       k == 0, k == KD - 1)
                last.then_inc(s_proj, 1)

            pe.wait_ge(s_ql, H // 2)
            pe.wait_ge(s_wkvl, KD)
            for i in range(HG):
                project(0, 0, i, P, True)

            def round_(it, first, last_round):
                w = P if first else CW
                tiles = w // P

                def transpose_p(t):
                    T = STEPS * it + t
                    pe.wait_ge(s_exp, T + 1)
                    if not (first and t < 2):
                        pe.wait_ge(s_ptl, T - 1)
                    for n in range(tiles):
                        last = te.transpose(pT[:, t % 2, P * n:P * n + P], SP[:, t % 2, P * n:P * n + P], ident[:, :])
                    last.then_inc(s_tr, 1)

                def values(t):
                    u, i = t // HG, t % HG
                    T = STEPS * it + t
                    U = UNITS * it + u
                    pe.wait_ge(s_ptl, T + 1)
                    if i == 0:
                        pe.wait_ge(s_kvl, HG * U + HG)
                        if not (first and u == 0):
                            pe.wait_ge(s_oadd, U)
                    for n in range(tiles):
                        last = product(pV[:, DH * i:DH * i + DH], lambda s: PT[:, t % 2, s, P * n:P * n + P],
                                       lambda s: VT[:, u % 2, s, n, DH * i:DH * i + DH], n == 0, n == tiles - 1)
                    last.then_inc(s_pv, 1)

                for t in range(STEPS):
                    u, i, c = t // HG, t % HG, t // (STEPS // 2)
                    b, g = u // G, u % G
                    T = STEPS * it + t
                    if i % 2 == 0:
                        pe.wait_ge(s_kvl, T + i // 2 - i + 1)
                    if not (first and t < 2):
                        pe.wait_ge(s_ttr, T - 1)
                    product(pS[:, t % 2, 0:w], lambda s: QT[:, s, HG * g + i, L * b:L * b + L],
                            lambda s: KT[:, u % 2, s, i // 2, 0:w], True, True).then_inc(s_qk, 1)
                    if not (last_round and u == UNITS - 1):
                        if i == 0 and u == G - 1 and not first:
                            pe.wait_ge(s_xT, 8 * it + 4)
                        if i == 0 and u == UNITS - 1:
                            pe.wait_ge(s_xT, 8 * it + 8)
                        project(it, u + 1, i, w if u + 1 < UNITS else CW, first)
                    k = t % (STEPS // 2) - 6
                    if 0 <= k < KD and ((c == 0 and not first) or (c == 1 and not last_round)):
                        r = 2 * it - 1 + c
                        if k == 0:
                            pe.wait_ge(s_norm, r + 1)
                        pe.wait_ge(s_xev, 4 + 4 * r + k)
                        for n in range(NT):
                            last = te.transpose(pX[:, P * n:P * n + P], rawc[:, n, P * k:P * k + P], ident[:, :])
                        last.then_inc(s_xtr, 1)
                    if t >= 1:
                        transpose_p(t - 1)
                    if t >= 2:
                        values(t - 2)
                transpose_p(STEPS - 1)
                values(STEPS - 2)
                values(STEPS - 1)

            round_(0, True, False)
            with pe.Fori(1, ROUNDS) as it:
                round_(it, False, False)
            round_(ROUNDS, False, True)

            pe.wait_ge(s_ptl, STEPS * (ROUNDS + 1))
            pe.wait_ge(s_oadd, UNITS * (ROUNDS + 1))
            nb = [0]

            def transpose_rows(src, n_banks, ready):
                pe.wait_ge(s_src, ready)
                for cc in range(n_banks):
                    if nb[0] >= 2:
                        pe.wait_ge(s_tl, nb[0] - 1)
                    for ci in range(2):
                        for b in range(B):
                            col = P * (2 * cc + ci)
                            last = te.transpose(pT[:, nb[0] % 2, P * (2 * ci + b):P * (2 * ci + b) + P],
                                                src[:, b, col:col + P], ident[:, :])
                    last.then_inc(s_tt, 1)
                    nb[0] += 1

            def weight_ready(n):
                pe.wait_ge(s_wlo, n_split(n) + 1)

            def rows(dst, src, n, k0=0, start=True, stop=True):
                for b in range(B):
                    for k in range(4):
                        last = product(dst(b), lambda s: src[:, s, k0 + k, L * b:L * b + L], lambda s: slot4(n, s)[:, k, :],
                                       start and k == 0, stop and k == 3)
                return last.then_inc(s_wuse, 1)

            transpose_rows(O, 4, 1)
            pe.wait_ge(s_tl, 4)
            weight_ready(0)
            rows(lambda b: pS[:, b, :], OT, 0, 0, True, False)
            weight_ready(1)
            rows(lambda b: pS[:, b, :], OT, 1, 4, False, True)
            transpose_rows(hn, 2, 2)
            pe.wait_ge(s_tl, 6)
            for m, dst in enumerate((lambda b: pS[:, b, :], lambda b: pJ[:, b, :], lambda b: (pV, pX)[b][:, :])):
                weight_ready(2 + m)
                rows(dst, HT, 2 + m)
            pe.wait_ge(s_rope, 2)
            transpose_rows(QR, 2, 2)
            pe.wait_ge(s_rope, 4)
            transpose_rows(KR, 2, 2)
            pe.wait_ge(s_tl, 10)

            def scores(n):
                b, c = n // 4, n % 4
                if n >= 2:
                    pe.wait_ge(s_sm, n - 1)
                product(pS[:, n % 2, :], lambda s: QTs[:, s, c, L * b:L * b + L],
                        lambda s: KB[:, s, c, b, :, :], True, True).then_inc(s_sc, 1)

            def probs_values(n):
                b, c = n // 4, n % 4
                pe.wait_ge(s_se, n + 1)
                if n >= 2:
                    pe.wait_ge(s_p2l, n - 1)
                for h in range(4):
                    last = te.transpose(pJ[:, n % 2, P * h:P * h + P], SM[:, n % 2, P * h:P * h + P], ident[:, :])
                last.then_inc(s_pt2, 1)
                pe.wait_ge(s_p2l, n + 1)
                for h in range(4):
                    col = SD * (4 * c + h)
                    last = product((pV, pX)[b][:, col:col + SD], lambda s: PT[:, n % 2, s, P * h:P * h + P],
                                   lambda s: VV[:, s, b, col:col + SD], True, True)
                last.then_inc(s_pv2, 1)

            pe.wait_ge(s_vl, 2)
            scores(0)
            for n in range(8):
                if n + 1 < 8:
                    scores(n + 1)
                probs_values(n)
            transpose_rows(an, 2, 3)
            pe.wait_ge(s_tl, 12)
            pe.wait_ge(s_sm, 8)
            weight_ready(5)
            rows(lambda b: pS[:, b, :], AT, 5)
            transpose_rows(hn, 2, 4)

            pe.wait_ge(d_key, 32)
            for m in range(4):
                last = te.transpose(pV[:, NK * m:NK * m + NK], xst[0:NK, P * m:P * m + P], ident[0:NK, 0:NK])
            last.then_inc(s_kt, 1)
            pe.wait_ge(s_tl, 14)
            pe.wait_ge(s_yread, 2)
            weight_ready(6)
            for m in range(4):
                for k in range(4):
                    last = product(pS[:, m // 2, T2 * (m % 2):T2 * (m % 2) + T2],
                                   lambda s: slot4(6, s)[:, k, P * m:P * m + P], lambda s: HT[:, s, k, :], k == 0, k == 3)
                if m % 2:
                    last.then_inc(s_q2, 1)
            pe.wait_ge(s_kl, 1)
            pe.wait_ge(s_q2l, 2)
            for b in range(B):
                for m in range(4):
                    last = product(pJ[:, b, P * m:P * m + P], lambda s: QT2[:, s, m, L * b:L * b + L],
                                   lambda s: KBk[:, s, m, :], True, True)
                last.then_inc(s_sim, 1)

            def gate_up(ft):
                q, j = ft // 4, ft % 4
                if ft >= 2:
                    pe.wait_ge(s_a, ft - 1)
                for i in range(2):
                    n = FB + 3 * q + i
                    if j == 0:
                        weight_ready(n)
                    for k in range(4):
                        last = product(pS[:, ft % 2, T2 * i:T2 * i + T2], lambda s: slot4(n, s)[:, k, P * j:P * j + P],
                                       lambda s: HT[:, s, k, :], k == 0, k == 3)
                    if i == 1:
                        last.then_inc(s_gu, 1)

            def add_tile(coef, n, j, start, stop, done):
                for b in range(B):
                    last = product((pV, pX)[b][:, :], lambda s: coef[:, s, L * b:L * b + L], lambda s: slot4(n, s)[:, j, :],
                                   start, stop)
                last.then_inc(done, 1)

            gate_up(0)
            for ft in range(16):
                if ft < 15:
                    gate_up(ft + 1)
                n = FB + 3 * (ft // 4) + 2
                if ft % 4 == 0:
                    weight_ready(n)
                pe.wait_ge(s_al, ft + 1)
                add_tile(ACTT[:, ft % 2], n, ft % 4, ft == 0, False, s_mo)
                if ft in (5, 10):
                    b = ft // 10
                    pe.wait_ge(s_gn, b + 1)
                    for h in range(RH):
                        te.transpose(pJ[:, b, P * h:P * h + P], GN[:, h, :], ident[:, :])
                        last = te.transpose(pT[:, b, P * h:P * h + P], RN[:, h, :], ident[:, :])
                    last.then_inc(s_gt, 1)
                if ft == 11:
                    pe.wait_ge(s_gl, 2)
                    pe.wait_ge(s_simc, 2)
                    for b in range(B):
                        last = te.transpose(pJ[0:1, 0, P * b:P * b + P], EXB[:, b:b + 1], ident[:, :])
                    last.then_inc(s_ex, 1)
                if ft == 12:
                    pe.wait_ge(s_exe, 1)
                    te.matmul(pJ[:, 1, 0:T2], delta[:, :], exrow[:, :], start=True, stop=True).then_inc(s_ex, 1)

            def front(e):
                q, j = e // 4, e % 4
                n = EB + 2 * q
                if j == 0:
                    wait_staged(pe, n)
                if e >= 1:
                    pe.wait_ge(s_dl, e)
                for k in range(4):
                    last = te.transpose(pS[:, 0, P * k:P * k + P], staged(n)[:, 512 * j + P * k:512 * j + P * k + P], ident[:, :])
                last.then_inc(s_dt, 1)
                if e >= 1:
                    pe.wait_ge(s_gexp, e)
                    pe.wait_ge(s_md, e)
                for i in range(2):
                    te.matmul(pJ[:, i, :], SEL[:, e, :], GX[:, HI, 2 * i:2 * i + 2, :, :], start=True, stop=False)
                    te.matmul(pJ[:, i, :], SEL[:, e, :], GX[:, LO, 2 * i:2 * i + 2, :, :], start=False, stop=True)
                    last = te.matmul(pT[:, i, :], SEL[:, e, :], RT[:, 2 * i:2 * i + 2, :, :], start=True, stop=True)
                last.then_inc(s_gd, 1)

            def reach(e):
                q, j = e // 4, e % 4
                n = EB + 2 * q
                pe.wait_ge(s_dl, e + 1)
                if e >= 1:
                    pe.wait_ge(s_c, e)
                for k in range(4):
                    cs = slice(512 * j + P * k, 512 * j + P * k + P)
                    last = product(pS[:, 1, 0:T2], lambda s: slot(n, s)[:, cs], lambda s: HT[:, s, k, :], k == 0, k == 3)
                last.then_inc(s_w, 1)

            def spread(e):
                n = EB + 2 * (e // 4) + 1
                if e % 4 == 0:
                    weight_ready(n)
                pe.wait_ge(s_cl, e + 1)
                add_tile(GT[:, e % 2], n, e % 4, False, e == ETS - 1, s_eo)

            pe.wait_ge(s_a, 16)
            pe.wait_ge(s_exe, 2)
            pe.wait_ge(s_selr, 1)
            front(0)
            for e in range(ETS):
                if e + 1 < ETS:
                    front(e + 1)
                reach(e)
                if e >= 1:
                    spread(e - 1)
            spread(ETS - 1)


_INS = ["x", "ctx_1024", "mask_BxS2_bk0", "L0_xattn_g1", "L0_xattn_b1", "L0_xattn_g2", "L0_xattn_b2", "L0_xattn_Wq",
        "L0_xattn_Wkv", "L0_xattn_Wout", "L0_attn_qw", "L0_attn_kw", "L0_attn_vw", "L0_attn_ow", "L0_ffn_Wg", "L0_ffn_bg",
        "L0_ffn_Wu", "L0_ffn_bu", "L0_ffn_Wd", "L0_ffn_bd", "L0_ffn_Wq", "L0_ffn_keys", "L0_ffn_down_embed", "L0_ffn_up_embed"]


def constants(seq, head):
    inv = (1.0 / 10000.0 ** (np.arange(0, head, 2, dtype=np.float32) / head)).astype(np.float32)
    freq = np.arange(seq, dtype=np.float32)[:, None] * inv[None, :]
    causal = np.where(np.arange(seq)[:, None] >= np.arange(seq)[None, :], 0.0, -1e30).astype(np.float32)
    select = np.zeros((128, 16, 128), np.float32)
    e = np.arange(128)
    for t in range(16):
        select[2 * t + e // 64, t, e] = 1.0
        select[64 + e % 64, t, e] = 1.0
    return {"rope_cos": np.cos(freq), "rope_sin": np.sin(freq), "causal": causal, "select": select.reshape(128, 2048)}


def kernel(**inputs):
    import concourse.bacc as bacc
    from concourse.bass_utils import run_bass_kernel_spmd

    nc = bacc.Bacc("TRN2", target_bir_lowering=False, num_devices=1)
    arrays, args = {}, []
    seq = inputs["x"].shape[1]
    given = {n: np.ascontiguousarray(inputs[n]) for n in _INS}
    given.update(constants(seq, 32))
    for name, a in given.items():
        arrays[f"in_{name}"] = a
        args.append(nc.dram_tensor(f"in_{name}", a.shape, mybir.dt.from_np(a.dtype), kind="ExternalInput").ap())
    args.append(nc.dram_tensor("out_0", inputs["x"].shape, F32, kind="ExternalOutput").ap())
    perceiver_layer(nc, *args)
    r = run_bass_kernel_spmd(nc, [arrays], core_ids=[0])
    return r.results[0]["out_0"]
```

```python
from contextlib import ExitStack

import numpy as np
import concourse.bass as bass
from concourse import mybir

F32 = mybir.dt.float32
F32R = mybir.dt.float32r
U8 = mybir.dt.uint8
U32 = mybir.dt.uint32
ALU = mybir.AluOpType
ACT = mybir.ActivationFunctionType
AX = mybir.AxisListType

P = 128
EPS = 1e-5
HI, LO = 0, 1


def perceiver_layer(nc, x, ctx1024, mask, g1, b1, g2, b2, Wq, Wkv, Wout, qw, kw, vw, ow,
                    Wg, bg, Wu, bu, Wd, bd, fWq, keys, down, up, rope_cos, rope_sin, causal, select, out):
    B, L, D = x.shape
    N = ctx1024.shape[1]
    KD = D // P
    INNER = Wq.shape[1]
    DH = 64
    H = INNER // DH
    CW = 512
    NT = CW // P
    ROUNDS = N // CW
    HG = 4
    G = H // HG
    STEPS = B * H
    UNITS = B * G
    XSC = DH ** -0.5
    SH, SD = 16, D // 16
    SSC = SD ** -0.5
    BIG = 1e30
    T2 = B * L
    F = Wg.shape[1]
    NEXP = down.shape[0]
    NK = 64
    RH = 4
    ETS = NEXP // P
    assert (B, L, D, N, F, NEXP) == (2, 128, 512, 2048, 2048, 2048)

    with ExitStack() as stack:
        def sb(name, shape, dt=F32):
            return stack.enter_context(nc.sbuf_tensor(name, shape, dt))

        def sem(name):
            return stack.enter_context(nc.semaphore(name))

        W = sb("W", [P, 16384], F32R)
        with nc.sbuf_tensor("QA", [P, 8192], F32R) as QA:
            pass
        with nc.sbuf_tensor("OTA", [P, 4096], F32R) as OTA:
            pass
        tail = sb("tail", [P, 4096])
        late = sb("late", [P, 4096])
        XA = sb("XA", [P, 8192], F32R)
        KV = sb("KV", [P, 8192], F32R)
        raw = sb("raw", [P, 2048])
        work = sb("work", [P, 2048])
        xst = sb("xst", [P, CW])
        PT = sb("PT", [P, 2, 2, CW], F32R)
        O = sb("O", [P, B, INNER])
        xres = sb("xres", [P, B, D])
        ident = sb("ident", [P, P])
        vrow = sb("vrow", [48, P])
        vec = sb("vec", [P, 48])
        mraw = sb("mraw", [P, CW], U8)
        st = sb("st", [P, 4, 6])
        mv = sb("mv", [P, 4, 2])
        rstd = sb("rstd", [P, 4])
        half = sb("half", [P, 4])
        mold = sb("mold", [P, B, H])
        mcur = sb("mcur", [P, 2, HG])
        negm = sb("negm", [P, 2, HG])
        dm = sb("dm", [P, 2, HG])
        alpha = sb("alpha", [P, 2, HG])
        rs = sb("rs", [P, 2, HG])
        lsum = sb("lsum", [P, B, H])
        small = sb("small", [P, 64])

        pS = stack.enter_context(nc.psum_tensor("pS", [P, 2, 512], F32))
        pJ = stack.enter_context(nc.psum_tensor("pJ", [P, 2, 512], F32))
        pT = stack.enter_context(nc.psum_tensor("pT", [P, 2, 512], F32))
        pV = stack.enter_context(nc.psum_tensor("pV", [P, 512], F32))
        pX = stack.enter_context(nc.psum_tensor("pX", [P, 512], F32))

        WKV = W[:, :].rearrange("p (s k n) -> p s k n", s=2, k=KD)
        WQ = KV[:, :].rearrange("p (s k n) -> p s k n", s=2, k=KD)
        QT = QA[:, :].rearrange("p (s h t) -> p s h t", s=2, h=H)
        XT = XA[:, :].rearrange("p (c s k n) -> p c s k n", c=2, s=2, k=KD)
        KT = KV[:, 0:4096].rearrange("p (c s j n) -> p c s j n", c=2, s=2, j=2)
        VT = KV[:, 4096:8192].rearrange("p (c s t n) -> p c s t n", c=2, s=2, t=NT)
        SP = work[:, 0:1024].rearrange("p (c n) -> p c n", c=2)
        MB = work[:, 1024:2048].rearrange("p (c n) -> p c n", c=2)
        pVh = pV[:, :].rearrange("p (h s e) -> p h s e", h=HG, s=2)
        rawc = raw[:, :].rearrange("p (t d) -> p t d", t=NT)
        Of = O[:, :, :].rearrange("p b n -> p (b n)")
        Kg1, Kb1, Kg2, Kb2, Kbg, Kbu = 0, 4, 8, 12, 16, 32

        d_x = sem("d_x"); d_vec = sem("d_vec"); d_wq = sem("d_wq"); d_wkv = [sem("d_wkvA"), sem("d_wkvB")]
        d_raw = sem("d_raw"); d_mask = sem("d_mask")
        s_ident = sem("s_ident"); s_zero = sem("s_zero"); s_vt = sem("s_vt"); s_vec = sem("s_vec")
        s_wqh = sem("s_wqh"); s_wql = sem("s_wql"); s_wkvh = sem("s_wkvh"); s_wkvl = sem("s_wkvl")
        s_q = sem("s_q"); s_qh = sem("s_qh"); s_ql = sem("s_ql")
        s_stat = sem("s_stat"); s_rst = sem("s_rst"); s_lat = sem("s_lat"); s_latn = sem("s_latn"); s_bn = sem("s_bn"); s_ch = sem("s_chain")
        s_norm = sem("s_norm"); s_xtr = sem("s_xtr"); s_xh = sem("s_xh"); s_xT = sem("s_xT")
        s_mb = sem("s_mb")
        s_qk = sem("s_qk"); s_ttr = sem("s_ttr"); s_negm = sem("s_negm"); s_exp = sem("s_exp")
        s_proj = sem("s_proj"); s_kvh = sem("s_kvh"); s_kvl = sem("s_kvl")
        s_tr = sem("s_tr"); s_pth = sem("s_pth"); s_ptl = sem("s_ptl"); s_pv = sem("s_pv")
        s_dmt = sem("s_dmt"); s_dm = sem("s_dm"); s_alpha = sem("s_alpha"); s_lt = sem("s_lt"); s_osc = sem("s_osc"); s_ohalf = sem("s_ohalf"); s_oadd = sem("s_oadd")

        d_w = [sem(f"d_w{i}") for i in range(4)]; d_key = sem("d_key"); d_rope = sem("d_rope"); d_sel = sem("d_sel"); d_out = sem("d_out"); d_bd = sem("d_bd")
        s_whi = sem("s_whi"); s_wlo = sem("s_wlo"); s_wuse = sem("s_wuse")
        s_src = sem("s_src")
        s_tt = sem("s_tt"); s_th = sem("s_th"); s_tl = sem("s_tl")
        s_dve = sem("s_dve"); s_ln = sem("s_ln"); s_pn = sem("s_pn")
        s_yread = sem("s_yread")
        s_vh = sem("s_vh"); s_vl = sem("s_vl"); s_rope = sem("s_rope"); s_kz = sem("s_kz")
        s_sc = sem("s_sc"); s_sm = sem("s_sm"); s_se = sem("s_se"); s_pt2 = sem("s_pt2"); s_p2h = sem("s_p2h"); s_p2l = sem("s_p2l"); s_pv2 = sem("s_pv2")
        s_kt = sem("s_kt"); s_kh = sem("s_kh"); s_kl = sem("s_kl"); s_q2 = sem("s_q2"); s_q2h = sem("s_q2h"); s_q2l = sem("s_q2l"); s_sim = sem("s_sim")
        s_gu = sem("s_gu"); s_ge = sem("s_ge"); s_gur = sem("s_gur"); s_a = sem("s_a"); s_ah = sem("s_ah"); s_al = sem("s_al"); s_mo = sem("s_mo")
        s_dve2 = sem("s_dve2"); s_tk = sem("s_tk"); s_tke = sem("s_tke"); s_gn = sem("s_gn"); s_pl = sem("s_pl"); s_simc = sem("s_simc"); s_gt = sem("s_gt"); s_gh = sem("s_gh"); s_gl = sem("s_gl")
        s_selr = sem("s_selr"); s_iota = sem("s_iota")
        s_gd = sem("s_gd"); s_gexp = sem("s_gexp"); s_md = sem("s_md"); s_hs = sem("s_hs"); s_hs1 = sem("s_hs1"); s_dt = sem("s_dt"); s_dh = sem("s_dh"); s_dl = sem("s_dl")
        s_w = sem("s_w"); s_we = sem("s_we"); s_wr = sem("s_wr"); s_c = sem("s_c"); s_chi = sem("s_chi"); s_cl = sem("s_cl"); s_eo = sem("s_eo")
        s_ex = sem("s_ex"); s_exe = sem("s_exe"); s_fin = sem("s_fin")

        w4 = lambda w: w.rearrange("(k p) n -> p k n", p=P)
        blocks = [w4(Wout)[:, 0:4, :], w4(Wout)[:, 4:8, :], w4(qw), w4(kw), w4(vw), w4(ow), w4(fWq)]
        for f in range(4):
            blocks += [w4(Wg)[:, :, 512 * f:512 * f + 512], w4(Wu)[:, :, 512 * f:512 * f + 512],
                       w4(Wd)[:, 4 * f:4 * f + 4, :]]
        for f in range(4):
            blocks += [w4(down)[:, 4 * f:4 * f + 4, :], w4(up)[:, 4 * f:4 * f + 4, :]]
        NB = len(blocks)
        FB = 7
        EB = FB + 12
        is_down = lambda n: n >= EB and (n - EB) % 2 == 0
        n_split = lambda n: sum(not is_down(m) for m in range(n))
        stage_of = lambda n: 0 if n < 2 else n if n < 4 else 1 - n % 2
        users = lambda n: [m for m in range(n) if stage_of(m) == stage_of(n)]
        staged = lambda n: (raw[:, :], work[:, :], late[:, 0:2048], late[:, 2048:4096])[stage_of(n)]
        slot_of = lambda n: 5 if n == 0 else (n - 1) % 4 if n < FB else (2, 3, 0, 4, 1)[(n - FB) % 5]
        slot = lambda n, part: (XA[:, 4096:8192] if slot_of(n) == 4 else XA[:, 0:4096] if slot_of(n) == 5 else W[:, 4096 * slot_of(n):4096 * slot_of(n) + 4096])[
            :, 2048 * part:2048 * part + 2048]

        def wait_used(eng, n):
            kind, q = ((n - FB) % 3, (n - FB) // 3) if n < EB else ((n - EB) % 2, (n - EB) // 2)
            if n < 6:
                eng.wait_ge(s_wuse, n + 1)
            elif n == 6:
                eng.wait_ge(s_q2, 2)
            elif n < EB:
                eng.wait_ge(s_mo if kind == 2 else s_gu, 4 * q + 4)
            else:
                eng.wait_ge(s_eo if kind == 1 else s_w, 4 * q + 4)

        def slot_free(eng, n):
            before = [m for m in range(n) if slot_of(m) == slot_of(n)]
            if before or slot_of(n) == 4:
                wait_used(eng, before[-1] if before else 5)
            elif n > 0:
                eng.wait_ge(s_proj, LAT + STEPS * ROUNDS)
            else:
                eng.wait_ge(s_proj, LAT + STEPS * ROUNDS - STEPS // 2)

        slot4 = lambda n, part: slot(n, part).rearrange("p (k n) -> p k n", k=4)

        def wait_staged(eng, n):
            eng.wait_ge(d_w[stage_of(n)], 16 * (len(users(n)) + 1))

        OT = OTA[:, :].rearrange("p (s c t) -> p s c t", s=2, c=8)
        HT = XA[:, 0:2048].rearrange("p (s c t) -> p s c t", s=2, c=4)
        QTs = XA[:, 2048:4096].rearrange("p (s c t) -> p s c t", s=2, c=4)
        AT = XA[:, 4096:6144].rearrange("p (s c t) -> p s c t", s=2, c=4)
        VV = XA[:, 6144:8192].rearrange("p (s b n) -> p s b n", s=2, b=B)
        KB = KV[:, :].rearrange("p (s c b h t) -> p s c b h t", s=2, c=4, b=B, h=4)
        rope = sb("rope", [P, 2, 16])
        cmask = sb("cmask", [P, P])
        QR = late[:, 0:1024].rearrange("p (b n) -> p b n", b=B)
        KR = late[:, 1024:2048].rearrange("p (b n) -> p b n", b=B)
        RTMP = late[:, 2048:3072].rearrange("p (i h e) -> p i h e", i=4, h=SH)
        SM = late[:, 3072:4096].rearrange("p (c n) -> p c n", c=2)
        hn = Of[:, 0:1024].rearrange("p (b n) -> p b n", b=B)
        an = Of[:, 1024:2048].rearrange("p (b n) -> p b n", b=B)

        def passed(eng):
            eng.sem_inc(s_passed, 1)

        s_passed = sem("s_passed")

        QT2 = XA[:, 2048:4096].rearrange("p (s m t) -> p s m t", s=2, m=4)
        KBk = KV[:, 0:1024].rearrange("p (s m n) -> p s m n", s=2, m=4)
        SEL = KV[:, 1024:3072].rearrange("p (e n) -> p e n", e=ETS)
        GT = KV[:, 3072:4096].rearrange("p (c s n) -> p c s n", c=2, s=2)
        ACTT = KV[:, 4096:5120].rearrange("p (c s n) -> p c s n", c=2, s=2)
        RT = KV[:, 5120:6144].rearrange("p (h b t) -> p h b t", h=RH, b=B)
        GX = KV[:, 6144:8192].rearrange("p (s h b t) -> p s h b t", s=2, h=RH, b=B)
        SIM = late[:, 0:1024].rearrange("p (b n) -> p b n", b=B)
        SC = late[:, 1024:1280]
        REP = late[:, 1280:1536]
        CM = late[:, 1536:1792]
        EXC = late[:, 1792:2048]
        EQ = late[:, 2048:4096]
        EW, MW = late[:, 2048:3072], late[:, 3072:4096]
        GN = tail[:, 0:512].rearrange("p (h n) -> p h n", h=RH)
        RN = tail[:, 512:1024].rearrange("p (h n) -> p h n", h=RH)
        ME = tail[:, 1024:1536].rearrange("p (c n) -> p c n", c=2)
        MA = tail[:, 1536:2048].rearrange("p (c n) -> p c n", c=2)
        HS = tail[:, 2048:2560].rearrange("p (c n) -> p c n", c=2)
        WE, WR_ = tail[:, 2560:2816], tail[:, 2816:3072]
        WC = tail[:, 3072:3584].rearrange("p (c n) -> p c n", c=2)
        V8, IXF, VALS, EV, N8 = (tail[:, a:b] for a, b in ((3584, 3648), (3648, 3712), (3712, 3744), (3744, 3776), (3776, 3808)))
        ZS, OFF, EXB = tail[:, 3808:3812], tail[:, 3812:3816], tail[:, 3816:3818]
        IOTA, W8, GE = tail[:, 3818:3882], tail[:, 3882:3890], tail[:, 3890:3922]
        IX = sb("IX", [P, 64], U32)
        delta = sb("delta", [1, P])
        exrow = sb("exrow", [1, T2])
        EXT = xst[:, 256:512]

        def tile_splits(ft):
            q, j = ft // 4, ft % 4
            if q < 3:
                return [FB + 3 * (q + 1) + {0: 0, 1: 1, 3: 2}[j]] if j != 2 else []
            return [EB + 1] if j == 1 else []

        def unit_of(u, first):
            return (u % B, u // B, u // B % 2) if first else (u // G, u % G, u % 2)

        LAT = G * HG

        def part_at(it, t, first, last):
            u, i = t // HG, t % HG
            if first and u < UNITS - 2:
                g, slot_ = u // B + 1, 2 * (u % B) + i // 2
                return (HG * g + slot_, slot_, g % 2, g, 1, True, HG * B * (g - 1)) if i % 2 else None
            if (first and u == UNITS - 2) or (last and u == UNITS - 1):
                return None
            U = UNITS * it + u
            return (HG * (U + 1) + i - (STEPS - LAT), i, (u + 1) % 2, (u + 1) % G, (u + 1) // G % 2, False, HG * U)

        block = stack.enter_context(nc.Block())
        x_v = x.rearrange("b p d -> p b d")
        ctx_v = ctx1024.rearrange("b (j n p) d -> b j p n d", n=NT, p=P)
        mask_v = mask.rearrange("b (j n) -> b j n", n=CW)

        def kv_copy(i, par, lat, s, op):
            src = pJ[:, i % 2, 0:T2 if lat else CW]
            if i < 2:
                return op(KT[:, par, s, i, 0:T2 if lat else CW], src)
            if lat:
                return op(VT[:, par, s, i - 2, :], src)
            return op(VT[:, par, s, 2 * i - 4:2 * i - 2, :], src.rearrange("p (t n) -> p t n", t=2))

        @block.sync
        def _(sp):
            sp.dma_start(xres[:, :, :], x_v).then_inc(d_x, 16)
            for v, (w, at) in enumerate(((g1, 0), (b1, 4), (g2, 8), (b2, 12), (bg, 16), (bu, 32))):
                n = w.shape[0] // P
                sp.dma_start(vrow[at:at + n, :], w.rearrange("(a p) -> a p", p=P)).then_inc(d_vec, 16)
            sp.dma_start(raw[:, :].rearrange("p (k n) -> p k n", k=2), w4(Wq)[:, 0:2, :]).then_inc(d_wq, 16)
            sp.dma_start(O[:, :, :], w4(Wq)[:, 2:4, :]).then_inc(d_wq, 16)
            for k in range(KD):
                if k < 2:
                    sp.wait_ge(s_wql, k + 1)
                else:
                    sp.wait_ge(s_wkvl, k - 1)
                sp.dma_start((raw[:, :], Of)[k % 2], w4(Wkv)[:, k, :]).then_inc(d_wkv[k % 2], 16)

            def load_chunk(b, j):
                sp.dma_start(rawc, ctx_v[b, j]).then_inc(d_raw, 16)
                sp.dma_start(mraw[:, :], mask_v[b, j].partition_broadcast(P)).then_inc(d_mask, 16)

            sp.wait_ge(s_wkvl, 3)
            load_chunk(0, 0)

            def round_(it, last):
                if not (type(it) is int and it == 0) and not last:
                    r = 2 * it - 1
                    sp.wait_ge(s_xtr, 4 * r + 8)
                    passed(sp)
                    sp.wait_ge(s_mb, r + 1)
                    passed(sp)
                    load_chunk(0, it)
                if not last:
                    r = 2 * it
                    sp.wait_ge(s_xtr, 4 * r + 8)
                    passed(sp)
                    sp.wait_ge(s_mb, r + 1)
                    passed(sp)
                    load_chunk(1, it)

            round_(0, False)
            with sp.Fori(1, ROUNDS) as it:
                round_(it, False)

            sp.dma_start(rope[:, 0, :], rope_cos).then_inc(d_rope, 16)
            sp.dma_start(rope[:, 1, :], rope_sin).then_inc(d_rope, 16)
            sp.dma_start(cmask[:, :], causal).then_inc(d_rope, 16)
            order = list(range(EB + 2)) + [n + d for n in range(EB + 2, NB, 2) for d in (1, 0)]
            for n in order:
                if n == FB + 2:
                    sp.wait_ge(s_pv2, 8)
                    sp.dma_start(EQ, select).then_inc(d_sel, 16)
                    for side in range(2):
                        sp.dma_start(xst[0:NK, 256 * side:256 * side + 256].rearrange("k (h n) -> k h n", h=RH),
                                     keys.rearrange("h k p n -> p k h n")[side]).then_inc(d_key, 16)
                if n == FB + 4:
                    sp.wait_ge(s_tt, 14)
                    sp.dma_start(hn[:, 0, :], bd.partition_broadcast(P)).then_inc(d_bd, 16)
                if n == 0:
                    sp.wait_ge(s_xtr, 4 * 2 * ROUNDS + 4)
                if n == 2:
                    sp.wait_ge(s_qk, STEPS * (ROUNDS + 1))
                if n == 4:
                    sp.wait_ge(s_tr, STEPS * (ROUNDS + 1))
                if users(n):
                    m = users(n)[-1]
                    if is_down(m):
                        sp.wait_ge(s_dt, 4 * ((m - EB) // 2 + 1))
                    else:
                        sp.wait_ge(s_wlo, n_split(m) + 1)
                sp.dma_start(staged(n).rearrange("p (k n) -> p k n", k=4), blocks[n]).then_inc(d_w[stage_of(n)], 16)
            sp.wait_ge(s_fin, 1)
            sp.dma_start(out.rearrange("b p d -> p b d"), an).then_inc(d_out, 16)
            sp.wait_ge(d_out, 16)

        @block.gpsimd
        def _(pool):
            gp = nc.gpsimd
            gp.memset(ident[:, :], 0.0).then_inc(s_ident, 1)
            gp.memset(half[:, :], -0.5).then_inc(s_zero, 1)
            gp.memset(QA[:, :].bitcast(U32), 0).then_inc(s_zero, 1)
            gp.memset(work[:, :], 0.0).then_inc(s_zero, 1)
            pool.wait_ge(s_ident, 1)
            gp.affine_select(out=ident[:, :], in_=ident[:, :], compare_op=ALU.not_equal, fill=1.0,
                             base=0, pattern=[[-1, P]], channel_multiplier=1).then_inc(s_ident, 1)

            def rsqrt(n, ready, count, done):
                pool.wait_ge(ready, count)
                gp.tensor_scalar(rstd[:, 0:n], mv[:, 0:n, 1], EPS, None, ALU.add).then_inc(s_rst, 1)
                rs_count[0] += 1
                pool.wait_ge(s_rst, rs_count[0])
                gp.tensor_tensor(rstd[:, 0:n], rstd[:, 0:n], half[:, 0:n], ALU.pow).then_inc(done, 1)

            def split_lo(n):
                pool.wait_ge(s_whi, n_split(n) + 1)
                gp.tensor_tensor(slot(n, LO), staged(n), slot(n, HI).bitcast(F32), ALU.subtract).then_inc(s_wlo, 1)

            rs_count = [0]
            pool.wait_ge(s_zero, 3)
            rsqrt(2, s_stat, 1, s_lat)
            rsqrt(2, s_stat, 2, s_lat)

            def block_lo(e, k, c, n):
                pool.wait_ge(s_xh, e + 1)
                gp.tensor_tensor(XT[:, c, LO, k, 0:n], xst[:, 0:n], XT[:, c, HI, k, 0:n].bitcast(F32), ALU.subtract).then_inc(s_xT, 1)

            for k in range(KD):
                block_lo(k, k, 1, T2)

            def chunk_rstd(r):
                pool.wait_ge(s_stat, r + 3)
                passed(pool)
                gp.tensor_scalar(rstd[:, :], mv[:, :, 1], EPS, None, ALU.add).then_inc(s_rst, 1)
                pool.wait_ge(s_rst, r + 3)
                gp.tensor_tensor(rstd[:, :], rstd[:, :], half[:, :], ALU.pow).then_inc(s_lat, 1)

            def unit(it, u, first):
                b, g, _ = unit_of(u, first)
                par = u % 2
                U = UNITS * it + u
                hs = slice(HG * g, HG * g + HG)
                pool.wait_ge(s_negm, HG * U + HG)
                if not first:
                    gp.tensor_tensor(dm[:, par, :], mold[:, b, hs], mcur[:, par, :], ALU.subtract).then_inc(s_dmt, 1)
                    pool.wait_ge(s_dmt, U - UNITS + 1)
                passed(pool)
                gp.tensor_copy(mold[:, b, hs], mcur[:, par, :]).then_inc(s_dm, 1)
                pool.wait_ge(s_exp, HG * U + HG)
                if first:
                    gp.tensor_copy(lsum[:, b, hs], rs[:, par, :]).then_inc(s_osc, 1)
                else:
                    pool.wait_ge(s_alpha, U - UNITS + 1)
                    gp.tensor_tensor(lsum[:, b, hs], lsum[:, b, hs], alpha[:, par, :], ALU.mult).then_inc(s_lt, 1)
                    ov = O[:, b, 256 * g:256 * g + 256].rearrange("p (h e) -> p h e", h=HG)
                    gp.tensor_tensor(ov, ov, alpha[:, par, :].unsqueeze(2).broadcast_to([P, HG, DH]), ALU.mult)
                    pool.wait_ge(s_lt, U - UNITS + 1)
                    gp.tensor_tensor(lsum[:, b, hs], lsum[:, b, hs], rs[:, par, :], ALU.add).then_inc(s_osc, 1)

            def round_(it, first, last):
                for u in range(UNITS):
                    c = u // G
                    prep = (c == 0 and not first) or (c == 1 and not last)
                    r = 2 * it - 1 + c
                    if prep and u % G in (1, 2):
                        for k in (2 * (u % G) - 2, 2 * (u % G) - 1):
                            block_lo(4 + 4 * r + k, k, 1 - c, CW)
                    if prep and u % G == 0:
                        chunk_rstd(r)
                    unit(it, u, first)
                    if last and u == G:
                        split_lo(0)

            round_(0, True, False)
            with pool.Fori(1, ROUNDS) as it:
                round_(it, False, False)
            round_(ROUNDS, False, True)

            def row_rstd(i):
                pool.wait_ge(s_ln, i + 1)
                gp.tensor_scalar(rstd[:, 0:2], mv[:, 0:2, 1], EPS, None, ALU.add).then_inc(s_rst, 1)
                pool.wait_ge(s_rst, 2 + 2 * ROUNDS + i + 1)
                gp.tensor_tensor(rstd[:, 0:2], rstd[:, 0:2], half[:, 0:2], ALU.pow).then_inc(s_pn, 1)

            for n in range(1, 4):
                split_lo(n)
            row_rstd(0)
            for n in range(4, FB + 2):
                split_lo(n)
            row_rstd(1)
            pool.wait_ge(s_pv2, 8)
            gp.memset(KV[:, 0:1024].bitcast(U32), 0).then_inc(s_kz, 1)
            gp.iota(IOTA, [[1, NK]], base=0, channel_multiplier=0, allow_small_or_imprecise_dtypes=True)
            gp.iota(W8, [[-1, 8]], base=8, channel_multiplier=0, allow_small_or_imprecise_dtypes=True)
            gp.memset(delta[:, :], 0.0).then_inc(s_iota, 1)
            pool.wait_ge(s_iota, 1)
            gp.memset(delta[:, P - 1:P], 1.0).then_inc(s_iota, 1)
            split_lo(FB + 2)
            for ft in range(16):
                for n in tile_splits(ft):
                    split_lo(n)
            for e in range(ETS):
                if e % 4 == 2 and e < ETS - 4:
                    split_lo(EB + 2 * (e // 4) + 3)
                pool.wait_ge(s_md, e + 1)
                gp.tensor_tensor(MW[:, 0:512], MW[:, 0:512], MW[:, 512:1024], ALU.add).then_inc(s_hs1, 1)
                pool.wait_ge(s_hs1, e + 1)
                if e >= 2:
                    pool.wait_ge(s_c, e - 1)
                gp.tensor_tensor(HS[:, e % 2, :], MW[:, 0:256], MW[:, 256:512], ALU.add).then_inc(s_hs, 1)


        @block.scalar
        def _(act):
            ac = nc.scalar
            act.wait_ge(s_vt, 1)
            ac.activation(vec[:, :], pX[:, 0:48], ACT.Copy).then_inc(s_vec, 1)
            act.wait_ge(d_wq, 32)
            ac.activation(WQ[:, HI, 0:2, :], raw[:, :].rearrange("p (k n) -> p k n", k=2), ACT.Copy).then_inc(s_wqh, 1)
            ac.activation(WQ[:, HI, 2:4, :], O[:, :, :], ACT.Copy).then_inc(s_wqh, 1)

            def wkv_hi(k):
                act.wait_ge(d_wkv[k % 2], 16 * (k // 2 + 1))
                ac.activation(WKV[:, HI, k, :], (raw[:, :], Of)[k % 2], ACT.Copy).then_inc(s_wkvh, 1)

            def x_evac(e, k, c, n, kg, kb):
                act.wait_ge(s_xtr, e + 1)
                if not (type(e) is int and e == 0):
                    act.wait_ge(s_xT, e)
                for dst in (xst[:, 0:n], XT[:, c, HI, k, 0:n]):
                    last = ac.activation(dst, pX[:, 0:n], ACT.Identity, bias=vec[:, kb:kb + 1], scale=vec[:, kg:kg + 1])
                last.then_inc(s_xh, 1)

            def split_hi(n, quarter=None):
                if not quarter:
                    wait_staged(act, n)
                    slot_free(act, n)
                cs = slice(0, 2048) if quarter is None else slice(512 * quarter, 512 * quarter + 512)
                ins = ac.activation(slot(n, HI)[:, cs], staged(n)[:, cs], ACT.Copy)
                if quarter in (None, 3):
                    ins.then_inc(s_whi, 1)

            for k in range(KD):
                x_evac(k, k, 1, T2, Kg2 + k, Kb2 + k)
            for k in range(2):
                wkv_hi(k)
            for m in range(H // 2):
                act.wait_ge(s_q, m + 1)
                if m == 0:
                    act.wait_ge(s_zero, 3)
                ac.activation(QT[0:DH, HI, 2 * m, :], pJ[0:DH, m % 2, 0:T2], ACT.Copy)
                ac.activation(QT[DH:P, HI, 2 * m + 1, :], pJ[DH:P, m % 2, 0:T2], ACT.Copy).then_inc(s_qh, 1)
                if m in (2, 5):
                    wkv_hi(2 + m // 5)

            def kv_hi(q, i, par, g, c, lat, used):
                act.wait_ge(s_proj, q + 1)
                if not (type(used) is int and used == 0):
                    act.wait_ge(s_qk if i < 2 else s_pv, used)
                kv_copy(i, par, lat, HI, lambda dst, src: ac.activation(dst, src, ACT.Copy)).then_inc(s_kvh, 1)

            for i in range(HG):
                kv_hi(i, i, 0, 0, 1, True, 0)

            def round_(it, first, last):
                w = P if first else CW

                def pt_hi(t):
                    T = STEPS * it + t
                    act.wait_ge(s_tr, T + 1)
                    if not (first and t < 2):
                        act.wait_ge(s_pv, T - 1)
                    ac.activation(PT[:, t % 2, HI, 0:w], pT[:, t % 2, 0:w], ACT.Copy).then_inc(s_pth, 1)

                def rescale(u):
                    if not first:
                        U = UNITS * it + u
                        act.wait_ge(s_dm, U + 1)
                        ac.activation(alpha[:, u % 2, :], dm[:, u % 2, :], ACT.Exp, scale=XSC).then_inc(s_alpha, 1)

                for t in range(STEPS):
                    u, i, c = t // HG, t % HG, t // (STEPS // 2)
                    par = u % 2
                    T = STEPS * it + t
                    act.wait_ge(s_negm, T + 1)
                    if i == 0 and not (first and u < 2):
                        act.wait_ge(s_osc, UNITS * it + u - 1)
                    ac.activation(SP[:, t % 2, 0:w], SP[:, t % 2, 0:w], ACT.Exp, bias=negm[:, par, i:i + 1],
                                  scale=XSC, accum_out=rs[:, par, i:i + 1]).then_inc(s_exp, 1)
                    part = part_at(it, t, first, last)
                    if part:
                        kv_hi(*part)
                    if i == 0 and u > 0:
                        rescale(u - 1)
                    if t > 0:
                        pt_hi(t - 1)
                    k = t % (STEPS // 2) - 6
                    if 0 <= k < KD and ((c == 0 and not first) or (c == 1 and not last)):
                        x_evac(4 + 4 * (2 * it - 1 + c) + k, k, 1 - c, CW, Kg1 + k, Kb1 + k)
                    if last and STEPS // 2 <= t < STEPS // 2 + 4:
                        split_hi(0, t - STEPS // 2)
                    if last and t >= STEPS - 4 + 1:
                        split_hi(1, t - STEPS + 3)
                rescale(UNITS - 1)
                pt_hi(STEPS - 1)

            round_(0, True, False)
            with act.Fori(1, ROUNDS) as it:
                round_(it, False, False)
            round_(ROUNDS, False, True)

            split_hi(1, 3)
            split_hi(2)
            nb = [0]

            def transposed_hi(dst, n_banks):
                for cc in range(n_banks):
                    act.wait_ge(s_tt, nb[0] + 1)
                    ac.activation(dst[:, HI, 2 * cc:2 * cc + 2, :], pT[:, nb[0] % 2, :].rearrange("p (c t) -> p c t", c=2),
                                  ACT.Copy).then_inc(s_th, 1)
                    nb[0] += 1

            transposed_hi(OT, 4)
            split_hi(3)
            transposed_hi(HT, 2)
            split_hi(4)
            split_hi(5)
            split_hi(6)
            act.wait_ge(s_wuse, 5)
            for b in range(B):
                ac.activation(VV[:, HI, b, :], (pV, pX)[b][:, :], ACT.Copy).then_inc(s_vh, 1)
            transposed_hi(QTs, 2)
            split_hi(7)
            act.wait_ge(s_kz, 1)
            for cc in range(2):
                act.wait_ge(s_tt, nb[0] + 1)
                for h in range(4):
                    rows = slice(SD * h, SD * h + SD)
                    last = ac.activation(KB[rows, HI, 2 * cc:2 * cc + 2, :, h, :],
                                         pT[rows, nb[0] % 2, :].rearrange("p (c b t) -> p c b t", c=2, b=B), ACT.Copy)
                last.then_inc(s_th, 1)
                nb[0] += 1

            def p_hi(n):
                act.wait_ge(s_pt2, n + 1)
                if n >= 2:
                    act.wait_ge(s_pv2, n - 1)
                ac.activation(PT[:, n % 2, HI, :], pJ[:, n % 2, :], ACT.Copy).then_inc(s_p2h, 1)

            for n in range(8):
                act.wait_ge(s_sm, n + 1)
                ac.activation(SM[:, n % 2, :], SM[:, n % 2, :], ACT.Exp, scale=SSC).then_inc(s_se, 1)
                if n >= 1:
                    p_hi(n - 1)
                if n == 3:
                    split_hi(8)
            p_hi(7)
            transposed_hi(AT, 2)
            transposed_hi(HT, 2)

            act.wait_ge(s_kt, 1)
            act.wait_ge(s_kz, 2)
            kz = pV[:, 0:256].rearrange("p (m n) -> p m n", m=4)
            ac.activation(KBk[0:NK, HI, :, 0:NK], kz[0:NK], ACT.Copy)
            ac.activation(KBk[NK:P, HI, :, NK:P], kz[NK:P], ACT.Copy).then_inc(s_kh, 1)
            for j in range(2):
                act.wait_ge(s_q2, j + 1)
                ac.activation(QT2[:, HI, 2 * j:2 * j + 2, :], pS[:, j, :].rearrange("p (m t) -> p m t", m=2), ACT.Copy).then_inc(s_q2h, 1)

            act.wait_ge(d_sel, 16)
            ac.activation(KV[:, 1024:3072], EQ, ACT.Copy).then_inc(s_selr, 1)
            split_hi(FB + 2)

            def gate_silu(ft):
                act.wait_ge(s_gu, ft + 1)
                if ft >= 2:
                    act.wait_ge(s_a, ft - 1)
                ac.activation(ME[:, ft % 2, :], pS[:, ft % 2, 0:T2], ACT.Silu, bias=vec[:, Kbg + ft:Kbg + ft + 1]).then_inc(s_ge, 1)

            gate_silu(0)
            for ft in range(16):
                act.wait_ge(s_a, ft + 1)
                if ft >= 2:
                    act.wait_ge(s_mo, ft - 1)
                ac.activation(ACTT[:, ft % 2, HI, :], MA[:, ft % 2, :], ACT.Copy).then_inc(s_ah, 1)
                if ft < 15:
                    gate_silu(ft + 1)
                for n in tile_splits(ft):
                    split_hi(n)
                j = ft % 5
                if ft < 10 and j == 1:
                    act.wait_ge(s_tk, 3 * (ft // 5) + 1)
                    ac.activation(EV, EV, ACT.Exp).then_inc(s_tke, 1)
                if ft < 10 and j == 2:
                    act.wait_ge(s_tk, 3 * (ft // 5) + 2)
                    ac.activation(ZS, ZS, ACT.Ln).then_inc(s_tke, 1)
                if ft < 10 and j == 3:
                    act.wait_ge(s_tk, 3 * (ft // 5) + 3)
                    ac.activation(EXC, EXC, ACT.Exp).then_inc(s_tke, 1)
                if ft in (6, 11):
                    b = ft // 11
                    act.wait_ge(s_gt, b + 1)
                    ac.activation(GX[:, HI, :, b, :], pJ[:, b, :].rearrange("p (h t) -> p h t", h=RH), ACT.Copy)
                    ac.activation(RT[:, :, b, :], pT[:, b, :].rearrange("p (h t) -> p h t", h=RH), ACT.Copy).then_inc(s_gh, 1)

            def front(e):
                n = EB + 2 * (e // 4)
                act.wait_ge(s_dt, e + 1)
                if e % 4 == 0:
                    slot_free(act, n)
                ac.activation(slot(n, HI)[:, 512 * (e % 4):512 * (e % 4) + 512], pS[:, 0, :], ACT.Copy).then_inc(s_dh, 1)
                act.wait_ge(s_gd, e + 1)
                if e >= 1:
                    act.wait_ge(s_md, e)
                ac.activation(EW, pJ[:, :, :].rearrange("p a n -> p (a n)"), ACT.Exp).then_inc(s_gexp, 1)

            front(0)
            for e in range(ETS):
                if e + 1 < ETS:
                    front(e + 1)
                if e % 4 == 2 and e < ETS - 4:
                    split_hi(EB + 2 * (e // 4) + 3)
                act.wait_ge(s_w, e + 1)
                if e >= 1:
                    act.wait_ge(s_c, e)
                ac.activation(WE, pS[:, 1, 0:T2], ACT.Tanh, scale=0.5).then_inc(s_we, 1)
                act.wait_ge(s_c, e + 1)
                if e >= 2:
                    act.wait_ge(s_eo, e - 1)
                ac.activation(GT[:, e % 2, HI, :], WC[:, e % 2, :], ACT.Copy).then_inc(s_chi, 1)

        @block.vector
        def _(dve):
            ve = nc.vector
            links = [0]

            def link(ins):
                links[0] += 1
                ins.then_inc(s_ch, 1)
                dve.wait_ge(s_ch, links[0])

            def low(dst, src, hi):
                return ve.tensor_tensor(dst, src, hi.bitcast(F32), ALU.subtract)

            dve.wait_ge(d_x, 16)
            for i, src in enumerate((xres, SP)):
                for b in range(B):
                    last = ve.bn_stats(st[:, b, :], src[:, b, :])
                link(last)
                for b in range(B):
                    last = ve.bn_aggr(mv[:, b, :], st[:, b, :])
                last.then_inc(s_stat, 1)
                dve.wait_ge(s_lat, i + 1)
                dve.wait_ge(s_stat, i + 1)
                for b in range(B):
                    last = ve.tensor_scalar(SP[:, b, :], src[:, b, :], mv[:, b, 0:1], rstd[:, b:b + 1], ALU.subtract, ALU.mult)
                if i == 0:
                    link(last)
                else:
                    last.then_inc(s_latn, 1)
            for j in range(2):
                dve.wait_ge(s_wqh, j + 1)
                src = (raw[:, :].rearrange("p (k n) -> p k n", k=2), O[:, :, :])[j]
                low(WQ[:, LO, 2 * j:2 * j + 2, :], src, WQ[:, HI, 2 * j:2 * j + 2, :]).then_inc(s_wql, 1)

            def wkv_lo(k):
                dve.wait_ge(s_wkvh, k + 1)
                low(WKV[:, LO, k, :], (raw[:, :], Of)[k % 2], WKV[:, HI, k, :]).then_inc(s_wkvl, 1)

            for k in range(2):
                wkv_lo(k)
            for m in range(H // 2):
                dve.wait_ge(s_qh, m + 1)
                low(QT[0:DH, LO, 2 * m, :], pJ[0:DH, m % 2, 0:T2], QT[0:DH, HI, 2 * m, :])
                low(QT[DH:P, LO, 2 * m + 1, :], pJ[DH:P, m % 2, 0:T2], QT[DH:P, HI, 2 * m + 1, :]).then_inc(s_ql, 1)
                if m in (2, 5):
                    wkv_lo(2 + m // 5)

            def kv_lo(q, i, par, g, c, lat, used):
                dve.wait_ge(s_kvh, q + 1)
                hi = kv_copy(i, par, lat, HI, lambda dst, src: dst)
                kv_copy(i, par, lat, LO, lambda dst, src: low(dst, src, hi)).then_inc(s_kvl, 1)

            for i in range(HG):
                kv_lo(i, i, 0, 0, 1, True, 0)

            def round_(it, first, last):
                w = P if first else CW

                def pt_lo(t):
                    dve.wait_ge(s_pth, STEPS * it + t + 1)
                    low(PT[:, t % 2, LO, 0:w], pT[:, t % 2, 0:w], PT[:, t % 2, HI, 0:w]).then_inc(s_ptl, 1)

                def add_output(u):
                    U = UNITS * it + u
                    b, g, _ = unit_of(u, first)
                    o = O[:, b, 256 * g:256 * g + 256].rearrange("p (h e) -> p h e", h=HG)
                    dve.wait_ge(s_pv, HG * U + HG)
                    dve.wait_ge(s_osc, U + 1)
                    if first:
                        ve.tensor_copy(o, pVh[:, :, HI, :]).then_inc(s_ohalf, 1)
                    else:
                        ve.tensor_tensor(o, pVh[:, :, HI, :], o, ALU.add).then_inc(s_ohalf, 1)
                    dve.wait_ge(s_ohalf, U + 1)
                    ve.tensor_tensor(o, pVh[:, :, LO, :], o, ALU.add).then_inc(s_oadd, 1)

                for t in range(STEPS):
                    u, i, c = t // HG, t % HG, t // (STEPS // 2)
                    b, g, _ = unit_of(u, first)
                    par = u % 2
                    T = STEPS * it + t
                    prep = (c == 0 and not first) or (c == 1 and not last)
                    r = 2 * it - 1 + c
                    dve.wait_ge(s_qk, T + 1)
                    if not (first and t < 2):
                        dve.wait_ge(s_tr, T - 1)
                    if i == 0 and not (first and u < 2):
                        dve.wait_ge(s_dm, UNITS * it + u - 1)
                    if t % 16 == 0 and not first:
                        dve.wait_ge(s_mb, 2 * it - 1 + c)
                    passed(dve)
                    ve.tensor_tensor_reduce(out=SP[:, t % 2, 0:w], in0=pS[:, t % 2, 0:w], in1=MB[:, c, 0:w], scale=1.0,
                                            scalar=-3e38 if first else mold[:, b, HG * g + i:HG * g + i + 1],
                                            op0=ALU.add, op1=ALU.max, accum_out=mcur[:, par, i:i + 1]).then_inc(s_ttr, 1)
                    dve.wait_ge(s_ttr, T + 1)
                    ve.tensor_scalar(negm[:, par, i:i + 1], mcur[:, par, i:i + 1], -XSC, None, ALU.mult).then_inc(s_negm, 1)
                    if i == 1 and u > 0:
                        add_output(u - 1)
                    part = part_at(it, t, first, last)
                    if part:
                        kv_lo(*part)
                    if t > 0:
                        pt_lo(t - 1)
                    if prep and t % 16 < NT:
                        if t % 16 == 0:
                            dve.wait_ge(d_raw, 16 * r + 16)
                        ve.bn_stats(st[:, t % 16, :], rawc[:, t % 16, :]).then_inc(s_bn, 1)
                        if t % 16 == NT - 1:
                            dve.wait_ge(s_bn, NT * r + NT)
                            passed(dve)
                            for k in range(NT):
                                ins = ve.bn_aggr(mv[:, k, :], st[:, k, :])
                            ins.then_inc(s_stat, 1)
                    if prep and t % 16 in (4, 5):
                        if t % 16 == 4:
                            dve.wait_ge(s_stat, r + 3)
                            dve.wait_ge(s_lat, r + 3)
                            passed(dve)
                        for k in (2 * (t % 16) - 8, 2 * (t % 16) - 7):
                            ins = ve.tensor_scalar(rawc[:, k, :], rawc[:, k, :], mv[:, k, 0:1], rstd[:, k:k + 1],
                                                   ALU.subtract, ALU.mult)
                        if t % 16 == 5:
                            ins.then_inc(s_norm, 1)
                    if prep and t % 16 == 6:
                        dve.wait_ge(d_mask, 16 * r + 16)
                        passed(dve)
                        ve.tensor_scalar(MB[:, 1 - c, :], mraw[:, :], BIG, -BIG, ALU.mult, ALU.add).then_inc(s_mb, 1)
                pt_lo(STEPS - 1)
                add_output(UNITS - 1)

            round_(0, True, False)
            with dve.Fori(1, ROUNDS) as it:
                round_(it, False, False)
            round_(ROUNDS, False, True)

            nb = [0]

            def transposed_lo(dst, n_banks):
                for cc in range(n_banks):
                    dve.wait_ge(s_th, nb[0] + 1)
                    low(dst[:, LO, 2 * cc:2 * cc + 2, :], pT[:, nb[0] % 2, :].rearrange("p (c t) -> p c t", c=2),
                        dst[:, HI, 2 * cc:2 * cc + 2, :]).then_inc(s_tl, 1)
                    nb[0] += 1

            def add_rows(i):
                dve.wait_ge(s_wuse, (2, 6)[i])
                for b in range(B):
                    last = ve.tensor_tensor(xres[:, b, :], pS[:, b, :], xres[:, b, :], ALU.add)
                last.then_inc(s_yread, 1)
                dve.wait_ge(s_yread, i + 1)
                for b in range(B):
                    last = ve.bn_stats(st[:, b, :], xres[:, b, :])
                link(last)
                for b in range(B):
                    last = ve.bn_aggr(mv[:, b, :], st[:, b, :])
                last.then_inc(s_ln, 1)
                dve.wait_ge(s_ln, i + 1)
                dve.wait_ge(s_pn, i + 1)
                for b in range(B):
                    last = ve.tensor_scalar(hn[:, b, :], xres[:, b, :], mv[:, b, 0:1], rstd[:, b:b + 1], ALU.subtract, ALU.mult)
                last.then_inc(s_src, 1)

            dve.wait_ge(s_osc, UNITS * (ROUNDS + 1))
            dve.wait_ge(s_oadd, UNITS * (ROUNDS + 1))
            link(ve.reciprocal(small[:, 0:32], lsum[:, :, :].rearrange("p b h -> p (b h)")))
            ov = Of.rearrange("p (h e) -> p h e", e=DH)
            ve.tensor_tensor(ov, ov, small[:, 0:32].unsqueeze(2).broadcast_to([P, B * H, DH]), ALU.mult).then_inc(s_src, 1)
            transposed_lo(OT, 4)
            dve.wait_ge(s_pv, STEPS * (ROUNDS + 1))
            ve.memset(KV[:, :].bitcast(U32), 0).then_inc(s_kz, 1)
            add_rows(0)
            transposed_lo(HT, 2)

            dve.wait_ge(d_rope, 48)
            dve.wait_ge(s_wlo, 4)
            for m, (bank, R) in enumerate(((pS, QR), (pJ, KR))):
                dve.wait_ge(s_wuse, m + 3)
                for b in range(B):
                    z = bank[:, b, :].rearrange("p (h e two) -> p h e two", h=SH, two=2)
                    r = R[:, b, :].rearrange("p (h e two) -> p h e two", h=SH, two=2)
                    cos = rope[:, 0, :].unsqueeze(1).broadcast_to([P, SH, SD // 2])
                    sin = rope[:, 1, :].unsqueeze(1).broadcast_to([P, SH, SD // 2])
                    ve.tensor_tensor(RTMP[:, 0], z[:, :, :, 0], cos, ALU.mult)
                    ve.tensor_tensor(RTMP[:, 1], z[:, :, :, 1], sin, ALU.mult)
                    ve.tensor_tensor(RTMP[:, 2], z[:, :, :, 0], sin, ALU.mult)
                    link(ve.tensor_tensor(RTMP[:, 3], z[:, :, :, 1], cos, ALU.mult))
                    ve.tensor_tensor(r[:, :, :, 0], RTMP[:, 0], RTMP[:, 1], ALU.subtract)
                    ve.tensor_tensor(r[:, :, :, 1], RTMP[:, 2], RTMP[:, 3], ALU.add).then_inc(s_rope, 1)
                    dve.wait_ge(s_rope, 2 * m + b + 1)
            for b in range(B):
                dve.wait_ge(s_vh, b + 1)
                low(VV[:, LO, b, :], (pV, pX)[b][:, :], VV[:, HI, b, :]).then_inc(s_vl, 1)
            transposed_lo(QTs, 2)
            for cc in range(2):
                dve.wait_ge(s_th, nb[0] + 1)
                for h in range(4):
                    rows = slice(SD * h, SD * h + SD)
                    last = low(KB[rows, LO, 2 * cc:2 * cc + 2, :, h, :],
                               pT[rows, nb[0] % 2, :].rearrange("p (c b t) -> p c b t", c=2, b=B),
                               KB[rows, HI, 2 * cc:2 * cc + 2, :, h, :])
                last.then_inc(s_tl, 1)
                nb[0] += 1

            def p_lo(n):
                dve.wait_ge(s_se, n + 1)
                b, c = n // 4, n % 4
                ve.tensor_reduce(small[:, 16 * b + 4 * c:16 * b + 4 * c + 4], SM[:, n % 2, :].rearrange("p (h t) -> p h t", h=4),
                                 AX.X, ALU.add)
                dve.wait_ge(s_p2h, n + 1)
                low(PT[:, n % 2, LO, :], pJ[:, n % 2, :], PT[:, n % 2, HI, :]).then_inc(s_p2l, 1)

            for n in range(8):
                sm = SM[:, n % 2, :].rearrange("p (h t) -> p h t", h=4)
                dve.wait_ge(s_sc, n + 1)
                if n >= 2:
                    dve.wait_ge(s_pt2, n - 1)
                link(ve.tensor_tensor(sm, pS[:, n % 2, :].rearrange("p (h t) -> p h t", h=4),
                                      cmask[:, :].unsqueeze(1).broadcast_to([P, 4, P]), ALU.add))
                link(ve.tensor_reduce(small[:, 32:36], sm, AX.X, ALU.max))
                ve.tensor_tensor(sm, sm, small[:, 32:36].unsqueeze(2).broadcast_to([P, 4, P]), ALU.subtract).then_inc(s_sm, 1)
                if n >= 1:
                    p_lo(n - 1)
            p_lo(7)
            dve.wait_ge(s_p2l, 8)
            link(ve.reciprocal(small[:, 0:32], small[:, 0:32]))
            dve.wait_ge(s_pv2, 8)
            for b in range(B):
                last = ve.tensor_tensor(an[:, b, :].rearrange("p (h e) -> p h e", e=SD),
                                        (pV, pX)[b][:, :].rearrange("p (h e) -> p h e", e=SD),
                                        small[:, 16 * b:16 * b + 16].unsqueeze(2).broadcast_to([P, SH, SD]), ALU.mult)
            last.then_inc(s_src, 1)
            transposed_lo(AT, 2)
            add_rows(1)
            transposed_lo(HT, 2)
            dve.wait_ge(s_kh, 1)
            kz = pV[:, 0:256].rearrange("p (m n) -> p m n", m=4)
            low(KBk[0:NK, LO, :, 0:NK], kz[0:NK], KBk[0:NK, HI, :, 0:NK])
            low(KBk[NK:P, LO, :, NK:P], kz[NK:P], KBk[NK:P, HI, :, NK:P]).then_inc(s_kl, 1)
            for j in range(2):
                dve.wait_ge(s_q2h, j + 1)
                low(QT2[:, LO, 2 * j:2 * j + 2, :], pS[:, j, :].rearrange("p (m t) -> p m t", m=2), QT2[:, HI, 2 * j:2 * j + 2, :]).then_inc(s_q2l, 1)
            for b in range(B):
                dve.wait_ge(s_sim, b + 1)
                ve.tensor_copy(SIM[:, b, :], pJ[:, b, :]).then_inc(s_simc, 1)
            dve.wait_ge(s_simc, 2)
            dve.wait_ge(d_bd, 16)
            for b in range(B):
                ve.tensor_tensor(an[:, b, :], xres[:, b, :], hn[:, 0, :], ALU.add)

            hk = lambda t: t.rearrange("p (h k) -> p h k", h=RH)
            V8v = V8.rearrange("p (s h k) -> p s h k", s=2, h=RH)
            IXv = IX[:, :].rearrange("p (s h k) -> p s h k", s=2, h=RH)
            IXFv = IXF.rearrange("p (s n) -> p s n", s=2)
            SC4 = SC.rearrange("p (h a k) -> p h a k", h=RH, a=8)
            SC3 = SC.rearrange("p (h n) -> p h n", h=RH)
            EXC3 = EXC.rearrange("p (h n) -> p h n", h=RH)
            EQ3 = EQ.rearrange("p (n k) -> p n k", k=NK)

            def top_sides(b):
                for s in range(2):
                    for h in range(RH):
                        col = 256 * s + NK * h
                        last = ve.max(V8v[:, s, h, :], SIM[:, b, col:col + NK])
                link(last)
                for s in range(2):
                    for h in range(RH):
                        col = 256 * s + NK * h
                        last = ve.max_index(IXv[:, s, h, :], V8v[:, s, h, :], SIM[:, b, col:col + NK])
                link(last)
                ve.tensor_copy(IXF, IX[:, :])
                link(ve.tensor_tensor(SC4, V8v[:, 0].unsqueeze(3).broadcast_to([P, RH, 8, 8]),
                                      V8v[:, 1].unsqueeze(2).broadcast_to([P, RH, 8, 8]), ALU.add))

            def top_sums(b):
                for h in range(RH):
                    last = ve.max(hk(VALS)[:, h, :], SC3[:, h, :])
                link(last)
                for h in range(RH):
                    last = ve.match_replace(REP.rearrange("p (h n) -> p h n", h=RH)[:, h, :], hk(VALS)[:, h, :], SC3[:, h, :], -3e38)
                ve.tensor_tensor(hk(EV), hk(VALS), hk(VALS)[:, :, 0:1].broadcast_to([P, RH, 8]), ALU.subtract).then_inc(s_tk, 1)
                dve.wait_ge(s_tk, 3 * b + 1)
                link(ve.tensor_tensor(CM, REP, SC, ALU.not_equal))
                link(ve.tensor_reduce(N8, CM.rearrange("p (n k) -> p n k", k=8), AX.X, ALU.add))

            def softmax_sum(b):
                dve.wait_ge(s_tke, 3 * b + 1)
                ve.tensor_reduce(ZS, hk(EV), AX.X, ALU.add).then_inc(s_tk, 1)

            def place_x(b):
                dve.wait_ge(s_tke, 3 * b + 2)
                if b == 1:
                    dve.wait_ge(s_gt, 1)
                link(ve.tensor_tensor(OFF, hk(VALS)[:, :, 0], ZS, ALU.add))
                ve.tensor_tensor(EXC3, SC3, OFF.unsqueeze(2).broadcast_to([P, RH, NK]), ALU.subtract).then_inc(s_tk, 1)
                sim = SIM[:, b, :].rearrange("p (s h n) -> p s h n", s=2, h=RH)
                ve.tensor_tensor(GN[:, :, 0:NK], sim[:, 0], OFF.unsqueeze(2).broadcast_to([P, RH, NK]), ALU.subtract)
                ve.tensor_copy(GN[:, :, NK:P], sim[:, 1])
                place(0, N8.unsqueeze(2).broadcast_to([P, 32, NK]), EQ3)
                ve.tensor_reduce(RN[:, :, 0:NK], EQ.rearrange("p (h a n) -> p h n a", h=RH, a=8), AX.X, ALU.add).then_inc(s_pl, 1)
                dve.wait_ge(s_pl, 2 * b + 1)

            def place(side, weight, eq):
                if side == 0:
                    dve.wait_ge(s_selr, 1)
                link(ve.tensor_tensor(EQ3, IOTA.unsqueeze(1).broadcast_to([P, 32, NK]),
                                      IXFv[:, side, :].unsqueeze(2).broadcast_to([P, 32, NK]), ALU.is_equal))
                link(ve.tensor_tensor(eq, eq, weight, ALU.mult))

            def place_y(b):
                place(1, W8.unsqueeze(1).unsqueeze(3).broadcast_to([P, RH, 8, NK]), EQ.rearrange("p (h a n) -> p h a n", h=RH, a=8))
                ve.tensor_reduce(RN[:, :, NK:P], EQ.rearrange("p (h a n) -> p h n a", h=RH, a=8), AX.X, ALU.add).then_inc(s_pl, 1)
                dve.wait_ge(s_pl, 2 * b + 2)
                ve.tensor_scalar(RN[:, :, NK:P], RN[:, :, NK:P], -8.0, None, ALU.add).then_inc(s_gn, 1)
                ve.tensor_scalar(GE, IXFv[:, 0, :], float(NEXP // NK), None, ALU.is_ge)
                dve.wait_ge(s_tke, 3 * b + 3)
                link(ve.tensor_tensor(EXC, EXC, CM, ALU.mult))
                e8 = EXC.rearrange("p (n k) -> p n k", k=8)
                link(ve.tensor_tensor(e8, e8, GE.unsqueeze(2).broadcast_to([P, 32, 8]), ALU.mult))
                link(ve.tensor_reduce(EXB[:, b:b + 1], EXC, AX.X, ALU.add))

            dve.wait_ge(s_iota, 2)
            for ft in range(16):
                dve.wait_ge(s_ge, ft + 1)
                ve.scalar_tensor_tensor(out=MA[:, ft % 2, :], in0=pS[:, ft % 2, T2:2 * T2], scalar=vec[:, Kbu + ft:Kbu + ft + 1],
                                        in1=ME[:, ft % 2, :], op0=ALU.add, op1=ALU.mult).then_inc(s_a, 1)
                dve.wait_ge(s_ah, ft + 1)
                low(ACTT[:, ft % 2, LO, :], MA[:, ft % 2, :], ACTT[:, ft % 2, HI, :]).then_inc(s_al, 1)
                if ft < 10:
                    (top_sides, top_sums, softmax_sum, place_x, place_y)[ft % 5](ft // 5)
                if ft in (6, 11):
                    b = ft // 11
                    dve.wait_ge(s_gh, b + 1)
                    low(GX[:, LO, :, b, :], pJ[:, b, :].rearrange("p (h t) -> p h t", h=RH), GX[:, HI, :, b, :]).then_inc(s_gl, 1)
                if ft == 12:
                    dve.wait_ge(s_ex, 1)
                    ve.tensor_copy(exrow[:, :], pJ[0:1, 0, 0:T2]).then_inc(s_exe, 1)
                if ft == 13:
                    dve.wait_ge(s_ex, 2)
                    ve.tensor_copy(EXT, pJ[:, 1, 0:T2]).then_inc(s_exe, 1)

            def front(e):
                n = EB + 2 * (e // 4)
                cs = slice(512 * (e % 4), 512 * (e % 4) + 512)
                dve.wait_ge(s_dh, e + 1)
                low(slot(n, LO)[:, cs], pS[:, 0, :], slot(n, HI)[:, cs]).then_inc(s_dl, 1)
                dve.wait_ge(s_gexp, e + 1)
                if e >= 1:
                    dve.wait_ge(s_hs, e)
                ve.scalar_tensor_tensor(out=MW, in0=pT[:, :, :].rearrange("p a n -> p (a n)"), scalar=0.0, in1=EW,
                                        op0=ALU.is_gt, op1=ALU.mult).then_inc(s_md, 1)

            front(0)
            for e in range(ETS):
                if e + 1 < ETS:
                    front(e + 1)
                dve.wait_ge(s_we, e + 1)
                link(ve.scalar_tensor_tensor(out=WR_, in0=WE, scalar=1.0, in1=pS[:, 1, 0:T2], op0=ALU.add, op1=ALU.mult))
                dve.wait_ge(s_hs, e + 1)
                if e == ETS - 1:
                    link(ve.tensor_tensor(HS[:, e % 2, :], HS[:, e % 2, :], EXT, ALU.add))
                ve.scalar_tensor_tensor(out=WC[:, e % 2, :], in0=WR_, scalar=0.5, in1=HS[:, e % 2, :],
                                        op0=ALU.mult, op1=ALU.mult).then_inc(s_c, 1)
                dve.wait_ge(s_chi, e + 1)
                low(GT[:, e % 2, LO, :], WC[:, e % 2, :], GT[:, e % 2, HI, :]).then_inc(s_cl, 1)
            dve.wait_ge(s_eo, ETS)
            for b in range(B):
                last = ve.tensor_tensor(an[:, b, :], (pV, pX)[b][:, :], an[:, b, :], ALU.add)
            last.then_inc(s_fin, 1)

        @block.tensor
        def _(pe):
            te = nc.tensor

            def product(dst, a, b, start, stop):
                te.matmul(dst, a(HI), b(HI), start=start, stop=False)
                te.matmul(dst, a(HI), b(LO), start=False, stop=False)
                return te.matmul(dst, a(LO), b(HI), start=False, stop=stop)

            pe.wait_ge(d_vec, 96)
            pe.wait_ge(s_ident, 2)
            te.transpose(pX[:, 0:48], vrow[:, :], ident[0:48, 0:48]).then_inc(s_vt, 1)
            pe.wait_ge(s_vec, 1)
            pe.wait_ge(s_latn, 1)
            for k in range(KD):
                if k > 0:
                    pe.wait_ge(s_xh, k)
                for b in range(B):
                    last = te.transpose(pX[:, P * b:P * b + P], SP[:, b, P * k:P * k + P], ident[:, :])
                last.then_inc(s_xtr, 1)
            pe.wait_ge(s_xT, KD)
            pe.wait_ge(s_wql, 2)
            for m in range(H // 2):
                if m >= 2:
                    pe.wait_ge(s_ql, m - 1)
                for k in range(KD):
                    last = product(pJ[:, m % 2, 0:T2], lambda s: WQ[:, s, k, P * m:P * m + P],
                                   lambda s: XT[:, 1, s, k, 0:T2], k == 0, k == KD - 1)
                last.then_inc(s_q, 1)

            def project(q, i, par, g, c, lat, used):
                if not (type(q) is int and q < 2):
                    pe.wait_ge(s_kvl, q - 1)
                if i < 2:
                    w = T2 if lat else CW
                    for k in range(KD):
                        last = product(pJ[:, i % 2, 0:w], lambda s: WKV[:, s, k, P * (2 * g + i):P * (2 * g + i + 1)],
                                       lambda s: XT[:, c, s, k, 0:w], k == 0, k == KD - 1)
                else:
                    for n, t in enumerate([i - 2] if lat else [2 * i - 4, 2 * i - 3]):
                        for k in range(KD):
                            last = product(pJ[:, i % 2, 256 * n:256 * n + 256],
                                           lambda s: XT[:, c, s, k, P * t:P * t + P],
                                           lambda s: WKV[:, s, k, INNER + 256 * g:INNER + 256 * g + 256], k == 0, k == KD - 1)
                last.then_inc(s_proj, 1)

            pe.wait_ge(s_ql, H // 2)
            pe.wait_ge(s_wkvl, KD)
            for i in range(HG):
                project(i, i, 0, 0, 1, True, 0)

            def round_(it, first, last_round):
                w = P if first else CW
                tiles = w // P

                def transpose_p(t):
                    T = STEPS * it + t
                    pe.wait_ge(s_exp, T + 1)
                    if not (first and t < 2):
                        pe.wait_ge(s_ptl, T - 1)
                    for n in range(tiles):
                        last = te.transpose(pT[:, t % 2, P * n:P * n + P], SP[:, t % 2, P * n:P * n + P], ident[:, :])
                    last.then_inc(s_tr, 1)

                def values(t):
                    u, i = t // HG, t % HG
                    T = STEPS * it + t
                    U = UNITS * it + u
                    pe.wait_ge(s_ptl, T + 1)
                    b, g, par = unit_of(u, first)
                    if i == 0:
                        pe.wait_ge(s_kvl, HG * g + HG if first else HG * U + HG - (STEPS - LAT))
                        if not (first and u == 0):
                            pe.wait_ge(s_oadd, U)
                    for n in range(tiles):
                        for s in (HI, LO):
                            last = te.matmul(pVh[:, i, :, :], PT[:, t % 2, s, P * n:P * n + P],
                                             VT[:, par, :, b if first else n, DH * i:DH * i + DH],
                                             start=n == 0 and s == HI, stop=n == tiles - 1 and s == LO)
                    last.then_inc(s_pv, 1)

                for t in range(STEPS):
                    u, i, c = t // HG, t % HG, t // (STEPS // 2)
                    b, g, par = unit_of(u, first)
                    T = STEPS * it + t
                    if i % 2 == 0:
                        pe.wait_ge(s_kvl, HG * g + i // 2 + 1 if first else T + i // 2 - i + 1 - (STEPS - LAT))
                    if not (first and t < 2):
                        pe.wait_ge(s_ttr, T - 1)
                    q = lambda s: QT[:, s, HG * g + i, L * b:L * b + L]
                    keys_ = lambda s: KT[:, par, s, i // 2, L * b:L * b + L] if first else KT[:, par, s, i // 2, :]
                    product(pS[:, t % 2, 0:w], q, keys_, True, True).then_inc(s_qk, 1)
                    part = part_at(it, t, first, last_round)
                    if part:
                        if i == 0 and u == G - 1 and not first:
                            pe.wait_ge(s_xT, 8 * it + 4)
                        if i == 0 and u == UNITS - 1:
                            pe.wait_ge(s_xT, 8 * it + 8)
                        project(*part)
                    k = t % (STEPS // 2) - 6
                    if 0 <= k < KD and ((c == 0 and not first) or (c == 1 and not last_round)):
                        r = 2 * it - 1 + c
                        if k == 0:
                            pe.wait_ge(s_norm, r + 1)
                        pe.wait_ge(s_xh, 4 + 4 * r + k)
                        for n in range(NT):
                            last = te.transpose(pX[:, P * n:P * n + P], rawc[:, n, P * k:P * k + P], ident[:, :])
                        last.then_inc(s_xtr, 1)
                    if t >= 1:
                        transpose_p(t - 1)
                    if t >= 2:
                        values(t - 2)
                transpose_p(STEPS - 1)
                values(STEPS - 2)
                values(STEPS - 1)

            round_(0, True, False)
            with pe.Fori(1, ROUNDS) as it:
                round_(it, False, False)
            round_(ROUNDS, False, True)

            pe.wait_ge(s_ptl, STEPS * (ROUNDS + 1))
            pe.wait_ge(s_oadd, UNITS * (ROUNDS + 1))
            nb = [0]

            def transpose_rows(src, n_banks, ready):
                pe.wait_ge(s_src, ready)
                for cc in range(n_banks):
                    if nb[0] >= 2:
                        pe.wait_ge(s_tl, nb[0] - 1)
                    for ci in range(2):
                        for b in range(B):
                            col = P * (2 * cc + ci)
                            last = te.transpose(pT[:, nb[0] % 2, P * (2 * ci + b):P * (2 * ci + b) + P],
                                                src[:, b, col:col + P], ident[:, :])
                    last.then_inc(s_tt, 1)
                    nb[0] += 1

            def weight_ready(n):
                pe.wait_ge(s_wlo, n_split(n) + 1)

            def rows(dst, src, n, k0=0, start=True, stop=True):
                for b in range(B):
                    for k in range(4):
                        last = product(dst(b), lambda s: src[:, s, k0 + k, L * b:L * b + L], lambda s: slot4(n, s)[:, k, :],
                                       start and k == 0, stop and k == 3)
                return last.then_inc(s_wuse, 1)

            transpose_rows(O, 4, 1)
            pe.wait_ge(s_tl, 4)
            weight_ready(0)
            rows(lambda b: pS[:, b, :], OT, 0, 0, True, False)
            weight_ready(1)
            rows(lambda b: pS[:, b, :], OT, 1, 4, False, True)
            transpose_rows(hn, 2, 2)
            pe.wait_ge(s_tl, 6)
            for m, dst in enumerate((lambda b: pS[:, b, :], lambda b: pJ[:, b, :], lambda b: (pV, pX)[b][:, :])):
                weight_ready(2 + m)
                rows(dst, HT, 2 + m)
            pe.wait_ge(s_rope, 2)
            transpose_rows(QR, 2, 2)
            pe.wait_ge(s_rope, 4)
            transpose_rows(KR, 2, 2)
            pe.wait_ge(s_tl, 10)

            def scores(n):
                b, c = n // 4, n % 4
                if n >= 2:
                    pe.wait_ge(s_sm, n - 1)
                product(pS[:, n % 2, :], lambda s: QTs[:, s, c, L * b:L * b + L],
                        lambda s: KB[:, s, c, b, :, :], True, True).then_inc(s_sc, 1)

            def probs_values(n):
                b, c = n // 4, n % 4
                pe.wait_ge(s_se, n + 1)
                if n >= 2:
                    pe.wait_ge(s_p2l, n - 1)
                for h in range(4):
                    last = te.transpose(pJ[:, n % 2, P * h:P * h + P], SM[:, n % 2, P * h:P * h + P], ident[:, :])
                last.then_inc(s_pt2, 1)
                pe.wait_ge(s_p2l, n + 1)
                for h in range(4):
                    col = SD * (4 * c + h)
                    last = product((pV, pX)[b][:, col:col + SD], lambda s: PT[:, n % 2, s, P * h:P * h + P],
                                   lambda s: VV[:, s, b, col:col + SD], True, True)
                last.then_inc(s_pv2, 1)

            pe.wait_ge(s_vl, 2)
            scores(0)
            for n in range(8):
                if n + 1 < 8:
                    scores(n + 1)
                probs_values(n)
            transpose_rows(an, 2, 3)
            pe.wait_ge(s_tl, 12)
            pe.wait_ge(s_sm, 8)
            weight_ready(5)
            rows(lambda b: pS[:, b, :], AT, 5)
            transpose_rows(hn, 2, 4)

            pe.wait_ge(d_key, 32)
            for m in range(4):
                last = te.transpose(pV[:, NK * m:NK * m + NK], xst[0:NK, P * m:P * m + P], ident[0:NK, 0:NK])
            last.then_inc(s_kt, 1)
            pe.wait_ge(s_tl, 14)
            pe.wait_ge(s_yread, 2)
            weight_ready(6)
            for m in range(4):
                for k in range(4):
                    last = product(pS[:, m // 2, T2 * (m % 2):T2 * (m % 2) + T2],
                                   lambda s: slot4(6, s)[:, k, P * m:P * m + P], lambda s: HT[:, s, k, :], k == 0, k == 3)
                if m % 2:
                    last.then_inc(s_q2, 1)
            pe.wait_ge(s_kl, 1)
            pe.wait_ge(s_q2l, 2)
            for b in range(B):
                for m in range(4):
                    last = product(pJ[:, b, P * m:P * m + P], lambda s: QT2[:, s, m, L * b:L * b + L],
                                   lambda s: KBk[:, s, m, :], True, True)
                last.then_inc(s_sim, 1)

            def gate_up(ft):
                q, j = ft // 4, ft % 4
                if ft >= 2:
                    pe.wait_ge(s_a, ft - 1)
                for i in range(2):
                    n = FB + 3 * q + i
                    if j == 0:
                        weight_ready(n)
                    for k in range(4):
                        last = product(pS[:, ft % 2, T2 * i:T2 * i + T2], lambda s: slot4(n, s)[:, k, P * j:P * j + P],
                                       lambda s: HT[:, s, k, :], k == 0, k == 3)
                    if i == 1:
                        last.then_inc(s_gu, 1)

            def add_tile(coef, n, j, start, stop, done):
                for b in range(B):
                    last = product((pV, pX)[b][:, :], lambda s: coef[:, s, L * b:L * b + L], lambda s: slot4(n, s)[:, j, :],
                                   start, stop)
                last.then_inc(done, 1)

            gate_up(0)
            for ft in range(16):
                if ft < 15:
                    gate_up(ft + 1)
                n = FB + 3 * (ft // 4) + 2
                if ft % 4 == 0:
                    weight_ready(n)
                pe.wait_ge(s_al, ft + 1)
                add_tile(ACTT[:, ft % 2], n, ft % 4, ft == 0, False, s_mo)
                if ft in (5, 10):
                    b = ft // 10
                    pe.wait_ge(s_gn, b + 1)
                    for h in range(RH):
                        te.transpose(pJ[:, b, P * h:P * h + P], GN[:, h, :], ident[:, :])
                        last = te.transpose(pT[:, b, P * h:P * h + P], RN[:, h, :], ident[:, :])
                    last.then_inc(s_gt, 1)
                if ft == 11:
                    pe.wait_ge(s_gl, 2)
                    pe.wait_ge(s_simc, 2)
                    for b in range(B):
                        last = te.transpose(pJ[0:1, 0, P * b:P * b + P], EXB[:, b:b + 1], ident[:, :])
                    last.then_inc(s_ex, 1)
                if ft == 12:
                    pe.wait_ge(s_exe, 1)
                    te.matmul(pJ[:, 1, 0:T2], delta[:, :], exrow[:, :], start=True, stop=True).then_inc(s_ex, 1)

            def front(e):
                q, j = e // 4, e % 4
                n = EB + 2 * q
                if j == 0:
                    wait_staged(pe, n)
                if e >= 1:
                    pe.wait_ge(s_dl, e)
                for k in range(4):
                    last = te.transpose(pS[:, 0, P * k:P * k + P], staged(n)[:, 512 * j + P * k:512 * j + P * k + P], ident[:, :])
                last.then_inc(s_dt, 1)
                if e >= 1:
                    pe.wait_ge(s_gexp, e)
                    pe.wait_ge(s_md, e)
                for i in range(2):
                    te.matmul(pJ[:, i, :], SEL[:, e, :], GX[:, HI, 2 * i:2 * i + 2, :, :], start=True, stop=False)
                    te.matmul(pJ[:, i, :], SEL[:, e, :], GX[:, LO, 2 * i:2 * i + 2, :, :], start=False, stop=True)
                    last = te.matmul(pT[:, i, :], SEL[:, e, :], RT[:, 2 * i:2 * i + 2, :, :], start=True, stop=True)
                last.then_inc(s_gd, 1)

            def reach(e):
                q, j = e // 4, e % 4
                n = EB + 2 * q
                pe.wait_ge(s_dl, e + 1)
                if e >= 1:
                    pe.wait_ge(s_c, e)
                for k in range(4):
                    cs = slice(512 * j + P * k, 512 * j + P * k + P)
                    last = product(pS[:, 1, 0:T2], lambda s: slot(n, s)[:, cs], lambda s: HT[:, s, k, :], k == 0, k == 3)
                last.then_inc(s_w, 1)

            def spread(e):
                n = EB + 2 * (e // 4) + 1
                if e % 4 == 0:
                    weight_ready(n)
                pe.wait_ge(s_cl, e + 1)
                add_tile(GT[:, e % 2], n, e % 4, False, e == ETS - 1, s_eo)

            pe.wait_ge(s_a, 16)
            pe.wait_ge(s_exe, 2)
            pe.wait_ge(s_selr, 1)
            front(0)
            for e in range(ETS):
                if e + 1 < ETS:
                    front(e + 1)
                reach(e)
                if e >= 1:
                    spread(e - 1)
            spread(ETS - 1)


_INS = ["x", "ctx_1024", "mask_BxS2_bk0", "L0_xattn_g1", "L0_xattn_b1", "L0_xattn_g2", "L0_xattn_b2", "L0_xattn_Wq",
        "L0_xattn_Wkv", "L0_xattn_Wout", "L0_attn_qw", "L0_attn_kw", "L0_attn_vw", "L0_attn_ow", "L0_ffn_Wg", "L0_ffn_bg",
        "L0_ffn_Wu", "L0_ffn_bu", "L0_ffn_Wd", "L0_ffn_bd", "L0_ffn_Wq", "L0_ffn_keys", "L0_ffn_down_embed", "L0_ffn_up_embed"]


def constants(seq, head):
    inv = (1.0 / 10000.0 ** (np.arange(0, head, 2, dtype=np.float32) / head)).astype(np.float32)
    freq = np.arange(seq, dtype=np.float32)[:, None] * inv[None, :]
    causal = np.where(np.arange(seq)[:, None] >= np.arange(seq)[None, :], 0.0, -1e30).astype(np.float32)
    select = np.zeros((128, 16, 128), np.float32)
    e = np.arange(128)
    for t in range(16):
        select[2 * t + e // 64, t, e] = 1.0
        select[64 + e % 64, t, e] = 1.0
    return {"rope_cos": np.cos(freq), "rope_sin": np.sin(freq), "causal": causal, "select": select.reshape(128, 2048)}


def kernel(**inputs):
    import concourse.bacc as bacc
    from concourse.bass_utils import run_bass_kernel_spmd

    nc = bacc.Bacc("TRN2", target_bir_lowering=False, num_devices=1)
    arrays, args = {}, []
    seq = inputs["x"].shape[1]
    given = {n: np.ascontiguousarray(inputs[n]) for n in _INS}
    given.update(constants(seq, 32))
    for name, a in given.items():
        arrays[f"in_{name}"] = a
        args.append(nc.dram_tensor(f"in_{name}", a.shape, mybir.dt.from_np(a.dtype), kind="ExternalInput").ap())
    args.append(nc.dram_tensor("out_0", inputs["x"].shape, F32, kind="ExternalOutput").ap())
    perceiver_layer(nc, *args)
    r = run_bass_kernel_spmd(nc, [arrays], core_ids=[0])
    return r.results[0]["out_0"]
```

```python
from contextlib import ExitStack

import numpy as np
import concourse.bass as bass
from concourse import mybir

F32 = mybir.dt.float32
F32R = mybir.dt.float32r
U8 = mybir.dt.uint8
U32 = mybir.dt.uint32
ALU = mybir.AluOpType
ACT = mybir.ActivationFunctionType
AX = mybir.AxisListType

P = 128
EPS = 1e-5
HI, LO = 0, 1


def perceiver_layer(nc, x, ctx1024, mask, g1, b1, g2, b2, Wq, Wkv, Wout, qw, kw, vw, ow,
                    Wg, bg, Wu, bu, Wd, bd, fWq, keys, down, up, rope_cos, rope_sin, causal, select, out):
    B, L, D = x.shape
    N = ctx1024.shape[1]
    KD = D // P
    INNER = Wq.shape[1]
    DH = 64
    H = INNER // DH
    CW = 512
    NT = CW // P
    ROUNDS = N // CW
    HG = 4
    G = H // HG
    STEPS = B * H
    UNITS = B * G
    XSC = DH ** -0.5
    SH, SD = 16, D // 16
    SSC = SD ** -0.5
    BIG = 1e30
    T2 = B * L
    F = Wg.shape[1]
    NEXP = down.shape[0]
    NK = 64
    RH = 4
    ETS = NEXP // P
    assert (B, L, D, N, F, NEXP) == (2, 128, 512, 2048, 2048, 2048)

    with ExitStack() as stack:
        def sb(name, shape, dt=F32):
            return stack.enter_context(nc.sbuf_tensor(name, shape, dt))

        def sem(name):
            return stack.enter_context(nc.semaphore(name))

        W = sb("W", [P, 16384], F32R)
        with nc.sbuf_tensor("QA", [P, 8192], F32R) as QA:
            pass
        with nc.sbuf_tensor("OTA", [P, 4096], F32R) as OTA:
            pass
        tail = sb("tail", [P, 4096])
        late = sb("late", [P, 4096])
        with nc.sbuf_tensor("XS", [P, 4096], F32) as XS:
            pass
        XA = sb("XA", [P, 8192], F32R)
        KV = sb("KV", [P, 8192], F32R)
        raw = sb("raw", [P, 2048])
        work = sb("work", [P, 2048])
        xst = sb("xst", [P, CW])
        with nc.sbuf_tensor("xres", [P, B, D], F32) as xres:
            pass
        with nc.sbuf_tensor("QL", [P, 2048], F32R) as QL:
            pass
        PT = sb("PT", [P, 2, 2, CW], F32R)
        with nc.sbuf_tensor("wst", [P, 2048], F32) as wst:
            pass
        KLO = sb("KLO", [P, 2, 2, CW], F32R)
        O = sb("O", [P, B, INNER])
        ident = sb("ident", [P, P])
        vrow = sb("vrow", [48, P])
        vec = sb("vec", [P, 48])
        hbg = sb("hbg", [P, 16])
        mraw = sb("mraw", [P, CW], U8)
        st = sb("st", [P, 4, 6])
        mv = sb("mv", [P, 4, 2])
        rstd = sb("rstd", [P, 4])
        half = sb("half", [P, 4])
        mold = sb("mold", [P, B, H])
        mcur = sb("mcur", [P, 2, HG])
        negm = sb("negm", [P, 2, HG])
        dm = sb("dm", [P, 2, HG])
        alpha = sb("alpha", [P, 2, HG])
        rs = sb("rs", [P, 2, HG])
        lsum = sb("lsum", [P, B, H])
        small = sb("small", [P, 64])

        pS = stack.enter_context(nc.psum_tensor("pS", [P, 2, 512], F32))
        pJ = stack.enter_context(nc.psum_tensor("pJ", [P, 2, 512], F32))
        pT = stack.enter_context(nc.psum_tensor("pT", [P, 2, 512], F32))
        pV = stack.enter_context(nc.psum_tensor("pV", [P, 512], F32))
        pX = stack.enter_context(nc.psum_tensor("pX", [P, 512], F32))

        WKV = W[:, :].rearrange("p (s k n) -> p s k n", s=2, k=KD)
        WQ = KV[:, :].rearrange("p (s k n) -> p s k n", s=2, k=KD)
        QT = QA[:, :].rearrange("p (s h t) -> p s h t", s=2, h=H)
        QZ, QHL = 0, 1
        XT = XA[:, :].rearrange("p (c s k n) -> p c s k n", c=2, s=2, k=KD)
        KHH = KV[:, 0:4096].rearrange("p (c j h n) -> p c j h n", c=2, j=2, h=2)
        QLv = QL[:, :].rearrange("p (m t) -> p m t", m=H // 2)
        ROWS = (slice(0, DH), slice(DH, P))
        VT = KV[:, 4096:8192].rearrange("p (c s t n) -> p c s t n", c=2, s=2, t=NT)
        SP = work[:, 0:1024].rearrange("p (c n) -> p c n", c=2)
        MB = work[:, 1024:2048].rearrange("p (c n) -> p c n", c=2)
        pVh = pV[:, :].rearrange("p (h s e) -> p h s e", h=HG, s=2)
        rawc = raw[:, :].rearrange("p (t d) -> p t d", t=NT)
        Of = O[:, :, :].rearrange("p b n -> p (b n)")
        Kg1, Kb1, Kg2, Kb2, Kbg, Kbu = 0, 4, 8, 12, 16, 32

        d_x = sem("d_x"); d_vec = sem("d_vec"); d_wq = sem("d_wq"); d_wkv = [sem(f"d_wkv{k}") for k in range(4)]
        d_raw = sem("d_raw"); d_kd = sem("d_kd"); d_q = [sem("d_q0"), sem("d_q1")]; d_mask = sem("d_mask")
        s_ident = sem("s_ident"); s_zero = sem("s_zero"); s_vt = sem("s_vt"); s_vec = sem("s_vec")
        s_wqh = sem("s_wqh"); s_wql = sem("s_wql"); s_wkvh = sem("s_wkvh"); s_wkvl = sem("s_wkvl")
        s_wkvl1 = sem("s_wkvl1")
        s_q = sem("s_q"); s_qh = sem("s_qh"); s_qhl = sem("s_qhl"); s_ql = sem("s_ql")
        s_stat = sem("s_stat"); s_rst = sem("s_rst"); s_rstd = sem("s_rstd"); s_latn = sem("s_latn")
        s_bn = sem("s_bn"); s_ch = sem("s_chain")
        s_norm = sem("s_norm"); s_norm2 = sem("s_norm2"); s_xtr = sem("s_xtr"); s_xh = sem("s_xh"); s_xT = sem("s_xT")
        s_mb = sem("s_mb")
        s_qk = sem("s_qk"); s_ttr = sem("s_ttr"); s_negm = sem("s_negm"); s_exp = sem("s_exp")
        s_proj = sem("s_proj"); s_kvh = sem("s_kvh"); s_kvl = sem("s_kvl")
        s_tr = sem("s_tr"); s_pth = sem("s_pth"); s_ptl = sem("s_ptl"); s_pv = sem("s_pv")
        s_dmt = sem("s_dmt"); s_dm = sem("s_dm"); s_alpha = sem("s_alpha"); s_lt = sem("s_lt"); s_osc = sem("s_osc")
        s_ohalf = sem("s_ohalf"); s_oadd = sem("s_oadd")

        d_w = [sem(f"d_w{i}") for i in range(5)]; d_key = sem("d_key"); d_rope = sem("d_rope"); d_sel = sem("d_sel")
        d_out = sem("d_out"); d_bd = sem("d_bd"); d_down = [sem("d_down0"), sem("d_down1")]; s_eh = sem("s_eh")
        s_el = sem("s_el")
        s_whi = sem("s_whi"); s_wlo = sem("s_wlo"); s_wuse = sem("s_wuse")
        s_src = sem("s_src")
        s_tt = sem("s_tt"); s_th = sem("s_th"); s_tl = sem("s_tl")
        s_ln = sem("s_ln"); s_pn = sem("s_pn")
        s_y = sem("s_y"); s_qkv = sem("s_qkv"); s_mx = sem("s_mx"); s_pn2 = sem("s_pn2"); s_ath = sem("s_ath")
        s_atl = sem("s_atl")
        s_vh = sem("s_vh"); s_rope = sem("s_rope"); s_kz = sem("s_kz")
        s_sc = sem("s_sc"); s_sm = sem("s_sm"); s_se = sem("s_se"); s_pt2 = sem("s_pt2"); s_p2h = sem("s_p2h")
        s_pv2 = sem("s_pv2")
        s_kt = sem("s_kt"); s_kh = sem("s_kh"); s_kl = sem("s_kl"); s_q2 = sem("s_q2"); s_q2h = sem("s_q2h")
        s_q2l = sem("s_q2l"); s_sim = sem("s_sim")
        s_gu = sem("s_gu"); s_ge = sem("s_ge"); s_a = sem("s_a"); s_ah = sem("s_ah"); s_al = sem("s_al")
        s_mo = sem("s_mo")
        s_tk = sem("s_tk"); s_tke = sem("s_tke"); s_gn = sem("s_gn"); s_pl = sem("s_pl"); s_simc = sem("s_simc")
        s_gt = sem("s_gt"); s_gh = sem("s_gh"); s_gl = sem("s_gl")
        s_selr = sem("s_selr"); s_iota = sem("s_iota")
        s_gd = sem("s_gd"); s_gexp = sem("s_gexp"); s_md = sem("s_md"); s_hs = sem("s_hs"); s_hs1 = sem("s_hs1")
        s_dt = sem("s_dt"); s_dh = sem("s_dh"); s_dl = sem("s_dl")
        s_w = sem("s_w"); s_we = sem("s_we"); s_c = sem("s_c"); s_chi = sem("s_chi"); s_cl = sem("s_cl")
        s_eo = sem("s_eo")
        s_ex = sem("s_ex"); s_exe = sem("s_exe"); s_exb = sem("s_exb"); s_fin = sem("s_fin")

        w4 = lambda w: w.rearrange("(k p) n -> p k n", p=P)
        blocks = [w4(Wout)[:, 0:4, :], w4(Wout)[:, 4:8, :], w4(qw), w4(kw), w4(vw), w4(ow), w4(fWq)]
        for f in range(4):
            blocks += [w4(Wg)[:, :, 512 * f:512 * f + 512], w4(Wu)[:, :, 512 * f:512 * f + 512],
                       w4(Wd)[:, 4 * f:4 * f + 4, :]]
        for f in range(4):
            blocks += [w4(down)[:, 4 * f:4 * f + 4, :], w4(up)[:, 4 * f:4 * f + 4, :]]
        NB = len(blocks)
        FB = 7
        EB = FB + 12
        is_down = lambda n: n >= EB and (n - EB) % 2 == 0
        n_split = lambda n: sum(not is_down(m) for m in range(n))
        stage_of = lambda n: 0 if n < 2 else n if n < 4 else (4, 0, 1)[(n - FB) % 3] if FB <= n < EB else 1 - n % 2
        users = lambda n: [m for m in range(n) if stage_of(m) == stage_of(n)]
        staged = lambda n: (raw[:, :], work[:, :], late[:, 0:2048], late[:, 2048:4096], wst[:, :])[stage_of(n)]
        slot_of = lambda n: 5 if n == 0 else (n - 1) % 4 if n < FB else (2, 3, 0, 4, 1)[(n - FB) % 5]
        slot = lambda n, part: (XA[:, 4096:8192] if slot_of(n) == 4 else XA[:, 0:4096] if slot_of(n) == 5 else W[:, 4096 * slot_of(n):4096 * slot_of(n) + 4096])[
            :, 2048 * part:2048 * part + 2048]

        def wait_used(eng, n):
            kind, q = ((n - FB) % 3, (n - FB) // 3) if n < EB else ((n - EB) % 2, (n - EB) // 2)
            if n < 6:
                eng.wait_ge(s_wuse, n + 1)
            elif n == 6:
                eng.wait_ge(s_q2, 2)
            elif n < EB:
                eng.wait_ge(s_mo if kind == 2 else s_gu, 4 * q + 4)
            else:
                eng.wait_ge(s_eo if kind == 1 else s_w, 4 * q + 4)

        def slot_free(eng, n):
            before = [m for m in range(n) if slot_of(m) == slot_of(n)]
            if before or slot_of(n) == 4:
                wait_used(eng, before[-1] if before else 5)
            elif n > 0:
                eng.wait_ge(s_proj, LAT + STEPS * ROUNDS)
            else:
                eng.wait_ge(s_proj, LAT + STEPS * ROUNDS - STEPS // 2)

        slot4 = lambda n, part: slot(n, part).rearrange("p (k n) -> p k n", k=4)

        def wait_staged(eng, n):
            eng.wait_ge(d_w[stage_of(n)], 16 * (len(users(n)) + 1))

        OT = OTA[:, :].rearrange("p (s c t) -> p s c t", s=2, c=8)
        HT = XA[:, 0:2048].rearrange("p (s c t) -> p s c t", s=2, c=4)
        QTs = XA[:, 2048:4096].rearrange("p (s c t) -> p s c t", s=2, c=4)
        AT = XA[:, 4096:6144].rearrange("p (s c t) -> p s c t", s=2, c=4)
        VV = Of[:, 1024:2048].rearrange("p (b n) -> p b n", b=B)
        PV2 = tail[:, 0:1024].rearrange("p (c n) -> p c n", c=2)
        KB = KV[:, :].rearrange("p (s c b h t) -> p s c b h t", s=2, c=4, b=B, h=4)
        rope = sb("rope", [P, 2, 16])
        cmask = sb("cmask", [P, P])
        QR = late[:, 0:1024].rearrange("p (b n) -> p b n", b=B)
        KR = late[:, 1024:2048].rearrange("p (b n) -> p b n", b=B)
        RTMP = late[:, 2048:3072].rearrange("p (i h e) -> p i h e", i=4, h=SH)
        SM = late[:, 3072:4096].rearrange("p (c n) -> p c n", c=2)
        hn = Of[:, 0:1024].rearrange("p (b n) -> p b n", b=B)
        an = Of[:, 1024:2048].rearrange("p (b n) -> p b n", b=B)

        def passed(eng):
            eng.sem_inc(s_passed, 1)

        s_passed = sem("s_passed")

        QT2 = XA[:, 2048:4096].rearrange("p (s m t) -> p s m t", s=2, m=4)
        KBk = KV[:, 0:1024].rearrange("p (s m n) -> p s m n", s=2, m=4)
        SEL = KV[:, 1024:3072].rearrange("p (e n) -> p e n", e=ETS)
        GT = KV[:, 3072:4096].rearrange("p (c s n) -> p c s n", c=2, s=2)
        ACTT = KV[:, 4096:5120].rearrange("p (c s n) -> p c s n", c=2, s=2)
        RT = KV[:, 5120:6144].rearrange("p (h b t) -> p h b t", h=RH, b=B)
        GX = KV[:, 6144:8192].rearrange("p (s h b t) -> p s h b t", s=2, h=RH, b=B)
        SIM = late[:, 0:1024].rearrange("p (b n) -> p b n", b=B)
        SC = late[:, 1024:1280]
        REP = late[:, 1280:1536]
        CM = late[:, 1536:1792]
        EXC = late[:, 1792:2048]
        EQ = late[:, 2048:4096]
        EW, MW = late[:, 2048:3072], late[:, 3072:4096]
        GN = tail[:, 0:512].rearrange("p (h n) -> p h n", h=RH)
        RN = tail[:, 512:1024].rearrange("p (h n) -> p h n", h=RH)
        ME = tail[:, 1024:1536].rearrange("p (c n) -> p c n", c=2)
        MG, MS = tail[:, 2048:2560].rearrange("p (c n) -> p c n", c=2), tail[:, 2816:3072]
        MA = tail[:, 1536:2048].rearrange("p (c n) -> p c n", c=2)
        HS = tail[:, 2048:2560].rearrange("p (c n) -> p c n", c=2)
        WE, WR_ = tail[:, 2560:2816], tail[:, 2816:3072]
        WC = tail[:, 3072:3584].rearrange("p (c n) -> p c n", c=2)
        V8, IXF, VALS, EV, N8 = (tail[:, a:b] for a, b in ((3584, 3648), (3648, 3712), (3712, 3744), (3744, 3776), (3776, 3808)))
        ZS, OFF, EXB = tail[:, 3808:3812], tail[:, 3812:3816], tail[:, 3816:3818]
        IOTA, W8, GE = tail[:, 3818:3882], tail[:, 3882:3890], tail[:, 3890:3922]
        IX = sb("IX", [P, 64], U32)
        delta = sb("delta", [1, P])
        exrow = sb("exrow", [1, T2])
        EXT = xst[:, 256:512]

        def tile_splits(ft):
            q, j = ft // 4, ft % 4
            if q < 3:
                return [FB + 3 * (q + 1) + j] if j < 3 else []
            return [EB + 1] if j == 1 else []

        def unit_of(u, first):
            return (u % B, u // B, u // B % 2) if first else (u // G, u % G, u % 2)

        LAT = G * HG

        def part_at(it, t, first, last):
            u, i = t // HG, t % HG
            if first and u < UNITS - 2:
                g, slot_ = u // B + 1, 2 * (u % B) + i // 2
                return (HG * g + slot_, slot_, g % 2, g, 1, True, HG * B * (g - 1)) if i % 2 else None
            if (first and u == UNITS - 2) or (last and u == UNITS - 1):
                return None
            U = UNITS * it + u
            return (HG * (U + 1) + i - (STEPS - LAT), i, (u + 1) % 2, (u + 1) % G, (u + 1) // G % 2, False, HG * U)

        block = stack.enter_context(nc.Block())
        x_v = x.rearrange("b p d -> p b d")
        ctx_v = ctx1024.rearrange("b (j n p) d -> b j p n d", n=NT, p=P)
        mask_v = mask.rearrange("b (j n) -> b j n", n=CW)

        wkv_stage = lambda k: (XS[:, 0:2048], XS[:, 2048:4096], raw[:, :], Of)[k]
        pL = (pX, pV)

        def kv_copy(i, par, lat, s, op):
            src = pJ[:, i % 2, 0:T2 if lat else CW]
            if i < 2:
                for h, r in enumerate(ROWS):
                    w = T2 if lat else CW
                    hi = KHH[r, par, i, h, 0:w]
                    last = op(hi if s == HI else KLO[r, par, i, 0:w], src[r], hi)
                return last
            if lat:
                return op(VT[:, par, s, i - 2, :], src, VT[:, par, HI, i - 2, :])
            ts = slice(2 * i - 4, 2 * i - 2)
            return op(VT[:, par, s, ts, :], src.rearrange("p (t n) -> p t n", t=2), VT[:, par, HI, ts, :])

        def normalise(eng, k):
            return eng.tensor_scalar(rawc[:, k, :], rawc[:, k, :], mv[:, k, 0:1], rstd[:, k:k + 1], ALU.subtract, ALU.mult)

        @block.sync
        def _(sp):
            sp.dma_start(xres[:, :, :], x_v).then_inc(d_x, 16)
            for v, (w, at) in enumerate(((g1, 0), (b1, 4), (g2, 8), (b2, 12), (bg, 16), (bu, 32))):
                n = w.shape[0] // P
                sp.dma_start(vrow[at:at + n, :], w.rearrange("(a p) -> a p", p=P)).then_inc(d_vec, 16)
            sp.dma_start(raw[:, :].rearrange("p (k n) -> p k n", k=2), w4(Wq)[:, 0:2, :]).then_inc(d_wq, 16)
            sp.dma_start(O[:, :, :], w4(Wq)[:, 2:4, :]).then_inc(d_wq, 16)
            for k in range(KD):
                if k >= 2:
                    sp.wait_ge(s_wql, k - 1)
                sp.dma_start(wkv_stage(k), w4(Wkv)[:, k, :]).then_inc(d_wkv[k], 16)

            def load_chunk(b, j):
                sp.dma_start(rawc, ctx_v[b, j]).then_inc(d_raw, 16)
                sp.dma_start(mraw[:, :], mask_v[b, j].partition_broadcast(P)).then_inc(d_mask, 16)

            sp.wait_ge(s_wkvl, 2)
            load_chunk(0, 0)

            def round_(it, first, last):
                for t in range(STEPS):
                    c = t // (STEPS // 2)
                    if t % (STEPS // 2) == 10 and not last and not (first and c == 0):
                        r = 2 * it - 1 + c
                        sp.wait_ge(s_xtr, 4 * r + 8)
                        passed(sp)
                        sp.wait_ge(s_mb, r + 1)
                        passed(sp)
                        load_chunk(c, it)

            round_(0, True, False)
            with sp.Fori(1, ROUNDS) as it:
                round_(it, False, False)
            round_(ROUNDS, False, True)

            sp.dma_start(rope[:, 0, :], rope_cos).then_inc(d_rope, 16)
            sp.dma_start(rope[:, 1, :], rope_sin).then_inc(d_rope, 16)
            sp.dma_start(cmask[:, :], causal).then_inc(d_rope, 16)
            order = list(range(EB + 2)) + [n + d for n in range(EB + 2, NB, 2) for d in (1, 0)]
            for n in order:
                if n == FB + 2:
                    sp.wait_ge(s_pv2, 8)
                    sp.dma_start(EQ, select).then_inc(d_sel, 16)
                    for side in range(2):
                        sp.dma_start(xst[0:NK, 256 * side:256 * side + 256].rearrange("k (h n) -> k h n", h=RH),
                                     keys.rearrange("h k p n -> p k h n")[side]).then_inc(d_key, 16)
                if n == FB + 4:
                    sp.wait_ge(s_tt, 12)
                    sp.dma_start(hn[:, 0, :], bd.partition_broadcast(P)).then_inc(d_bd, 16)
                if n == 0:
                    sp.wait_ge(s_xtr, 4 * 2 * ROUNDS + 4)
                if n == 2:
                    sp.wait_ge(s_qk, STEPS * (ROUNDS + 1))
                if n == 4:
                    sp.wait_ge(s_tr, STEPS * (ROUNDS + 1))
                if n == 5:
                    sp.wait_ge(s_pv, STEPS * (ROUNDS + 1))
                    sp.dma_start(xres[:, :, :], x_v).then_inc(d_x, 16)
                if is_down(n):
                    q = (n - EB) // 2
                    for j in range(2):
                        if q == 0 and j == 0:
                            sp.wait_ge(s_wlo, n_split(users(n)[-1]) + 1)
                        elif q > 0:
                            sp.wait_ge(s_dt, 4 * q - 2 + 2 * j)
                        sp.dma_start(raw[:, 1024 * j:1024 * j + 1024].rearrange("p (k n) -> p k n", k=2),
                                     blocks[n][:, 2 * j:2 * j + 2, :]).then_inc(d_down[j], 16)
                    continue
                if n > EB + 3:
                    sp.wait_ge(s_el, n - EB - 3)
                elif users(n):
                    sp.wait_ge(s_wlo, n_split(users(n)[-1]) + 1)
                sp.dma_start(staged(n).rearrange("p (k n) -> p k n", k=4), blocks[n]).then_inc(d_w[stage_of(n)], 16)
            sp.wait_ge(s_fin, 1)
            sp.dma_start(out.rearrange("b p d -> p b d"), an).then_inc(d_out, 16)
            sp.wait_ge(d_out, 16)

        @block.gpsimd
        def _(pool):
            gp = nc.gpsimd
            gp.memset(half[:, :], -0.5).then_inc(s_zero, 1)
            gp.memset(ident[:, :], 0.0).then_inc(s_ident, 1)
            pool.wait_ge(s_ident, 1)
            gp.affine_select(out=ident[:, :], in_=ident[:, :], compare_op=ALU.not_equal, fill=1.0,
                             base=0, pattern=[[-1, P]], channel_multiplier=1).then_inc(s_ident, 1)

            gp.memset(QA[:, 0:4096].bitcast(U32), 0).then_inc(s_zero, 1)

            def rsqrt(n, ready, count, done):
                pool.wait_ge(ready, count)
                gp.tensor_scalar(rstd[:, 0:n], mv[:, 0:n, 1], EPS, None, ALU.add).then_inc(s_rst, 1)
                rs_count[0] += 1
                pool.wait_ge(s_rst, rs_count[0])
                gp.tensor_tensor(rstd[:, 0:n], rstd[:, 0:n], half[:, 0:n], ALU.pow).then_inc(done, 1)

            def split_lo(n):
                pool.wait_ge(s_whi, n_split(n) + 1)
                gp.tensor_tensor(slot(n, LO), staged(n), slot(n, HI).bitcast(F32), ALU.subtract).then_inc(s_wlo, 1)

            rs_count = [0]
            pool.wait_ge(s_zero, 1)
            rsqrt(2, s_stat, 1, s_rstd)
            rsqrt(2, s_stat, 2, s_rstd)

            def block_lo(e, k, c, n):
                pool.wait_ge(s_xh, e + 1)
                gp.tensor_tensor(XT[:, c, LO, k, 0:n], xst[:, 0:n], XT[:, c, HI, k, 0:n].bitcast(F32), ALU.subtract).then_inc(s_xT, 1)

            gp.memset(work[:, 1024:2048], 0.0).then_inc(s_zero, 1)
            for k in range(KD):
                pool.wait_ge(s_xh, k + 1)
                gp.tensor_tensor(XT[:, 1, LO, k, 0:T2], xst[:, T2 * (k % 2):T2 * (k % 2) + T2], XT[:, 1, HI, k, 0:T2].bitcast(F32),
                                 ALU.subtract).then_inc(s_xT, 1)
            for k in (0, 2, 3):
                pool.wait_ge(s_wkvh, k + 1)
                gp.tensor_tensor(WKV[:, LO, k, :], wkv_stage(k), WKV[:, HI, k, :].bitcast(F32), ALU.subtract).then_inc(s_wkvl, 1)

            def beside(q, i, par, _g, _c, lat, _used):
                if i < 2:
                    w = T2 if lat else CW
                    pool.wait_ge(s_kvh, q + 1)
                    passed(pool)
                    for h in range(2):
                        pool.dma_start(KHH[ROWS[1 - h], par, i, h, 0:w], KHH[ROWS[h], par, i, h, 0:w]).then_inc(d_kd, 16)

            for j in range(2):
                pool.wait_ge(s_ql, 4 * j + 4)
                heads = QT.rearrange("p s (m h) t -> p s m h t", h=2)[:, :, 4 * j:4 * j + 4]
                for h in range(2):
                    pool.dma_start(heads[ROWS[1 - h], QHL, :, h, :], QLv[ROWS[h], 4 * j:4 * j + 4, :]).then_inc(d_q[j], 16)
                if j == 0:
                    for i in range(2):
                        beside(i, i, 0, 0, 1, True, 0)

            def chunk_half(r):
                pool.wait_ge(s_rstd, r + 3)
                passed(pool)
                normalise(gp, 2)
                normalise(gp, 3).then_inc(s_norm2, 1)

            def chunk_rstd(r):
                pool.wait_ge(s_stat, r + 3)
                passed(pool)
                gp.tensor_scalar(rstd[:, :], mv[:, :, 1], EPS, None, ALU.add).then_inc(s_rst, 1)
                pool.wait_ge(s_rst, r + 3)
                gp.tensor_tensor(rstd[:, :], rstd[:, :], half[:, :], ALU.pow).then_inc(s_rstd, 1)

            def unit(it, u, first):
                b, g, _ = unit_of(u, first)
                par = u % 2
                U = UNITS * it + u
                hs = slice(HG * g, HG * g + HG)
                pool.wait_ge(s_negm, HG * U + HG)
                if not first:
                    gp.tensor_tensor(dm[:, par, :], mold[:, b, hs], mcur[:, par, :], ALU.subtract).then_inc(s_dmt, 1)
                    pool.wait_ge(s_dmt, U - UNITS + 1)
                passed(pool)
                gp.tensor_copy(mold[:, b, hs], mcur[:, par, :]).then_inc(s_dm, 1)
                pool.wait_ge(s_exp, HG * U + HG)
                if first:
                    gp.tensor_copy(lsum[:, b, hs], rs[:, par, :]).then_inc(s_osc, 1)
                else:
                    pool.wait_ge(s_alpha, U - UNITS + 1)
                    gp.tensor_tensor(lsum[:, b, hs], lsum[:, b, hs], alpha[:, par, :], ALU.mult).then_inc(s_lt, 1)
                    ov = O[:, b, 256 * g:256 * g + 256].rearrange("p (h e) -> p h e", h=HG)
                    gp.tensor_tensor(ov, ov, alpha[:, par, :].unsqueeze(2).broadcast_to([P, HG, DH]), ALU.mult)
                    pool.wait_ge(s_lt, U - UNITS + 1)
                    gp.tensor_tensor(lsum[:, b, hs], lsum[:, b, hs], rs[:, par, :], ALU.add).then_inc(s_osc, 1)

            def round_(it, first, last):
                for u in range(UNITS):
                    c = u // G
                    prep = (c == 0 and not first) or (c == 1 and not last)
                    r = 2 * it - 1 + c
                    for i in range(HG):
                        part = part_at(it, HG * u + i, first, last)
                        if part:
                            beside(*part)
                        k = HG * (u % G) + i - 7
                        if prep and 0 <= k < KD:
                            block_lo(4 + 4 * r + k, k, 1 - c, CW)
                    if prep and u % G == 0:
                        chunk_rstd(r)
                    unit(it, u, first)
                    if prep and u % G == 0:
                        chunk_half(r)
                    if last and u == G:
                        split_lo(0)

            round_(0, True, False)
            with pool.Fori(1, ROUNDS) as it:
                round_(it, False, False)
            round_(ROUNDS, False, True)

            def row_rstd(i, b):
                pool.wait_ge(s_ln, 2 * i + b + 1)
                gp.tensor_scalar(rstd[:, b:b + 1], mv[:, b:b + 1, 1], EPS, None, ALU.add).then_inc(s_rst, 1)
                pool.wait_ge(s_rst, 2 + 2 * ROUNDS + 2 * i + b + 1)
                gp.tensor_tensor(rstd[:, b:b + 1], rstd[:, b:b + 1], half[:, b:b + 1], ALU.pow).then_inc(s_pn, 1)

            for n in range(1, 4):
                split_lo(n)
            for b in range(B):
                row_rstd(0, b)
            for n in range(4, FB + 2):
                split_lo(n)
            for b in range(B):
                row_rstd(1, b)
            pool.wait_ge(s_pv2, 8)
            gp.memset(KV[:, 0:1024].bitcast(U32), 0).then_inc(s_kz, 1)
            gp.iota(IOTA, [[1, NK]], base=0, channel_multiplier=0, allow_small_or_imprecise_dtypes=True)
            gp.iota(W8, [[-1, 8]], base=8, channel_multiplier=0, allow_small_or_imprecise_dtypes=True)
            gp.memset(delta[:, :], 0.0).then_inc(s_iota, 1)
            pool.wait_ge(s_iota, 1)
            gp.memset(delta[:, P - 1:P], 1.0).then_inc(s_iota, 1)
            split_lo(FB + 2)
            for ft in range(16):
                for n in tile_splits(ft):
                    split_lo(n)
            for e in range(ETS):
                pool.wait_ge(s_md, e + 1)
                gp.tensor_tensor(MW[:, 0:512], MW[:, 0:512], MW[:, 512:1024], ALU.add).then_inc(s_hs1, 1)
                pool.wait_ge(s_hs1, e + 1)
                if e >= 2:
                    pool.wait_ge(s_c, e - 1)
                gp.tensor_tensor(HS[:, e % 2, :], MW[:, 0:256], MW[:, 256:512], ALU.add).then_inc(s_hs, 1)


        @block.scalar
        def _(act):
            ac = nc.scalar
            act.wait_ge(s_vt, 1)
            ac.activation(vec[:, :], pX[:, 0:48], ACT.Copy).then_inc(s_vec, 1)
            act.wait_ge(s_vec, 1)
            ac.mul(hbg[:, :], vec[:, Kbg:Kbg + 16], 0.5)
            act.wait_ge(d_wq, 32)
            ac.activation(WQ[:, HI, 0:2, :], raw[:, :].rearrange("p (k n) -> p k n", k=2), ACT.Copy).then_inc(s_wqh, 1)
            ac.activation(WQ[:, HI, 2:4, :], O[:, :, :], ACT.Copy).then_inc(s_wqh, 1)

            def wkv_hi(k):
                act.wait_ge(d_wkv[k], 16)
                ac.activation(WKV[:, HI, k, :], wkv_stage(k), ACT.Copy).then_inc(s_wkvh, 1)

            def x_evac(e, k, c, kg, kb):
                act.wait_ge(s_xtr, e + 1)
                act.wait_ge(s_xT, e)
                for dst in (xst[:, :], XT[:, c, HI, k, :]):
                    last = ac.activation(dst, pX[:, :], ACT.Identity, bias=vec[:, kb:kb + 1], scale=vec[:, kg:kg + 1])
                last.then_inc(s_xh, 1)

            def split_hi(n, quarter=None):
                if not quarter:
                    wait_staged(act, n)
                    slot_free(act, n)
                cs = slice(0, 2048) if quarter is None else slice(512 * quarter, 512 * quarter + 512)
                ins = ac.activation(slot(n, HI)[:, cs], staged(n)[:, cs], ACT.Copy)
                if quarter in (None, 3):
                    ins.then_inc(s_whi, 1)

            for k in range(KD):
                act.wait_ge(s_xtr, k + 1)
                if k >= 2:
                    act.wait_ge(s_xT, k - 1)
                for dst in (xst[:, T2 * (k % 2):T2 * (k % 2) + T2], XT[:, 1, HI, k, 0:T2]):
                    last = ac.activation(dst, pL[k % 2][:, 0:T2], ACT.Identity, bias=vec[:, Kb2 + k:Kb2 + k + 1],
                                         scale=vec[:, Kg2 + k:Kg2 + k + 1])
                last.then_inc(s_xh, 1)
            wkv_hi(0)
            for m in range(H // 2):
                act.wait_ge(s_q, m + 1)
                if m == 0:
                    act.wait_ge(s_zero, 3)
                ac.activation(QT[0:DH, QZ, 2 * m, :], pJ[0:DH, m % 2, 0:T2], ACT.Copy)
                ac.activation(QT[DH:P, QZ, 2 * m + 1, :], pJ[DH:P, m % 2, 0:T2], ACT.Copy).then_inc(s_qh, 1)
                if m < 3:
                    wkv_hi(m + 1)

            def kv_hi(q, i, par, g, c, lat, used):
                act.wait_ge(s_proj, q + 1)
                if not (type(used) is int and used == 0):
                    act.wait_ge(s_qk if i < 2 else s_pv, used)
                kv_copy(i, par, lat, HI, lambda dst, src, hi: ac.activation(dst, src, ACT.Copy)).then_inc(s_kvh, 1)

            for i in range(HG):
                kv_hi(i, i, 0, 0, 1, True, 0)

            def round_(it, first, last):
                w = P if first else CW

                def pt_hi(t):
                    T = STEPS * it + t
                    act.wait_ge(s_tr, T + 1)
                    if not (first and t < 2):
                        act.wait_ge(s_pv, T - 1)
                    else:
                        act.wait_ge(d_q[t], 32)
                    ac.activation(PT[:, t % 2, HI, 0:w], pT[:, t % 2, 0:w], ACT.Copy).then_inc(s_pth, 1)

                def rescale(u):
                    if not first:
                        U = UNITS * it + u
                        act.wait_ge(s_dm, U + 1)
                        ac.activation(alpha[:, u % 2, :], dm[:, u % 2, :], ACT.Exp, scale=XSC).then_inc(s_alpha, 1)

                for t in range(STEPS):
                    u, i, c = t // HG, t % HG, t // (STEPS // 2)
                    par = u % 2
                    T = STEPS * it + t
                    act.wait_ge(s_negm, T + 1)
                    if i == 0 and not (first and u < 2):
                        act.wait_ge(s_osc, UNITS * it + u - 1)
                    ac.activation(SP[:, t % 2, 0:w], SP[:, t % 2, 0:w], ACT.Exp, bias=negm[:, par, i:i + 1],
                                  scale=XSC, accum_out=rs[:, par, i:i + 1]).then_inc(s_exp, 1)
                    part = part_at(it, t, first, last)
                    if part:
                        kv_hi(*part)
                    if i == 0 and u > 0:
                        rescale(u - 1)
                    if t > 0:
                        pt_hi(t - 1)
                    k = t % (STEPS // 2) - 7
                    if 0 <= k < KD and ((c == 0 and not first) or (c == 1 and not last)):
                        x_evac(4 + 4 * (2 * it - 1 + c) + k, k, 1 - c, Kg1 + k, Kb1 + k)
                    if last and STEPS // 2 <= t < STEPS // 2 + 4:
                        split_hi(0, t - STEPS // 2)
                    if last and t >= STEPS - 4 + 1:
                        split_hi(1, t - STEPS + 3)
                rescale(UNITS - 1)
                pt_hi(STEPS - 1)

            round_(0, True, False)
            with act.Fori(1, ROUNDS) as it:
                round_(it, False, False)
            round_(ROUNDS, False, True)

            split_hi(1, 3)
            split_hi(2)
            nb = [0]

            def transposed_hi(dst, b, c0=0):
                act.wait_ge(s_tt, nb[0] + 1)
                ac.activation(dst[:, HI, c0:c0 + 4, L * b:L * b + L], pT[:, nb[0] % 2, :].rearrange("p (c t) -> p c t", c=4),
                              ACT.Copy).then_inc(s_th, 1)
                nb[0] += 1

            for b in range(B):
                transposed_hi(OT, b)
                transposed_hi(OT, b, 4)
            split_hi(3)
            split_hi(4)

            def values_hi(b):
                if b == 0:
                    act.wait_ge(s_qkv, 3)
                else:
                    act.wait_ge(s_wuse, 5)
                ac.activation(VV[:, b, :], (pV, pX)[b][:, :], ACT.Copy).then_inc(s_vh, 1)

            def keys_hi(b):
                act.wait_ge(s_tt, nb[0] + 1)
                if b == 0:
                    act.wait_ge(s_kz, 1)
                for h in range(4):
                    rows = slice(SD * h, SD * h + SD)
                    last = ac.activation(KB[rows, HI, :, b, h, :], pT[rows, nb[0] % 2, :].rearrange("p (c t) -> p c t", c=4), ACT.Copy)
                last.then_inc(s_th, 1)
                nb[0] += 1

            transposed_hi(HT, 0)
            transposed_hi(HT, 1)
            split_hi(5)
            values_hi(0)
            transposed_hi(QTs, 0)
            keys_hi(0)
            values_hi(1)

            def exps(n):
                act.wait_ge(s_mx, n + 1)
                for i in range(4):
                    last = ac.activation(SM[:, n % 2, P * i:P * i + P], SM[:, n % 2, P * i:P * i + P], ACT.Exp,
                                         bias=negm[:, n % 2, i:i + 1], scale=SSC, accum_out=small[:, 4 * n + i:4 * n + i + 1])
                last.then_inc(s_se, 1)

            exps(0)
            exps(1)
            transposed_hi(QTs, 1)

            def p_hi(n):
                act.wait_ge(s_pt2, n + 1)
                if n >= 2:
                    act.wait_ge(s_pv2, n - 1)
                ac.activation(PV2[:, n % 2, :], pJ[:, n % 2, :], ACT.Copy).then_inc(s_p2h, 1)

            def outputs_hi(b):
                act.wait_ge(s_pv2, 4 * b + 4)
                ac.activation(AT[:, HI, :, L * b:L * b + L], (pV, pX)[b][:, :].rearrange("p (c t) -> p c t", c=4), ACT.Copy).then_inc(s_ath, 1)

            for n in range(1, 8):
                if n >= 2:
                    exps(n)
                p_hi(n - 1)
                if n == 1:
                    keys_hi(1)
                if n == 2:
                    split_hi(6)
                if n == 3:
                    split_hi(7)
                if n == 6:
                    split_hi(8)
                if n == 5:
                    outputs_hi(0)
            p_hi(7)
            outputs_hi(1)
            transposed_hi(HT, 0)

            act.wait_ge(s_kt, 1)
            act.wait_ge(s_kz, 2)
            kz = pJ[:, 1, 0:256].rearrange("p (m n) -> p m n", m=4)
            ac.activation(KBk[0:NK, HI, :, 0:NK], kz[0:NK], ACT.Copy)
            ac.activation(KBk[NK:P, HI, :, NK:P], kz[NK:P], ACT.Copy).then_inc(s_kh, 1)
            transposed_hi(HT, 1)
            for j in range(2):
                act.wait_ge(s_q2, j + 1)
                ac.activation(QT2[:, HI, 2 * j:2 * j + 2, :], pS[:, j, :].rearrange("p (m t) -> p m t", m=2), ACT.Copy).then_inc(s_q2h, 1)

            act.wait_ge(d_sel, 16)
            ac.activation(KV[:, 1024:3072], EQ, ACT.Copy).then_inc(s_selr, 1)
            split_hi(FB + 2)

            def gate_tanh(ft):
                act.wait_ge(s_gu, ft + 1)
                if ft >= 2:
                    act.wait_ge(s_a, ft - 1)
                ac.activation(MG[:, ft % 2, :], pS[:, ft % 2, 0:T2], ACT.Identity, bias=hbg[:, ft:ft + 1], scale=0.5)
                ac.activation(ME[:, ft % 2, :], pS[:, ft % 2, 0:T2], ACT.Tanh, bias=hbg[:, ft:ft + 1], scale=0.5).then_inc(s_ge, 1)

            gate_tanh(0)
            for ft in range(16):
                act.wait_ge(s_a, ft + 1)
                if ft >= 2:
                    act.wait_ge(s_mo, ft - 1)
                ac.activation(ACTT[:, ft % 2, HI, :], MA[:, ft % 2, :], ACT.Copy).then_inc(s_ah, 1)
                if ft in (9, 15):
                    b = ft // 15
                    act.wait_ge(s_gt, b + 1)
                    ac.activation(GX[:, HI, :, b, :], pJ[:, b, :].rearrange("p (h t) -> p h t", h=RH), ACT.Copy)
                    ac.activation(RT[:, :, b, :], pT[:, b, :].rearrange("p (h t) -> p h t", h=RH), ACT.Copy).then_inc(s_gh, 1)
                if ft < 15:
                    gate_tanh(ft + 1)
                for n in tile_splits(ft):
                    split_hi(n)
                j, b = (ft + 1) % 8, (ft + 1) // 8
                if j == 1:
                    act.wait_ge(s_tk, 3 * b + 1)
                    ac.activation(EV, EV, ACT.Exp).then_inc(s_tke, 1)
                if j == 2:
                    act.wait_ge(s_tk, 3 * b + 2)
                    ac.activation(ZS, ZS, ACT.Ln).then_inc(s_tke, 1)
                if j == 3:
                    act.wait_ge(s_tk, 3 * b + 3)
                    ac.activation(EXC, EXC, ACT.Exp).then_inc(s_tke, 1)

            def front(e):
                n = EB + 2 * (e // 4)
                act.wait_ge(s_dt, e + 1)
                if e % 4 == 0:
                    slot_free(act, n)
                ac.activation(slot(n, HI)[:, 512 * (e % 4):512 * (e % 4) + 512], pS[:, 0, :], ACT.Copy).then_inc(s_dh, 1)
                act.wait_ge(s_gd, e + 1)
                if e >= 1:
                    act.wait_ge(s_md, e)
                ac.activation(EW, pJ[:, :, :].rearrange("p a n -> p (a n)"), ACT.Exp).then_inc(s_gexp, 1)

            front(0)
            for e in range(ETS):
                if e + 1 < ETS:
                    front(e + 1)
                if e % 4 >= 2 and e < ETS - 4:
                    n, j = EB + 2 * (e // 4) + 3, e % 4 - 2
                    if j == 0:
                        wait_staged(act, n)
                        slot_free(act, n)
                    cs = slice(1024 * j, 1024 * j + 1024)
                    ac.activation(slot(n, HI)[:, cs], staged(n)[:, cs], ACT.Copy).then_inc(s_eh, 1)
                act.wait_ge(s_w, e + 1)
                if e >= 1:
                    act.wait_ge(s_c, e)
                ac.activation(WE, pS[:, 1, 0:T2], ACT.Tanh, scale=0.5).then_inc(s_we, 1)
                act.wait_ge(s_c, e + 1)
                if e >= 2:
                    act.wait_ge(s_eo, e - 1)
                ac.activation(GT[:, e % 2, HI, :], WC[:, e % 2, :], ACT.Copy).then_inc(s_chi, 1)

        @block.vector
        def _(dve):
            ve = nc.vector
            links = [0]

            def link(ins):
                links[0] += 1
                ins.then_inc(s_ch, 1)
                dve.wait_ge(s_ch, links[0])

            def low(dst, src, hi):
                return ve.tensor_tensor(dst, src, hi.bitcast(F32), ALU.subtract)

            dve.wait_ge(d_x, 16)
            for i, src in enumerate((xres, SP)):
                for b in range(B):
                    last = ve.bn_stats(st[:, b, :], src[:, b, :])
                link(last)
                for b in range(B):
                    last = ve.bn_aggr(mv[:, b, :], st[:, b, :])
                last.then_inc(s_stat, 1)
                dve.wait_ge(s_rstd, i + 1)
                dve.wait_ge(s_stat, i + 1)
                for b in range(B):
                    last = ve.tensor_scalar(SP[:, b, :], src[:, b, :], mv[:, b, 0:1], rstd[:, b:b + 1], ALU.subtract, ALU.mult)
                if i == 0:
                    link(last)
                else:
                    last.then_inc(s_latn, 1)
            for j in range(2):
                dve.wait_ge(s_wqh, j + 1)
                src = (raw[:, :].rearrange("p (k n) -> p k n", k=2), O[:, :, :])[j]
                low(WQ[:, LO, 2 * j:2 * j + 2, :], src, WQ[:, HI, 2 * j:2 * j + 2, :]).then_inc(s_wql, 1)

            for m in range(H // 2):
                dve.wait_ge(s_qh, m + 1)
                low(QLv[0:DH, m, :], pJ[0:DH, m % 2, 0:T2], QT[0:DH, QZ, 2 * m, :])
                low(QLv[DH:P, m, :], pJ[DH:P, m % 2, 0:T2], QT[DH:P, QZ, 2 * m + 1, :]).then_inc(s_ql, 1)
                for h in range(2):
                    last = ve.tensor_copy(QT[ROWS[h], QHL, 2 * m + h, :], QT[ROWS[h], QZ, 2 * m + h, :].bitcast(F32))
                last.then_inc(s_qhl, 1)
                if m == 1:
                    dve.wait_ge(s_wkvh, 2)
                    low(WKV[:, LO, 1, :], wkv_stage(1), WKV[:, HI, 1, :]).then_inc(s_wkvl1, 1)

            def kv_lo(q, i, par, _g, _c, lat, _used):
                dve.wait_ge(s_kvh, q + 1)
                kv_copy(i, par, lat, LO, low).then_inc(s_kvl, 1)

            for i in range(HG):
                kv_lo(i, i, 0, 0, 1, True, 0)

            def outputs_over_sums(b):
                dve.wait_ge(s_osc, UNITS * ROUNDS + G * (b + 1))
                dve.wait_ge(s_oadd, UNITS * ROUNDS + G * (b + 1))
                link(ve.reciprocal(small[:, H * b:H * b + H], lsum[:, b, :]))
                ov = O[:, b, :].rearrange("p (h e) -> p h e", e=DH)
                ve.tensor_tensor(ov, ov, small[:, H * b:H * b + H].unsqueeze(2).broadcast_to([P, H, DH]), ALU.mult).then_inc(s_src, 1)

            def round_(it, first, last):
                w = P if first else CW

                def pt_lo(t):
                    dve.wait_ge(s_pth, STEPS * it + t + 1)
                    low(PT[:, t % 2, LO, 0:w], pT[:, t % 2, 0:w], PT[:, t % 2, HI, 0:w]).then_inc(s_ptl, 1)

                def add_output(u):
                    U = UNITS * it + u
                    b, g, _ = unit_of(u, first)
                    o = O[:, b, 256 * g:256 * g + 256].rearrange("p (h e) -> p h e", h=HG)
                    dve.wait_ge(s_pv, HG * U + HG)
                    dve.wait_ge(s_osc, U + 1)
                    if first:
                        ve.tensor_copy(o, pVh[:, :, HI, :]).then_inc(s_ohalf, 1)
                    else:
                        ve.tensor_tensor(o, pVh[:, :, HI, :], o, ALU.add).then_inc(s_ohalf, 1)
                    dve.wait_ge(s_ohalf, U + 1)
                    ve.tensor_tensor(o, pVh[:, :, LO, :], o, ALU.add).then_inc(s_oadd, 1)

                for t in range(STEPS):
                    u, i, c = t // HG, t % HG, t // (STEPS // 2)
                    b, g, _ = unit_of(u, first)
                    par = u % 2
                    T = STEPS * it + t
                    prep = (c == 0 and not first) or (c == 1 and not last)
                    r = 2 * it - 1 + c
                    dve.wait_ge(s_qk, T + 1)
                    if not (first and t < 2):
                        dve.wait_ge(s_tr, T - 1)
                    if i == 0 and not (first and u < 2):
                        dve.wait_ge(s_dm, UNITS * it + u - 1)
                    if t % 16 == 0 and not first:
                        dve.wait_ge(s_mb, 2 * it - 1 + c)
                    passed(dve)
                    ve.tensor_tensor_reduce(out=SP[:, t % 2, 0:w], in0=pS[:, t % 2, 0:w], in1=MB[:, c, 0:w], scale=1.0,
                                            scalar=-3e38 if first else mold[:, b, HG * g + i:HG * g + i + 1],
                                            op0=ALU.add, op1=ALU.max, accum_out=mcur[:, par, i:i + 1]).then_inc(s_ttr, 1)
                    dve.wait_ge(s_ttr, T + 1)
                    ve.tensor_scalar(negm[:, par, i:i + 1], mcur[:, par, i:i + 1], -XSC, None, ALU.mult).then_inc(s_negm, 1)
                    part = part_at(it, t - 1, first, last) if t > 0 else None if first else part_at(it - 1, STEPS - 1, False, False)
                    if part:
                        kv_lo(*part)
                    if t > 0:
                        pt_lo(t - 1)
                    if i == 1 and u > 0:
                        add_output(u - 1)
                    if prep and t % 16 < NT:
                        if t % 16 == 0:
                            dve.wait_ge(d_raw, 16 * r + 16)
                        ve.bn_stats(st[:, t % 16, :], rawc[:, t % 16, :]).then_inc(s_bn, 1)
                        if t % 16 == NT - 1:
                            dve.wait_ge(s_bn, NT * r + NT)
                            passed(dve)
                            for k in range(NT):
                                ins = ve.bn_aggr(mv[:, k, :], st[:, k, :])
                            ins.then_inc(s_stat, 1)
                    if prep and t % 16 in (4, 5):
                        if t % 16 == 4:
                            dve.wait_ge(s_stat, r + 3)
                            dve.wait_ge(s_rstd, r + 3)
                            passed(dve)
                        ins = normalise(ve, t % 16 - 4)
                        if t % 16 == 5:
                            ins.then_inc(s_norm, 1)
                    if prep and t % 16 == 6:
                        dve.wait_ge(d_mask, 16 * r + 16)
                        passed(dve)
                        ve.tensor_scalar(MB[:, 1 - c, :], mraw[:, :], BIG, -BIG, ALU.mult, ALU.add).then_inc(s_mb, 1)
                    if last and t == STEPS // 2 + 4:
                        outputs_over_sums(0)
                pt_lo(STEPS - 1)
                add_output(UNITS - 1)

            round_(0, True, False)
            with dve.Fori(1, ROUNDS) as it:
                round_(it, False, False)
            round_(ROUNDS, False, True)

            nb = [0]

            def transposed_lo(dst, b, c0=0):
                dve.wait_ge(s_th, nb[0] + 1)
                hi = dst[:, HI, c0:c0 + 4, L * b:L * b + L]
                low(dst[:, LO, c0:c0 + 4, L * b:L * b + L], pT[:, nb[0] % 2, :].rearrange("p (c t) -> p c t", c=4), hi).then_inc(s_tl, 1)
                nb[0] += 1

            def add_rows(i, b):
                if b == 0:
                    dve.wait_ge(s_y, i + 1)
                else:
                    dve.wait_ge(s_wuse, (2, 6)[i])
                if i == 0 and b == 0:
                    dve.wait_ge(d_x, 32)
                y = (pS[:, b, :], (pV, pX)[b][:, :])[i]
                link(ve.tensor_tensor(xres[:, b, :], y, xres[:, b, :], ALU.add))
                link(ve.bn_stats(st[:, b, :], xres[:, b, :]))
                ve.bn_aggr(mv[:, b, :], st[:, b, :]).then_inc(s_ln, 1)

            def norm_rows(i, b):
                dve.wait_ge(s_ln, 2 * i + b + 1)
                dve.wait_ge(s_pn, 2 * i + b + 1)
                ve.tensor_scalar(hn[:, b, :], xres[:, b, :], mv[:, b, 0:1], rstd[:, b:b + 1], ALU.subtract, ALU.mult).then_inc(s_src, 1)

            outputs_over_sums(1)
            for b in range(B):
                transposed_lo(OT, b)
                transposed_lo(OT, b, 4)
                if b == 0:
                    dve.wait_ge(s_pv, STEPS * (ROUNDS + 1))
                last = ve.memset(KV[:, 4096 * b:4096 * b + 4096].bitcast(U32), 0)
            last.then_inc(s_kz, 1)
            add_rows(0, 0)
            norm_rows(0, 0)
            add_rows(0, 1)
            transposed_lo(HT, 0)
            norm_rows(0, 1)

            dve.wait_ge(d_rope, 48)
            dve.wait_ge(s_wlo, 4)

            def rotate(m, b):
                if b == 0:
                    dve.wait_ge(s_qkv, m + 1)
                else:
                    dve.wait_ge(s_wuse, m + 3)
                z = (pS, pJ)[m][:, b, :].rearrange("p (h e two) -> p h e two", h=SH, two=2)
                r = (QR, KR)[m][:, b, :].rearrange("p (h e two) -> p h e two", h=SH, two=2)
                cos = rope[:, 0, :].unsqueeze(1).broadcast_to([P, SH, SD // 2])
                sin = rope[:, 1, :].unsqueeze(1).broadcast_to([P, SH, SD // 2])
                ve.tensor_tensor(RTMP[:, 0], z[:, :, :, 0], cos, ALU.mult)
                ve.tensor_tensor(RTMP[:, 1], z[:, :, :, 1], sin, ALU.mult)
                ve.tensor_tensor(RTMP[:, 2], z[:, :, :, 0], sin, ALU.mult)
                link(ve.tensor_tensor(RTMP[:, 3], z[:, :, :, 1], cos, ALU.mult))
                ve.tensor_tensor(r[:, :, :, 0], RTMP[:, 0], RTMP[:, 1], ALU.subtract)
                ve.tensor_tensor(r[:, :, :, 1], RTMP[:, 2], RTMP[:, 3], ALU.add).then_inc(s_rope, 1)
                dve.wait_ge(s_rope, 2 * b + m + 1)

            def keys_lo(b):
                dve.wait_ge(s_th, nb[0] + 1)
                for h in range(4):
                    rows = slice(SD * h, SD * h + SD)
                    last = low(KB[rows, LO, :, b, h, :], pT[rows, nb[0] % 2, :].rearrange("p (c t) -> p c t", c=4),
                               KB[rows, HI, :, b, h, :])
                last.then_inc(s_tl, 1)
                nb[0] += 1

            rotate(0, 0)
            transposed_lo(HT, 1)
            rotate(1, 0)
            transposed_lo(QTs, 0)
            rotate(0, 1)
            keys_lo(0)
            rotate(1, 1)

            def row_max(n):
                dve.wait_ge(s_sc, n + 1)
                if n >= 2:
                    dve.wait_ge(s_pt2, n - 1)
                for i in range(4):
                    last = ve.tensor_tensor_reduce(out=SM[:, n % 2, P * i:P * i + P], in0=pS[:, n % 2, P * i:P * i + P],
                                                   in1=cmask[:, :], scale=1.0, scalar=-3e38, op0=ALU.add, op1=ALU.max,
                                                   accum_out=mcur[:, n % 2, i:i + 1])
                last.then_inc(s_sm, 1)
                dve.wait_ge(s_sm, n + 1)
                ve.tensor_scalar(negm[:, n % 2, :], mcur[:, n % 2, :], -SSC, None, ALU.mult).then_inc(s_mx, 1)

            def norm_probs(n):
                dve.wait_ge(s_se, n + 1)
                link(ve.reciprocal(small[:, 32 + 4 * n:36 + 4 * n], small[:, 4 * n:4 * n + 4]))
                sm = SM[:, n % 2, :].rearrange("p (h t) -> p h t", h=4)
                ve.tensor_tensor(sm, sm, small[:, 32 + 4 * n:36 + 4 * n].unsqueeze(2).broadcast_to([P, 4, P]), ALU.mult).then_inc(s_pn2, 1)

            row_max(0)
            row_max(1)
            norm_probs(0)
            transposed_lo(QTs, 1)

            def outputs_lo(b):
                dve.wait_ge(s_ath, b + 1)
                low(AT[:, LO, :, L * b:L * b + L], (pV, pX)[b][:, :].rearrange("p (c t) -> p c t", c=4),
                    AT[:, HI, :, L * b:L * b + L]).then_inc(s_atl, 1)

            for n in range(1, 8):
                if n < 7:
                    row_max(n + 1)
                norm_probs(n)
                if n == 1:
                    keys_lo(1)
                if n == 5:
                    outputs_lo(0)
            outputs_lo(1)
            add_rows(1, 0)
            norm_rows(1, 0)
            add_rows(1, 1)
            transposed_lo(HT, 0)
            norm_rows(1, 1)
            dve.wait_ge(s_kh, 1)
            kz = pJ[:, 1, 0:256].rearrange("p (m n) -> p m n", m=4)
            low(KBk[0:NK, LO, :, 0:NK], kz[0:NK], KBk[0:NK, HI, :, 0:NK])
            low(KBk[NK:P, LO, :, NK:P], kz[NK:P], KBk[NK:P, HI, :, NK:P]).then_inc(s_kl, 1)
            transposed_lo(HT, 1)
            for j in range(2):
                dve.wait_ge(s_q2h, j + 1)
                low(QT2[:, LO, 2 * j:2 * j + 2, :], pS[:, j, :].rearrange("p (m t) -> p m t", m=2), QT2[:, HI, 2 * j:2 * j + 2, :]).then_inc(s_q2l, 1)
            for b in range(B):
                dve.wait_ge(s_sim, b + 1)
                ve.tensor_copy(SIM[:, b, :], pJ[:, b, :]).then_inc(s_simc, 1)
            dve.wait_ge(s_simc, 2)
            dve.wait_ge(d_bd, 16)
            for b in range(B):
                ve.tensor_tensor(an[:, b, :], xres[:, b, :], hn[:, 0, :], ALU.add)

            hk = lambda t: t.rearrange("p (h k) -> p h k", h=RH)
            V8v = V8.rearrange("p (s h k) -> p s h k", s=2, h=RH)
            IXv = IX[:, :].rearrange("p (s h k) -> p s h k", s=2, h=RH)
            IXFv = IXF.rearrange("p (s n) -> p s n", s=2)
            SC4 = SC.rearrange("p (h a k) -> p h a k", h=RH, a=8)
            SC3 = SC.rearrange("p (h n) -> p h n", h=RH)
            EXC3 = EXC.rearrange("p (h n) -> p h n", h=RH)
            EQ3 = EQ.rearrange("p (n k) -> p n k", k=NK)

            def top_sides(b):
                for s in range(2):
                    for h in range(RH):
                        col = 256 * s + NK * h
                        last = ve.max(V8v[:, s, h, :], SIM[:, b, col:col + NK])
                link(last)
                for s in range(2):
                    for h in range(RH):
                        col = 256 * s + NK * h
                        last = ve.max_index(IXv[:, s, h, :], V8v[:, s, h, :], SIM[:, b, col:col + NK])
                link(last)
                ve.tensor_copy(IXF, IX[:, :])
                link(ve.tensor_tensor(SC4, V8v[:, 0].unsqueeze(3).broadcast_to([P, RH, 8, 8]),
                                      V8v[:, 1].unsqueeze(2).broadcast_to([P, RH, 8, 8]), ALU.add))

            def top_sums(b):
                for h in range(RH):
                    last = ve.max(hk(VALS)[:, h, :], SC3[:, h, :])
                link(last)
                for h in range(RH):
                    last = ve.match_replace(REP.rearrange("p (h n) -> p h n", h=RH)[:, h, :], hk(VALS)[:, h, :], SC3[:, h, :], -3e38)
                ve.tensor_tensor(hk(EV), hk(VALS), hk(VALS)[:, :, 0:1].broadcast_to([P, RH, 8]), ALU.subtract).then_inc(s_tk, 1)
                dve.wait_ge(s_tk, 3 * b + 1)
                link(ve.tensor_tensor(CM, REP, SC, ALU.not_equal))
                link(ve.tensor_reduce(N8, CM.rearrange("p (n k) -> p n k", k=8), AX.X, ALU.add))

            def match(b, side):
                if side == 0:
                    dve.wait_ge(s_tke, 3 * b + 1)
                    ve.tensor_reduce(ZS, hk(EV), AX.X, ALU.add).then_inc(s_tk, 1)
                    dve.wait_ge(s_selr, 1)
                link(ve.tensor_tensor(EQ3, IOTA.unsqueeze(1).broadcast_to([P, 32, NK]),
                                      IXFv[:, side, :].unsqueeze(2).broadcast_to([P, 32, NK]), ALU.is_equal))

            def weigh_x(b):
                dve.wait_ge(s_tke, 3 * b + 2)
                if b == 1:
                    dve.wait_ge(s_gt, 1)
                link(ve.tensor_tensor(OFF, hk(VALS)[:, :, 0], ZS, ALU.add))
                ve.tensor_tensor(EXC3, SC3, OFF.unsqueeze(2).broadcast_to([P, RH, NK]), ALU.subtract).then_inc(s_tk, 1)
                sim = SIM[:, b, :].rearrange("p (s h n) -> p s h n", s=2, h=RH)
                ve.tensor_tensor(GN[:, :, 0:NK], sim[:, 0], OFF.unsqueeze(2).broadcast_to([P, RH, NK]), ALU.subtract)
                ve.tensor_copy(GN[:, :, NK:P], sim[:, 1])
                link(ve.tensor_tensor(EQ3, EQ3, N8.unsqueeze(2).broadcast_to([P, 32, NK]), ALU.mult))

            def weigh_y(b):
                e = EQ.rearrange("p (h a n) -> p h a n", h=RH, a=8)
                link(ve.tensor_tensor(e, e, W8.unsqueeze(1).unsqueeze(3).broadcast_to([P, RH, 8, NK]), ALU.mult))

            def place(b, side):
                ve.tensor_reduce(RN[:, :, NK * side:NK * side + NK], EQ.rearrange("p (h a n) -> p h n a", h=RH, a=8), AX.X,
                                 ALU.add).then_inc(s_pl, 1)
                dve.wait_ge(s_pl, 2 * b + side + 1)

            def ranks(b):
                place(b, 1)
                ve.tensor_scalar(RN[:, :, NK:P], RN[:, :, NK:P], -8.0, None, ALU.add).then_inc(s_gn, 1)

            def beyond(b):
                ve.tensor_scalar(GE, IXFv[:, 0, :], float(NEXP // NK), None, ALU.is_ge)
                dve.wait_ge(s_tke, 3 * b + 3)
                link(ve.tensor_tensor(EXC, EXC, CM, ALU.mult))
                e8 = EXC.rearrange("p (n k) -> p n k", k=8)
                link(ve.tensor_tensor(e8, e8, GE.unsqueeze(2).broadcast_to([P, 32, 8]), ALU.mult))
                ve.tensor_reduce(EXB[:, b:b + 1], EXC, AX.X, ALU.add).then_inc(s_exb, 1)
                dve.wait_ge(s_exb, b + 1)

            def finish(b):
                ranks(b)
                if b == 0:
                    beyond(b)

            pieces = [top_sides, top_sums, lambda b: match(b, 0), weigh_x, lambda b: place(b, 0), lambda b: match(b, 1),
                      weigh_y, finish]
            top_sides(0)

            dve.wait_ge(s_iota, 2)
            for ft in range(16):
                dve.wait_ge(s_ge, ft + 1)
                link(ve.scalar_tensor_tensor(out=MS, in0=ME[:, ft % 2, :], scalar=1.0, in1=MG[:, ft % 2, :],
                                             op0=ALU.add, op1=ALU.mult))
                ve.scalar_tensor_tensor(out=MA[:, ft % 2, :], in0=pS[:, ft % 2, T2:2 * T2], scalar=vec[:, Kbu + ft:Kbu + ft + 1],
                                        in1=MS, op0=ALU.add, op1=ALU.mult).then_inc(s_a, 1)
                dve.wait_ge(s_ah, ft + 1)
                low(ACTT[:, ft % 2, LO, :], MA[:, ft % 2, :], ACTT[:, ft % 2, HI, :]).then_inc(s_al, 1)
                if ft < 15:
                    pieces[(ft + 1) % 8]((ft + 1) // 8)
                if ft in (9, 15):
                    b = ft // 15
                    dve.wait_ge(s_gh, b + 1)
                    low(GX[:, LO, :, b, :], pJ[:, b, :].rearrange("p (h t) -> p h t", h=RH), GX[:, HI, :, b, :]).then_inc(s_gl, 1)

            def turned_lo(e):
                n = EB + 2 * (e // 4)
                cs = slice(512 * (e % 4), 512 * (e % 4) + 512)
                dve.wait_ge(s_dh, e + 1)
                low(slot(n, LO)[:, cs], pS[:, 0, :], slot(n, HI)[:, cs]).then_inc(s_dl, 1)

            def mask_weights(e):
                dve.wait_ge(s_gexp, e + 1)
                if e >= 1:
                    dve.wait_ge(s_hs, e)
                ve.scalar_tensor_tensor(out=MW, in0=pT[:, :, :].rearrange("p a n -> p (a n)"), scalar=0.0, in1=EW,
                                        op0=ALU.is_gt, op1=ALU.mult).then_inc(s_md, 1)

            turned_lo(0)
            beyond(1)
            dve.wait_ge(s_ex, 1)
            ve.tensor_copy(exrow[:, :], pS[0:1, 1, 0:T2]).then_inc(s_exe, 1)
            dve.wait_ge(s_ex, 2)
            ve.tensor_copy(EXT, pS[:, 1, T2:2 * T2]).then_inc(s_exe, 1)
            mask_weights(0)
            for e in range(ETS):
                if e + 1 < ETS:
                    turned_lo(e + 1)
                    mask_weights(e + 1)
                dve.wait_ge(s_we, e + 1)
                link(ve.scalar_tensor_tensor(out=WR_, in0=WE, scalar=1.0, in1=pS[:, 1, 0:T2], op0=ALU.add, op1=ALU.mult))
                dve.wait_ge(s_hs, e + 1)
                if e == ETS - 1:
                    link(ve.tensor_tensor(HS[:, e % 2, :], HS[:, e % 2, :], EXT, ALU.add))
                ve.scalar_tensor_tensor(out=WC[:, e % 2, :], in0=WR_, scalar=0.5, in1=HS[:, e % 2, :],
                                        op0=ALU.mult, op1=ALU.mult).then_inc(s_c, 1)
                dve.wait_ge(s_chi, e + 1)
                low(GT[:, e % 2, LO, :], WC[:, e % 2, :], GT[:, e % 2, HI, :]).then_inc(s_cl, 1)
                if e % 4 >= 2 and e < ETS - 4:
                    n, j = EB + 2 * (e // 4) + 3, e % 4 - 2
                    cs = slice(1024 * j, 1024 * j + 1024)
                    dve.wait_ge(s_eh, 2 * (e // 4) + j + 1)
                    low(slot(n, LO)[:, cs], staged(n)[:, cs], slot(n, HI)[:, cs]).then_inc(s_el, 1)
            dve.wait_ge(s_eo, ETS)
            for b in range(B):
                last = ve.tensor_tensor(an[:, b, :], (pV, pX)[b][:, :], an[:, b, :], ALU.add)
            last.then_inc(s_fin, 1)

        @block.tensor
        def _(pe):
            te = nc.tensor

            def product(dst, a, b, start, stop):
                te.matmul(dst, a(HI), b(HI), start=start, stop=False)
                te.matmul(dst, a(HI), b(LO), start=False, stop=False)
                return te.matmul(dst, a(LO), b(HI), start=False, stop=stop)

            pe.wait_ge(d_vec, 96)
            pe.wait_ge(s_ident, 2)
            te.transpose(pX[:, 0:48], vrow[:, :], ident[0:48, 0:48]).then_inc(s_vt, 1)
            pe.wait_ge(s_vec, 1)
            pe.wait_ge(s_latn, 1)
            for k in range(KD):
                if k >= 2:
                    pe.wait_ge(s_xh, k - 1)
                for b in range(B):
                    last = te.transpose(pL[k % 2][:, P * b:P * b + P], SP[:, b, P * k:P * k + P], ident[:, :])
                last.then_inc(s_xtr, 1)
            pe.wait_ge(s_xT, KD)
            pe.wait_ge(s_wql, 2)
            for m in range(H // 2):
                if m >= 2:
                    pe.wait_ge(s_ql, m - 1)
                for k in range(KD):
                    last = product(pJ[:, m % 2, 0:T2], lambda s: WQ[:, s, k, P * m:P * m + P],
                                   lambda s: XT[:, 1, s, k, 0:T2], k == 0, k == KD - 1)
                last.then_inc(s_q, 1)

            def project(q, i, par, g, c, lat, used):
                if not (type(q) is int and q < 2):
                    pe.wait_ge(s_kvl, q - 1)
                if i < 2:
                    w = T2 if lat else CW
                    for k in range(KD):
                        last = product(pJ[:, i % 2, 0:w], lambda s: WKV[:, s, k, P * (2 * g + i):P * (2 * g + i + 1)],
                                       lambda s: XT[:, c, s, k, 0:w], k == 0, k == KD - 1)
                else:
                    for n, t in enumerate([i - 2] if lat else [2 * i - 4, 2 * i - 3]):
                        for k in range(KD):
                            last = product(pJ[:, i % 2, 256 * n:256 * n + 256],
                                           lambda s: XT[:, c, s, k, P * t:P * t + P],
                                           lambda s: WKV[:, s, k, INNER + 256 * g:INNER + 256 * g + 256], k == 0, k == KD - 1)
                last.then_inc(s_proj, 1)

            pe.wait_ge(s_ql, H // 2)
            pe.wait_ge(s_wkvl, KD - 1)
            pe.wait_ge(s_wkvl1, 1)
            for i in range(HG):
                project(i, i, 0, 0, 1, True, 0)

            def round_(it, first, last_round):
                w = P if first else CW
                tiles = w // P

                def transpose_p(t):
                    T = STEPS * it + t
                    pe.wait_ge(s_exp, T + 1)
                    if not (first and t < 2):
                        pe.wait_ge(s_ptl, T - 1)
                    for n in range(tiles):
                        last = te.transpose(pT[:, t % 2, P * n:P * n + P], SP[:, t % 2, P * n:P * n + P], ident[:, :])
                    last.then_inc(s_tr, 1)

                def values(t):
                    u, i = t // HG, t % HG
                    T = STEPS * it + t
                    U = UNITS * it + u
                    pe.wait_ge(s_ptl, T + 1)
                    b, g, par = unit_of(u, first)
                    if i == 0:
                        pe.wait_ge(s_kvl, HG * g + HG if first else HG * U + HG - (STEPS - LAT))
                        if not (first and u == 0):
                            pe.wait_ge(s_oadd, U)
                    for n in range(tiles):
                        for s in (HI, LO):
                            last = te.matmul(pVh[:, i, :, :], PT[:, t % 2, s, P * n:P * n + P],
                                             VT[:, par, :, b if first else n, DH * i:DH * i + DH],
                                             start=n == 0 and s == HI, stop=n == tiles - 1 and s == LO)
                    last.then_inc(s_pv, 1)

                for t in range(STEPS):
                    u, i, c = t // HG, t % HG, t // (STEPS // 2)
                    b, g, par = unit_of(u, first)
                    T = STEPS * it + t
                    if i % 2 == 0:
                        pe.wait_ge(s_kvl, HG * g + i // 2 + 1 if first else T + i // 2 - i + 1 - (STEPS - LAT))
                    if not (first and t < 2):
                        pe.wait_ge(s_ttr, T - 1)
                    if i == 0:
                        pe.wait_ge(d_kd, 64 * (g + 1) if first else 64 * (UNITS * it + u - (UNITS - G) + 1))
                        if first and t % (STEPS // 2) == 0:
                            pe.wait_ge(d_q[c], 32)
                            pe.wait_ge(s_qhl, 4 * c + 4)
                    h, cols = HG * g + i, slice(L * b, L * b + L)
                    n = cols if first else slice(0, CW)
                    te.matmul(pS[:, t % 2, 0:w], QT[:, QHL, h, cols], KHH[:, par, i // 2, i % 2, n], start=True, stop=False)
                    te.matmul(pS[:, t % 2, 0:w], QT[:, QZ, h, cols], KLO[:, par, i // 2, n], start=False, stop=True).then_inc(s_qk, 1)
                    part = part_at(it, t, first, last_round)
                    if part:
                        if i == 0 and u == G - 1 and not first:
                            pe.wait_ge(s_xT, 8 * it + 4)
                        if i == 0 and u == UNITS - 1:
                            pe.wait_ge(s_xT, 8 * it + 8)
                        project(*part)
                    k = t % (STEPS // 2) - 7
                    if 0 <= k < KD and ((c == 0 and not first) or (c == 1 and not last_round)):
                        r = 2 * it - 1 + c
                        if k == 0:
                            pe.wait_ge(s_norm, r + 1)
                            pe.wait_ge(s_norm2, r + 1)
                        pe.wait_ge(s_xh, 4 + 4 * r + k)
                        for n in range(NT):
                            last = te.transpose(pX[:, P * n:P * n + P], rawc[:, n, P * k:P * k + P], ident[:, :])
                        last.then_inc(s_xtr, 1)
                    if t >= 1:
                        transpose_p(t - 1)
                    if t >= 2:
                        values(t - 2)
                transpose_p(STEPS - 1)
                values(STEPS - 2)
                values(STEPS - 1)

            round_(0, True, False)
            with pe.Fori(1, ROUNDS) as it:
                round_(it, False, False)
            round_(ROUNDS, False, True)

            pe.wait_ge(s_ptl, STEPS * (ROUNDS + 1))
            nb = [0]

            def transpose_rows(src, b, ready, count, c0=0):
                pe.wait_ge(ready, count)
                if nb[0] >= 2:
                    pe.wait_ge(s_tl, nb[0] - 1)
                for c in range(4):
                    last = te.transpose(pT[:, nb[0] % 2, P * c:P * c + P], src[:, b, P * (c0 + c):P * (c0 + c) + P], ident[:, :])
                last.then_inc(s_tt, 1)
                nb[0] += 1

            def weight_ready(n):
                if n > EB + 1:
                    pe.wait_ge(s_el, n - EB - 1)
                else:
                    pe.wait_ge(s_wlo, n_split(n) + 1)

            def rows(dst, src, b, n, k0=0, start=True, stop=True):
                for k in range(4):
                    last = product(dst, lambda s: src[:, s, k0 + k, L * b:L * b + L], lambda s: slot4(n, s)[:, k, :],
                                   start and k == 0, stop and k == 3)
                return last

            for c in range(2):
                transpose_rows(O, 0, s_src, 1, 4 * c)
            for b in range(B):
                for n in range(2):
                    pe.wait_ge(s_tl, 2 * b + n + 1)
                    weight_ready(n)
                    last = rows(pS[:, b, :], OT, b, n, 4 * n, n == 0, n == 1)
                    if b == 1:
                        last.then_inc(s_wuse, 1)
                    elif n == 1:
                        last.then_inc(s_y, 1)
                    if b == 0 and n == 0:
                        pe.wait_ge(s_oadd, UNITS * (ROUNDS + 1))
                        for c in range(2):
                            transpose_rows(O, 1, s_src, 2, 4 * c)

            def project_rows(m, b):
                weight_ready(2 + m)
                rows((pS[:, b, :], pJ[:, b, :], (pV, pX)[b][:, :])[m], HT, b, 2 + m).then_inc(s_wuse if b == 1 else s_qkv, 1)

            transpose_rows(hn, 0, s_src, 3)
            pe.wait_ge(s_tl, 5)
            project_rows(0, 0)
            transpose_rows(hn, 1, s_src, 4)
            project_rows(1, 0)
            project_rows(2, 0)
            transpose_rows(QR, 0, s_rope, 1)
            pe.wait_ge(s_tl, 6)
            project_rows(0, 1)
            transpose_rows(KR, 0, s_rope, 2)
            project_rows(1, 1)
            project_rows(2, 1)

            def scores(n):
                b, c = n // 4, n % 4
                if c == 0:
                    pe.wait_ge(s_tl, 8 + 2 * b)
                if n >= 2:
                    pe.wait_ge(s_sm, n - 1)
                product(pS[:, n % 2, :], lambda s: QTs[:, s, c, L * b:L * b + L],
                        lambda s: KB[:, s, c, b, :, :], True, True).then_inc(s_sc, 1)

            def transpose_probs(n):
                pe.wait_ge(s_pn2, n + 1)
                if n >= 2:
                    pe.wait_ge(s_p2h, n - 1)
                for h in range(4):
                    last = te.transpose(pJ[:, n % 2, P * h:P * h + P], SM[:, n % 2, P * h:P * h + P], ident[:, :])
                last.then_inc(s_pt2, 1)

            def probs_values(n):
                b, c = n // 4, n % 4
                pe.wait_ge(s_p2h, n + 1)
                for h in range(4):
                    col = SD * (4 * c + h)
                    last = te.matmul((pV, pX)[b][SD * h:SD * h + SD, P * c:P * c + P], VV[:, b, col:col + SD],
                                     PV2[:, n % 2, P * h:P * h + P], start=True, stop=True)
                last.then_inc(s_pv2, 1)

            scores(0)
            pe.wait_ge(s_rope, 3)
            scores(1)
            transpose_rows(QR, 1, s_rope, 3)
            transpose_rows(KR, 1, s_rope, 4)
            pe.wait_ge(s_vh, 2)
            for n in range(8):
                if n + 2 < 8:
                    scores(n + 2)
                transpose_probs(n)
                if n >= 1:
                    probs_values(n - 1)
                if n == 6:
                    pe.wait_ge(s_atl, 1)
                    weight_ready(5)
                    rows(pV[:, :], AT, 0, 5).then_inc(s_y, 1)
            probs_values(7)
            pe.wait_ge(s_atl, 2)
            rows(pX[:, :], AT, 1, 5).then_inc(s_wuse, 1)
            transpose_rows(hn, 0, s_src, 5)

            pe.wait_ge(d_key, 32)
            for m in range(4):
                last = te.transpose(pJ[:, 1, NK * m:NK * m + NK], xst[0:NK, P * m:P * m + P], ident[0:NK, 0:NK])
            last.then_inc(s_kt, 1)
            transpose_rows(hn, 1, s_src, 6)
            pe.wait_ge(s_tl, 12)
            weight_ready(6)
            for m in range(4):
                for k in range(4):
                    last = product(pS[:, m // 2, T2 * (m % 2):T2 * (m % 2) + T2],
                                   lambda s: slot4(6, s)[:, k, P * m:P * m + P], lambda s: HT[:, s, k, :], k == 0, k == 3)
                if m % 2:
                    last.then_inc(s_q2, 1)
            pe.wait_ge(s_kl, 1)
            pe.wait_ge(s_q2l, 2)
            for b in range(B):
                for m in range(4):
                    last = product(pJ[:, b, P * m:P * m + P], lambda s: QT2[:, s, m, L * b:L * b + L],
                                   lambda s: KBk[:, s, m, :], True, True)
                last.then_inc(s_sim, 1)

            def gate_up(ft):
                q, j = ft // 4, ft % 4
                if ft >= 2:
                    pe.wait_ge(s_a, ft - 1)
                for i in range(2):
                    n = FB + 3 * q + i
                    if j == 0:
                        weight_ready(n)
                    for k in range(4):
                        last = product(pS[:, ft % 2, T2 * i:T2 * i + T2], lambda s: slot4(n, s)[:, k, P * j:P * j + P],
                                       lambda s: HT[:, s, k, :], k == 0, k == 3)
                    if i == 1:
                        last.then_inc(s_gu, 1)

            def add_tile(coef, n, j, start, stop, done):
                for b in range(B):
                    last = product((pV, pX)[b][:, :], lambda s: coef[:, s, L * b:L * b + L], lambda s: slot4(n, s)[:, j, :],
                                   start, stop)
                last.then_inc(done, 1)

            def log_weights(b):
                pe.wait_ge(s_gn, b + 1)
                for h in range(RH):
                    te.transpose(pJ[:, b, P * h:P * h + P], GN[:, h, :], ident[:, :])
                    last = te.transpose(pT[:, b, P * h:P * h + P], RN[:, h, :], ident[:, :])
                last.then_inc(s_gt, 1)

            def turn(e):
                q, j = e // 4, e % 4
                if j % 2 == 0:
                    pe.wait_ge(d_down[j // 2], 16 * q + 16)
                if e >= 1:
                    pe.wait_ge(s_dl, e)
                for k in range(4):
                    last = te.transpose(pS[:, 0, P * k:P * k + P], raw[:, 512 * j + P * k:512 * j + P * k + P], ident[:, :])
                last.then_inc(s_dt, 1)

            gate_up(0)
            for ft in range(16):
                if ft < 15:
                    gate_up(ft + 1)
                else:
                    pe.wait_ge(s_a, 15)
                    turn(0)
                n = FB + 3 * (ft // 4) + 2
                if ft % 4 == 0:
                    weight_ready(n)
                if ft == 15:
                    log_weights(1)
                pe.wait_ge(s_al, ft + 1)
                add_tile(ACTT[:, ft % 2], n, ft % 4, ft == 0, False, s_mo)
                if ft == 8:
                    log_weights(0)

            def select_(e):
                if e >= 1:
                    pe.wait_ge(s_gexp, e)
                    pe.wait_ge(s_md, e)
                for i in range(2):
                    te.matmul(pJ[:, i, :], SEL[:, e, :], GX[:, HI, 2 * i:2 * i + 2, :, :], start=True, stop=False)
                    te.matmul(pJ[:, i, :], SEL[:, e, :], GX[:, LO, 2 * i:2 * i + 2, :, :], start=False, stop=True)
                    last = te.matmul(pT[:, i, :], SEL[:, e, :], RT[:, 2 * i:2 * i + 2, :, :], start=True, stop=True)
                last.then_inc(s_gd, 1)

            def reach(e):
                q, j = e // 4, e % 4
                n = EB + 2 * q
                pe.wait_ge(s_dl, e + 1)
                if e >= 1:
                    pe.wait_ge(s_c, e)
                else:
                    pe.wait_ge(s_exe, 2)
                for k in range(4):
                    cs = slice(512 * j + P * k, 512 * j + P * k + P)
                    last = product(pS[:, 1, 0:T2], lambda s: slot(n, s)[:, cs], lambda s: HT[:, s, k, :], k == 0, k == 3)
                last.then_inc(s_w, 1)

            def spread(e):
                n = EB + 2 * (e // 4) + 1
                if e % 4 == 0:
                    weight_ready(n)
                pe.wait_ge(s_cl, e + 1)
                add_tile(GT[:, e % 2], n, e % 4, False, e == ETS - 1, s_eo)

            pe.wait_ge(s_gl, 2)
            pe.wait_ge(s_selr, 1)
            select_(0)
            pe.wait_ge(s_exb, 2)
            for b in range(B):
                last = te.transpose(pS[0:1, 1, P * b:P * b + P], EXB[:, b:b + 1], ident[:, :])
            last.then_inc(s_ex, 1)
            turn(1)
            pe.wait_ge(s_exe, 1)
            te.matmul(pS[:, 1, T2:2 * T2], delta[:, :], exrow[:, :], start=True, stop=True).then_inc(s_ex, 1)
            for e in range(ETS):
                if e + 1 < ETS:
                    if e > 0:
                        turn(e + 1)
                    select_(e + 1)
                reach(e)
                if e >= 1:
                    spread(e - 1)
            spread(ETS - 1)


_INS = ["x", "ctx_1024", "mask_BxS2_bk0", "L0_xattn_g1", "L0_xattn_b1", "L0_xattn_g2", "L0_xattn_b2", "L0_xattn_Wq",
        "L0_xattn_Wkv", "L0_xattn_Wout", "L0_attn_qw", "L0_attn_kw", "L0_attn_vw", "L0_attn_ow", "L0_ffn_Wg", "L0_ffn_bg",
        "L0_ffn_Wu", "L0_ffn_bu", "L0_ffn_Wd", "L0_ffn_bd", "L0_ffn_Wq", "L0_ffn_keys", "L0_ffn_down_embed", "L0_ffn_up_embed"]


def constants(seq, head):
    inv = (1.0 / 10000.0 ** (np.arange(0, head, 2, dtype=np.float32) / head)).astype(np.float32)
    freq = np.arange(seq, dtype=np.float32)[:, None] * inv[None, :]
    causal = np.where(np.arange(seq)[:, None] >= np.arange(seq)[None, :], 0.0, -1e30).astype(np.float32)
    select = np.zeros((128, 16, 128), np.float32)
    e = np.arange(128)
    for t in range(16):
        select[2 * t + e // 64, t, e] = 1.0
        select[64 + e % 64, t, e] = 1.0
    return {"rope_cos": np.cos(freq), "rope_sin": np.sin(freq), "causal": causal, "select": select.reshape(128, 2048)}


def kernel(**inputs):
    import concourse.bacc as bacc
    from concourse.bass_utils import run_bass_kernel_spmd

    nc = bacc.Bacc("TRN2", target_bir_lowering=False, num_devices=1)
    arrays, args = {}, []
    seq = inputs["x"].shape[1]
    given = {n: np.ascontiguousarray(inputs[n]) for n in _INS}
    given.update(constants(seq, 32))
    for name, a in given.items():
        arrays[f"in_{name}"] = a
        args.append(nc.dram_tensor(f"in_{name}", a.shape, mybir.dt.from_np(a.dtype), kind="ExternalInput").ap())
    args.append(nc.dram_tensor("out_0", inputs["x"].shape, F32, kind="ExternalOutput").ap())
    perceiver_layer(nc, *args)
    r = run_bass_kernel_spmd(nc, [arrays], core_ids=[0])
    return r.results[0]["out_0"]
```
